# Optimizing a Trainium2 kernel written in Bass

```python
import numpy as np
import jax
import jax.numpy as jnp

def _softmax(x, axis=-1):
    return jax.nn.softmax(x, axis=axis)

def _gelu(x):
    return jax.nn.gelu(x, approximate=True)

def _silu(x):
    return jax.nn.silu(x)

def _sigmoid(x):
    return jax.nn.sigmoid(x)

def _layernorm(x, axis=-1, eps=1e-05):
    m = jnp.mean(x, axis=axis, keepdims=True)
    v = jnp.var(x, axis=axis, keepdims=True)
    return (x - m) / jnp.sqrt(v + eps)

def _scatter_add(tgt, idx, src, axis=0):
    return tgt.at[idx].add(src)

def _segment_sum(src, seg, n):
    return jax.ops.segment_sum(src, seg, n)
kernel_name = 'mk_seq_postln_d2_jaxref_r8_7576e4'

def setup_inputs(seed: int=0):
    np.random.seed(seed)
    _w = jnp.asarray

    def _L0_attn_setup():
        import jax, jax.numpy as jnp
        import numpy as np
        N_HEADS, D_HEAD, D_EMBED = (16, 64, 128)
        BATCH, SEQ = (8, 128)
        WEIGHT_ALPHA = 1.0
        key = jax.random.key(seed)
        k1, k2, k3, k4, k5 = jax.random.split(key, 5)
        scale = WEIGHT_ALPHA / np.sqrt(D_EMBED)
        x = jax.random.normal(k1, (BATCH, SEQ, D_EMBED), dtype=jnp.float32)
        W_K = scale * jax.random.normal(k2, (N_HEADS, D_HEAD, D_EMBED), dtype=jnp.float32)
        W_Q = scale * jax.random.normal(k3, (N_HEADS, D_HEAD, D_EMBED), dtype=jnp.float32)
        W_V = scale * jax.random.normal(k4, (N_HEADS, D_HEAD, D_EMBED), dtype=jnp.float32)
        W_O = scale * jax.random.normal(k5, (D_EMBED, N_HEADS * D_HEAD), dtype=jnp.float32)
        return {'x': x, 'W_K': W_K, 'W_Q': W_Q, 'W_V': W_V, 'W_O': W_O}
    _L0_attn_in = _L0_attn_setup()

    def _L0_ffn_setup():
        import jax, jax.numpy as jnp
        import numpy as np
        DIM = 128

        def _reference_tuple_inner(x, W_r, W_k, W_v, mu_r, mu_k):
            B, T, C = x.shape
            x_prev = jnp.concatenate([jnp.zeros((B, 1, C), x.dtype), x[:, :-1, :]], axis=1)
            xr = mu_r * x + (1.0 - mu_r) * x_prev
            xk = mu_k * x + (1.0 - mu_k) * x_prev
            r = jax.nn.sigmoid(jnp.einsum('btc,dc->btd', xr, W_r))
            k = jnp.einsum('btc,dc->btd', xk, W_k)
            k_act = jnp.square(jax.nn.relu(k))
            out = r * jnp.einsum('btc,dc->btd', k_act, W_v)
            new_state = x[:, -1, :]
            return (out, new_state)
        key = jax.random.key(seed)
        ks = jax.random.split(key, 6)
        B, T, C = (8, 256, DIM)
        x = jax.random.normal(ks[0], (B, T, C), dtype=jnp.float32)
        s = 1.0 / np.sqrt(C)
        W_r = jax.random.uniform(ks[1], (C, C), jnp.float32, -s, s)
        W_k = jax.random.uniform(ks[2], (C, C), jnp.float32, -s, s)
        W_v = jax.random.uniform(ks[3], (C, C), jnp.float32, -s, s)
        mu_r = jax.random.uniform(ks[4], (C,), jnp.float32)
        mu_k = jax.random.uniform(ks[5], (C,), jnp.float32)
        return {'x': x, 'W_r': W_r, 'W_k': W_k, 'W_v': W_v, 'mu_r': mu_r, 'mu_k': mu_k}
    _L0_ffn_in = _L0_ffn_setup()

    def _L1_attn_setup():
        import jax, jax.numpy as jnp
        import numpy as np
        DIM = 128
        N_HEADS = 16
        HEAD_DIM = DIM // N_HEADS
        SCALE = HEAD_DIM ** (-0.5)
        key = jax.random.key(seed)
        kx, kq, kk, kv = jax.random.split(key, 4)
        x = jax.random.normal(kx, (2, 256, DIM), dtype=jnp.float32)
        bv_q = jax.random.normal(kq, (N_HEADS, HEAD_DIM), dtype=jnp.float32) * 0.02
        bv_k = jax.random.normal(kk, (N_HEADS, HEAD_DIM), dtype=jnp.float32) * 0.02
        bv_v = jax.random.normal(kv, (N_HEADS, HEAD_DIM), dtype=jnp.float32) * 0.02
        return {'x': x, 'bv_q': bv_q, 'bv_k': bv_k, 'bv_v': bv_v}
    _L1_attn_in = _L1_attn_setup()

    def _L1_ffn_setup():
        import jax, jax.numpy as jnp
        import numpy as np
        key = jax.random.key(seed)
        ks = jax.random.split(key, 5)
        B, T, D, E = (4, 256, 128, 8)
        inputs = jax.random.normal(ks[0], (B, T, D), dtype=jnp.float32)
        Wr = jax.random.normal(ks[1], (D, E), dtype=jnp.float32) * 0.02
        br = jnp.zeros((E,), dtype=jnp.float32)
        W1 = jax.random.normal(ks[2], (E, D, D), dtype=jnp.float32) * 0.02
        b1 = jnp.zeros((E, D), dtype=jnp.float32)
        W2 = jax.random.normal(ks[3], (E, D, D), dtype=jnp.float32) * 0.02
        b2 = jnp.zeros((E, D), dtype=jnp.float32)
        return {'inputs': inputs, 'Wr': Wr, 'br': br, 'W1': W1, 'b1': b1, 'W2': W2, 'b2': b2}
    _L1_ffn_in = _L1_ffn_setup()
    _d = {'L0_attn_x': _L0_attn_in['x'], 'L0_attn_W_K': _L0_attn_in['W_K'], 'L0_attn_W_Q': _L0_attn_in['W_Q'], 'L0_attn_W_V': _L0_attn_in['W_V'], 'L0_attn_W_O': _L0_attn_in['W_O'], 'L0_ffn_W_r': _L0_ffn_in['W_r'], 'L0_ffn_W_k': _L0_ffn_in['W_k'], 'L0_ffn_W_v': _L0_ffn_in['W_v'], 'L0_ffn_mu_r': _L0_ffn_in['mu_r'], 'L0_ffn_mu_k': _L0_ffn_in['mu_k'], 'L1_attn_bv_q': _L1_attn_in['bv_q'], 'L1_attn_bv_k': _L1_attn_in['bv_k'], 'L1_attn_bv_v': _L1_attn_in['bv_v'], 'L1_ffn_Wr': _L1_ffn_in['Wr'], 'L1_ffn_br': _L1_ffn_in['br'], 'L1_ffn_W1': _L1_ffn_in['W1'], 'L1_ffn_b1': _L1_ffn_in['b1'], 'L1_ffn_W2': _L1_ffn_in['W2'], 'L1_ffn_b2': _L1_ffn_in['b2']}
    _x0 = _d['L0_attn_x']
    _d['L0_attn_x'] = jax.random.normal(jax.random.fold_in(jax.random.key(seed), 1), (2, 1024, 128), dtype=_x0.dtype)
    del _x0
    return _d

def reference(L0_attn_x, L0_attn_W_K, L0_attn_W_Q, L0_attn_W_V, L0_attn_W_O, L0_ffn_W_r, L0_ffn_W_k, L0_ffn_W_v, L0_ffn_mu_r, L0_ffn_mu_k, L1_attn_bv_q, L1_attn_bv_k, L1_attn_bv_v, L1_ffn_Wr, L1_ffn_br, L1_ffn_W1, L1_ffn_b1, L1_ffn_W2, L1_ffn_b2):

    def _L0_attn_ref(x, W_K, W_Q, W_V, W_O):
        import jax, jax.numpy as jnp
        import numpy as np
        N_HEADS, D_HEAD, D_EMBED = (16, 64, 128)
        BATCH, SEQ = (8, 128)
        WEIGHT_ALPHA = 1.0
        b, seq, _ = x.shape
        d_head = W_K.shape[1]
        k = jnp.einsum('ahe,bce->bach', W_K, x)
        q = jnp.einsum('ahe,bce->bach', W_Q, x)
        v = jnp.einsum('ahe,bce->bach', W_V, x)
        scores = jnp.einsum('bach,baCh->bacC', k, q)
        mask = jnp.tril(jnp.ones((seq, seq), dtype=scores.dtype))
        masked = jnp.tril(scores) - 10000000000.0 * (1.0 - mask)
        attn = jax.nn.softmax(masked / np.sqrt(d_head), axis=-1)
        z = jnp.einsum('bach,bacC->baCh', v, attn)
        z_flat = z.transpose(0, 2, 1, 3).reshape(b, seq, -1)
        out = jnp.einsum('ef,bcf->bce', W_O, z_flat)
        return out

    def _L0_ffn_ref(x, W_r, W_k, W_v, mu_r, mu_k):
        import jax, jax.numpy as jnp
        import numpy as np
        DIM = 128

        def _reference_tuple_inner(x, W_r, W_k, W_v, mu_r, mu_k):
            B, T, C = x.shape
            x_prev = jnp.concatenate([jnp.zeros((B, 1, C), x.dtype), x[:, :-1, :]], axis=1)
            xr = mu_r * x + (1.0 - mu_r) * x_prev
            xk = mu_k * x + (1.0 - mu_k) * x_prev
            r = jax.nn.sigmoid(jnp.einsum('btc,dc->btd', xr, W_r))
            k = jnp.einsum('btc,dc->btd', xk, W_k)
            k_act = jnp.square(jax.nn.relu(k))
            out = r * jnp.einsum('btc,dc->btd', k_act, W_v)
            new_state = x[:, -1, :]
            return (out, new_state)
        return _reference_tuple_inner(x, W_r, W_k, W_v, mu_r, mu_k)[0]

    def _L1_attn_ref(x, bv_q, bv_k, bv_v):
        import jax, jax.numpy as jnp
        import numpy as np
        DIM = 128
        N_HEADS = 16
        HEAD_DIM = DIM // N_HEADS
        SCALE = HEAD_DIM ** (-0.5)
        B, T, D = x.shape
        H, HD = (N_HEADS, HEAD_DIM)
        x_h = x.reshape(B, T, H, HD)
        Q = x_h * jnp.sign(bv_q)
        K = x_h * jnp.sign(bv_k)
        V = x_h * jnp.sign(bv_v)
        scores = jnp.einsum('bqhd,bkhd->bhqk', Q, K) * SCALE
        causal = jnp.tril(jnp.ones((T, T), dtype=bool))
        attn = jnp.where(causal, jax.nn.sigmoid(scores * 4.0), 0.0)
        out = jnp.einsum('bhqk,bkhd->bqhd', attn, V)
        return out.reshape(B, T, D)

    def _L1_ffn_ref(inputs, Wr, br, W1, b1, W2, b2):
        import jax, jax.numpy as jnp
        import numpy as np
        B, T, D = inputs.shape
        E = Wr.shape[1]
        x = inputs.reshape(B * T, D)
        N = x.shape[0]
        C = N // E
        logits = x @ Wr + br
        probs = jax.nn.softmax(logits, axis=-1)
        gate = jnp.max(probs, axis=-1, keepdims=True)
        idx = jnp.argmax(probs, axis=-1)
        mask = jax.nn.one_hot(idx, E, dtype=jnp.float32)
        pos = (jnp.cumsum(mask, axis=0) * mask).astype(jnp.int32)
        mask = mask * (pos < C).astype(jnp.float32)
        mask_flat = jnp.sum(mask, axis=-1, keepdims=True)
        gate = gate * mask_flat
        combine = (gate * mask_flat * jax.nn.one_hot(idx, E, dtype=jnp.float32))[..., None] * jax.nn.one_hot(pos, C, dtype=jnp.float32)
        dispatch = combine
        expert_in = jnp.einsum('nd,nec->ecd', x, dispatch)
        h = jax.nn.relu(jnp.einsum('ecd,edf->ecf', expert_in, W1) + b1[:, None, :])
        eo = jnp.einsum('ecf,efd->ecd', h, W2) + b2[:, None, :]
        out = jnp.einsum('ecd,nec->nd', eo, combine)
        return out.reshape(B, T, D)
    x = L0_attn_x
    x = _layernorm(x + _L0_attn_ref(x, L0_attn_W_K, L0_attn_W_Q, L0_attn_W_V, L0_attn_W_O), axis=-1)
    x = _layernorm(x + _L0_ffn_ref(x, L0_ffn_W_r, L0_ffn_W_k, L0_ffn_W_v, L0_ffn_mu_r, L0_ffn_mu_k), axis=-1)
    x = _layernorm(x + _L1_attn_ref(x, L1_attn_bv_q, L1_attn_bv_k, L1_attn_bv_v), axis=-1)
    x = _layernorm(x + _L1_ffn_ref(x, L1_ffn_Wr, L1_ffn_br, L1_ffn_W1, L1_ffn_b1, L1_ffn_W2, L1_ffn_b2), axis=-1)
    return x

_drawn_inputs = setup_inputs


def setup_inputs(seed=0):
    import zlib

    import numpy as np

    out = dict(_drawn_inputs(seed))
    spreads = {'L1_ffn_br': (0.0, 0.667), 'L1_ffn_b1': (0.0, 0.8), 'L1_ffn_b2': (0.0, 0.54)}
    factors = {'L0_ffn_W_r': 2.99,
     'L0_ffn_mu_r': 6.161,
     'L1_ffn_Wr': 3.979,
     'L1_ffn_W1': 8.0,
     'L1_ffn_W2': 8.0}
    for name, (base, spread) in spreads.items():
        noise = np.random.default_rng([zlib.crc32(name.encode()), seed]).standard_normal(out[name].shape)
        drawn = base * np.exp(spread * noise) if base else spread * noise
        out[name] = jnp.asarray(drawn.astype(out[name].dtype))
    for name, factor in factors.items():
        out[name] = (out[name] * factor).astype(out[name].dtype)
    return out
```

```python
from contextlib import ExitStack

import concourse.bass as bass
from concourse import mybir

ALU = mybir.AluOpType
ACT = mybir.ActivationFunctionType
AX = mybir.AxisListType
F32 = mybir.dt.float32
F32R = mybir.dt.float32r
BF16 = mybir.dt.bfloat16

P = 128
B = 2
T = 1024
NB = T // P
HALF = 512

PAIRS = 8
DH0 = 64
STEPS = B * PAIRS
TILES = [[(0, 7)], [(1, 7)], "k", [(0, 6)], [(1, 6)], "q", [(0, 5)], [(1, 5)], "v", [(0, 4)], [(1, 4)],
         [(0, 3), (0, 2)], [(1, 3), (1, 2)], [(0, 1), (0, 0)], [(1, 1), (1, 0)]]
SLOTS = 3
UNITS = [unit for tile in TILES if tile not in ("k", "q", "v") for unit in tile]
UNIT_AT = {unit: n for n, unit in enumerate(UNITS)}
PIECES = {7: [(0, 0, 512), (512, 512, 512)], 6: [(0, 0, 512), (512, 512, 384)],
          5: [(128, 0, 384), (512, 384, 384)], 4: [(256, 0, 256), (512, 256, 384)],
          3: [(0, 0, 512)], 2: [(512, 0, 384)], 1: [(0, 0, 256)], 0: [(512, 0, 256)]}
RING = 4


def softmax_attention(nc, x_t, w_pairs, consts, z_t):
    with ExitStack() as ctx:
        def sb(name, shape, dt=F32):
            return ctx.enter_context(nc.sbuf_tensor("a0_" + name, shape, dt))

        def sem(name):
            return ctx.enter_context(nc.semaphore("a0_" + name))

        tiles = [ctx.enter_context(nc.psum_tensor(f"a0_tile{n}", [P, 2 * HALF], F32)) for n in range(SLOTS)]
        z_acc = ctx.enter_context(nc.psum_tensor("a0_z", [P, 2 * HALF], F32))

        w_cur = [sb(f"w{n}", [P, 3 * P]) for n in range(2)]
        x_cur = [sb(f"x{n}", [P, T]) for n in range(2)]
        k_hi, k_lo, q_hi, q_lo = (sb(n, [P, T], F32R) for n in ("k_hi", "k_lo", "q_hi", "q_lo"))
        k_stack, qh_stack, ql_stack = ([[sb(f"{s}{n}{h}", [P, T], F32R) for h in range(2)] for n in range(2)]
                                       for s in ("ks", "qh", "ql"))
        v_cur = [sb(f"v{n}", [P, T]) for n in range(2)]
        v_scaled = [sb(f"vs{n}", [P, 2, DH0]) for n in range(RING)]
        e = [[sb(f"e{h}{n}", [P, T]) for n in range(RING)] for h in range(2)]
        row_min = sb("min", [P, 2, NB])
        row_sum = sb("sum", [P, 2, NB])
        row_rec = sb("rec", [P, NB, 2])
        consts_f = sb("consts", [P, 2 * P])
        ident = sb("ident", [P, P], BF16)
        above = sb("above", [P, P], BF16)

        consts_loaded = sem("consts_loaded")
        consts_ready = sem("consts_ready")
        operands_loaded = [sem(f"operands_loaded{n}") for n in range(2)]
        proj_ready = sem("proj_ready")
        high_ready = sem("high_ready")
        low_ready = sem("low_ready")
        v_ready = sem("v_ready")
        k_stacked = sem("k_stacked")
        q_stacked = sem("q_stacked")
        scores_ready = sem("scores_ready")
        min_ready = sem("min_ready")
        exp_ready = sem("exp_ready")
        rec_ready = sem("rec_ready")
        v_scaled_ready = sem("v_scaled_ready")
        z_steps = sem("z_steps")
        z_copied = sem("z_copied")

        def ring_free(eng, s, i):
            if not (isinstance(s, int) and 8 * s + 7 - i < RING):
                eng.wait_ge(z_steps, s * 8 + (8 - i - RING))

        block = ctx.enter_context(nc.Block())

        @block.sync
        def _(sp):
            sp.dma_start(consts_f[:, :], consts).then_inc(consts_loaded, 16)

            def load_operands(n, par):
                sp.dma_start(w_cur[par][:, :], w_pairs[bass.ds(n % PAIRS * P, P), :]).then_inc(operands_loaded[par], 16)
                sp.dma_start(x_cur[par][:, :], x_t[bass.ds(n // PAIRS * P, P), :]).then_inc(operands_loaded[par], 16)

            def stack(n, par):
                sp.wait_ge(low_ready, n * 2 + 1)
                for h in range(2):
                    rows = slice(h * DH0, (h + 1) * DH0)
                    sp.dma_start(k_stack[par][h][0:DH0, :].bitcast(F32), k_hi[rows, :].bitcast(F32)).then_inc(k_stacked, 16)
                    sp.dma_start(k_stack[par][h][DH0:P, :].bitcast(F32), k_lo[rows, :].bitcast(F32)).then_inc(k_stacked, 16)
                sp.wait_ge(low_ready, n * 2 + 2)
                for h in range(2):
                    rows = slice(h * DH0, (h + 1) * DH0)
                    for half in (slice(0, DH0), slice(DH0, P)):
                        sp.dma_start(qh_stack[par][h][half, :].bitcast(F32), q_hi[rows, :].bitcast(F32)).then_inc(q_stacked, 16)
                        sp.dma_start(ql_stack[par][h][half, :].bitcast(F32), q_lo[rows, :].bitcast(F32)).then_inc(q_stacked, 16)

            def body(s, par):
                stack(s + 1, 1 - par)
                if not (isinstance(s, int) and s == STEPS - 2):
                    sp.wait_ge(v_ready, s + 2)
                    load_operands(s + 3, 1 - par)

            load_operands(0, 0)
            load_operands(1, 1)
            stack(0, 0)
            sp.wait_ge(v_ready, 1)
            load_operands(2, 0)
            body(0, 0)
            with sp.Fori(0, STEPS // 2 - 2) as u:
                body(u * 2 + 1, 1)
                body(u * 2 + 2, 0)
            for s in range(STEPS - 3, STEPS - 1):
                stack(s + 1, (s + 1) % 2)

        @block.tensor
        def _(pe):
            def project(n, par, what, tile):
                c = "kqv".index(what)
                if what == "k":
                    pe.wait_ge(operands_loaded[par], n * 16 + (16 if par else 32))
                if what == "v":
                    for i in range(NB):
                        m = pe.matmul(tile[:, i * P:(i + 1) * P], x_cur[par][:, i * P:(i + 1) * P],
                                      w_cur[par][:, c * P:(c + 1) * P], start=True, stop=True)
                else:
                    for c0 in (0, HALF):
                        m = pe.matmul(tile[:, c0:c0 + HALF], w_cur[par][:, c * P:(c + 1) * P],
                                      x_cur[par][:, c0:c0 + HALF], start=True, stop=True)
                m.then_inc(proj_ready, 1)

            def scores(par, unit, tile):
                h, i = unit
                keys = k_stack[par][h][:, i * P:(i + 1) * P]
                pieces = PIECES[i]
                for col, q0, n in pieces:
                    out = tile[:, col:col + n]
                    diagonal = (col, q0, n) == pieces[-1]
                    pe.matmul(out, keys, qh_stack[par][h][:, q0:q0 + n], start=True, stop=False)
                    if diagonal:
                        diag = col + i * P - q0
                        pe.matmul(tile[:, diag:diag + P], ident[:, :], above[:, :], start=False, stop=False,
                                  skip_group_check=True)
                    m = pe.matmul(out, keys, ql_stack[par][h][:, q0:q0 + n], start=False, stop=True)
                m.then_inc(scores_ready, 1)

            def weigh(s, i):
                pe.wait_ge(v_scaled_ready, s * 8 + (8 - i))
                if i == NB - 1 and not (isinstance(s, int) and s == 0):
                    pe.wait_ge(z_copied, s)
                w = (i + 1) * P
                for c0, c1 in ((0, min(w, HALF)), (HALF, w)):
                    if c1 <= c0:
                        continue
                    for h in range(2):
                        m = pe.matmul(z_acc[h * DH0:(h + 1) * DH0, c0:c1], v_scaled[i % RING][:, h, :],
                                      e[h][i % RING][:, c0:c1], start=(i == NB - 1),
                                      stop=True, skip_group_check=True)
                m.then_inc(z_steps, 1)

            def tile_free(s, k):
                last = isinstance(s, int) and s == STEPS - 1
                k -= SLOTS
                while last and k >= 0 and TILES[k] in ("k", "q", "v"):
                    k -= SLOTS
                if k < 0:
                    s, k = s - 1, k + len(TILES)
                if isinstance(s, int) and s < 0:
                    return
                if TILES[k] == "v":
                    pe.wait_ge(v_ready, s + 2)
                elif TILES[k] in ("k", "q"):
                    pe.wait_ge(low_ready, (s + 1) * 2 + 1 + "kq".index(TILES[k]))
                else:
                    pe.wait_ge(exp_ready, s * 16 + UNIT_AT[TILES[k][-1]] + 1)

            def body(s, par):
                last = isinstance(s, int) and s == STEPS - 1
                for k, what in enumerate(TILES):
                    tile = tiles[k % SLOTS]
                    if what in ("k", "q", "v"):
                        if not last:
                            tile_free(s, k)
                            project(s + 1, 1 - par, what, tile)
                        continue
                    tile_free(s, k)
                    if k == 0:
                        pe.wait_ge(k_stacked, s * 64 + 64)
                        pe.wait_ge(q_stacked, s * 128 + 128)
                    for unit in what:
                        scores(par, unit, tile)
                    if k == 1 and not (isinstance(s, int) and s == 0):
                        for i in (2, 1, 0):
                            weigh(s - 1, i)
                    for i in {7: [7], 10: [6], 12: [5], 14: [4, 3]}.get(k, []):
                        weigh(s, i)

            pe.wait_ge(consts_ready, 1)
            for k, what in enumerate("kqv"):
                project(0, 0, what, tiles[k])
            pe.wait_ge(low_ready, 2)
            pe.wait_ge(v_ready, 1)
            body(0, 0)
            with pe.Fori(0, STEPS // 2 - 1) as u:
                body(u * 2 + 1, 1)
                body(u * 2 + 2, 0)
            body(STEPS - 1, 1)
            for i in (2, 1, 0):
                weigh(STEPS - 1, i)

        @block.scalar
        def _(act):
            def high(n, what, tile):
                c = "kq".index(what)
                act.wait_ge(proj_ready, n * 3 + (1 + c))
                if what == "k" and not (isinstance(n, int) and n == 0):
                    act.wait_ge(k_stacked, n * 64)
                    act.wait_ge(q_stacked, n * 128)
                if what == "k":
                    nc.scalar.activation(k_hi[:, :], tile[:, :], ACT.Copy).then_inc(high_ready, 1)
                else:
                    nc.scalar.activation(q_hi[:, :], tile[:, :], ACT.Copy, scale=-DH0 ** -0.5).then_inc(high_ready, 1)

            def values(n, par, tile):
                act.wait_ge(proj_ready, n * 3 + 3)
                nc.scalar.activation(v_cur[par][:, :], tile[:, :], ACT.Copy).then_inc(v_ready, 1)

            def exponentials(s, unit, tile):
                h, i = unit
                n = UNIT_AT[unit]
                ring_free(act, s, i)
                act.wait_ge(min_ready, s * 16 + (n + 1))
                w, col = (i + 1) * P, PIECES[i][0][0]
                nc.scalar.activation(e[h][i % RING][:, 0:w], tile[:, col:col + w], ACT.Exp, bias=row_min[:, h, i:i + 1],
                                     scale=-1.0, accum_out=row_sum[:, h, i:i + 1]).then_inc(exp_ready, 1)

            def copy_z(s):
                act.wait_ge(z_steps, s * 8 + 8)
                nc.scalar.activation(z_t[:, bass.ds(s * T, T)], z_acc[:, :], ACT.Copy).then_inc(z_copied, 1)

            def body(s, par):
                last = isinstance(s, int) and s == STEPS - 1
                for k, what in enumerate(TILES):
                    tile = tiles[k % SLOTS]
                    if what in ("k", "q", "v"):
                        if last:
                            continue
                        if what == "v":
                            values(s + 1, 1 - par, tile)
                        else:
                            high(s + 1, what, tile)
                        continue
                    for unit in what:
                        exponentials(s, unit, tile)
                    if k == 1 and not (isinstance(s, int) and s == 0):
                        copy_z(s - 1)

            high(0, "k", tiles[0])
            high(0, "q", tiles[1])
            values(0, 0, tiles[2])
            body(0, 0)
            with act.Fori(0, STEPS // 2 - 1) as u:
                body(u * 2 + 1, 1)
                body(u * 2 + 2, 0)
            body(STEPS - 1, 1)
            copy_z(STEPS - 1)

        @block.vector
        def _(dve):
            def low(n, what, tile):
                c = "kq".index(what)
                dve.wait_ge(high_ready, n * 2 + (1 + c))
                if what == "k":
                    nc.vector.tensor_tensor(k_lo[:, :], tile[:, :], k_hi[:, :].bitcast(F32), ALU.subtract).then_inc(low_ready, 1)
                else:
                    nc.vector.scalar_tensor_tensor(q_lo[:, :], tile[:, :], -DH0 ** -0.5, q_hi[:, :].bitcast(F32), ALU.mult,
                                                   ALU.subtract).then_inc(low_ready, 1)

            def minimum(s, unit, tile):
                h, i = unit
                dve.wait_ge(scores_ready, s * 16 + (UNIT_AT[unit] + 1))
                w, col = (i + 1) * P, PIECES[i][0][0]
                nc.vector.tensor_reduce(row_min[:, h, i:i + 1], tile[:, col:col + w], AX.X, ALU.min).then_inc(min_ready, 1)

            def scale_values(s, par, i):
                dve.wait_ge(exp_ready, s * 16 + (UNIT_AT[(1, i)] + 1))
                nc.vector.reciprocal(row_rec[:, i, :], row_sum[:, :, i]).then_inc(rec_ready, 1)
                ring_free(dve, s, i)
                dve.wait_ge(rec_ready, s * 8 + (8 - i))
                nc.vector.tensor_tensor(v_scaled[i % RING][:, :, :],
                                        v_cur[par][:, i * P:(i + 1) * P].rearrange("p (h d) -> p h d", h=2),
                                        row_rec[:, i, :].unsqueeze(2).broadcast_to([P, 2, DH0]), ALU.mult).then_inc(v_scaled_ready, 1)

            def body(s, par):
                last = isinstance(s, int) and s == STEPS - 1
                for k, what in enumerate(TILES):
                    tile = tiles[k % SLOTS]
                    if what in ("k", "q"):
                        if not last:
                            low(s + 1, what, tile)
                        continue
                    if what == "v":
                        continue
                    for unit in what:
                        minimum(s, unit, tile)
                    if k == 1 and not (isinstance(s, int) and s == 0):
                        for i in (1, 0):
                            scale_values(s - 1, 1 - par, i)
                    for i in {4: [7], 7: [6], 10: [5], 12: [4], 14: [3, 2]}.get(k, []):
                        scale_values(s, par, i)

            dve.wait_ge(consts_loaded, 16)
            nc.vector.tensor_copy(ident[:, :], consts_f[:, 0:P])
            nc.vector.tensor_scalar(above[:, :], consts_f[:, P:2 * P], -1e30, 1e30, ALU.mult, ALU.add).then_inc(consts_ready, 1)
            low(0, "k", tiles[0])
            low(0, "q", tiles[1])
            dve.wait_ge(v_ready, 1)
            body(0, 0)
            with dve.Fori(0, STEPS // 2 - 1) as u:
                body(u * 2 + 1, 1)
                body(u * 2 + 2, 0)
            body(STEPS - 1, 1)
            for i in (1, 0):
                scale_values(STEPS - 1, 1, i)


GB = HALF // P
GROUPS = B * NB // GB
EPS = 1e-5


def norm_buffers(sb, sem, name):
    return {"stats": [sb(f"{name}_stats{n}", [P, GB, 6]) for n in range(2)],
            "moments": [sb(f"{name}_moments{n}", [P, GB, 2]) for n in range(2)],
            "std": [sb(f"{name}_std{n}", [P, GB]) for n in range(2)],
            "stats_ready": sem(f"{name}_stats_ready"), "variance_ready": sem(f"{name}_variance_ready"),
            "std_ready": sem(f"{name}_std_ready"), "inverse_ready": sem(f"{name}_inverse_ready")}


def norm_statistics(nc, dve, norm, g, y):
    stats, moments = norm["stats"][g % 2], norm["moments"][g % 2]
    for j in range(GB):
        nc.vector.bn_stats(stats[:, j, :], y[:, j, :]).then_inc(norm["stats_ready"], 1)
    dve.wait_ge(norm["stats_ready"], (g + 1) * GB)
    for j in range(GB):
        nc.vector.bn_aggr(moments[:, j, :], stats[:, j, :]).then_inc(norm["variance_ready"], 1)


def norm_root(nc, act, norm, g, eps):
    act.wait_ge(norm["variance_ready"], (g + 1) * GB)
    nc.scalar.activation(norm["std"][g % 2][:, :], norm["moments"][g % 2][:, :, 1], ACT.Sqrt,
                         bias=eps).then_inc(norm["std_ready"], 1)


def norm_apply(nc, dve, norm, g, y, out, ready):
    std, moments = norm["std"][g % 2], norm["moments"][g % 2]
    dve.wait_ge(norm["std_ready"], g + 1)
    nc.vector.reciprocal(std[:, :], std[:, :]).then_inc(norm["inverse_ready"], 1)
    dve.wait_ge(norm["inverse_ready"], g + 1)
    for j in range(GB):
        last = nc.vector.tensor_scalar(out[:, j, :], y[:, j, :], moments[:, j, 0:1], std[:, j:j + 1],
                                       ALU.subtract, ALU.mult)
    last.then_inc(ready, 1)


def channel_mix(nc, x_rows, w_o, w_rkv, columns, sign_v, consts, z_t, x2, x2_signed, q_parts, k_parts):
    with ExitStack() as ctx:
        def sb(name, shape, dt=F32):
            return ctx.enter_context(nc.sbuf_tensor("m_" + name, shape, dt))

        def sem(name):
            return ctx.enter_context(nc.semaphore("m_" + name))

        bank_a = [ctx.enter_context(nc.psum_tensor(f"m_a{g}", [P, HALF], F32)) for g in range(GROUPS)]
        bank_b = [ctx.enter_context(nc.psum_tensor(f"m_b{g}", [P, HALF], F32)) for g in range(GROUPS)]

        def blocks(bank):
            return bank[:, :].rearrange("p (j d) -> p j d", j=GB)

        xr0 = sb("x0", [P, B * NB, P])
        wo = sb("wo", [P, PAIRS, P])
        w3 = sb("w3", [P, 3, P])
        cols = sb("cols", [P, 8])
        sv = sb("sv", [P, P])
        consts_f = sb("consts", [P, P])
        x1 = sb("x1", [P, B * NB, P])
        x1t = sb("x1t", [P, B, T + 1])
        mixed = [[sb(f"{n}{g}", [P, HALF]) for g in range(2)] for n in ("xr", "xk")]
        prev = [[sb(f"pv{n}{g}", [P, HALF]) for g in range(2)] for n in ("r", "k")]
        gate = [sb(f"gate{g}", [P, GB, P]) for g in range(GROUPS)]
        k_act = [sb(f"kact{g}", [P, HALF]) for g in range(2)]
        y = [sb(f"y{g}", [P, GB, P]) for g in range(2)]
        rest = [sb(f"rest{g}", [P, HALF]) for g in range(GROUPS)]
        eps = sb("eps", [P, 1])
        parts = [sb(f"part{n}", [P, B * T], BF16) for n in range(3)]
        signed = [sb(f"signed{n}", [P, B * T], BF16) for n in range(3)]

        loaded = sem("loaded")
        mixed_in = sem("mixed_in")
        out_ready = sem("out_ready")
        x1_ready = sem("x1_ready")
        x1t_psum = sem("x1t_psum")
        x1t_ready = sem("x1t_ready")
        prev_ready = sem("prev_ready")
        rk_psum = sem("rk_psum")
        gate_ready = sem("gate_ready")
        k_act_ready = sem("k_act_ready")
        v_psum = sem("v_psum")
        x2_ready = sem("x2_ready")
        x2t_psum = sem("x2t_psum")
        high_ready = sem("high_ready")
        rest_ready = sem("rest_ready")
        mid_ready = sem("mid_ready")
        parts_ready = sem("parts_ready")
        signed_ready = sem("signed_ready")
        stored = sem("stored")
        signs_half = sem("signs_half")
        signs_ready = sem("signs_ready")
        y1_ready = sem("y1_ready")
        gated_ready = sem("gated_ready")
        y2_ready = sem("y2_ready")
        relu_ready = sem("relu_ready")
        setup_done = sem("setup_done")
        norm1 = norm_buffers(sb, sem, "norm1")
        norm2 = norm_buffers(sb, sem, "norm2")

        block = ctx.enter_context(nc.Block())
        MU_R, MU_K, SQ, SK, OMR, OMK, SS = range(7)

        @block.sync
        def _(sp):
            sp.dma_start(consts_f[:, :], consts).then_inc(loaded, 16)
            sp.dma_start(wo[:, :, :], w_o).then_inc(loaded, 16)
            sp.dma_start(xr0[:, :, :], x_rows).then_inc(loaded, 16)
            sp.dma_start(w3[:, :, :], w_rkv).then_inc(loaded, 16)
            sp.dma_start(cols[:, 0:4], columns).then_inc(loaded, 16)
            sp.dma_start(sv[:, :], sign_v.partition_broadcast(P)).then_inc(loaded, 16)
            sp.wait_ge(parts_ready, GROUPS)
            for n in range(3):
                sp.dma_start(q_parts[n, :, :], parts[n][:, :]).then_inc(stored, 16)
            sp.wait_ge(signed_ready, GROUPS * 3)
            for n in range(3):
                sp.dma_start(k_parts[n, :, :], signed[n][:, :]).then_inc(stored, 16)
            sp.wait_ge(stored, 16 * 6)

        @block.tensor
        def _(pe):
            pe.wait_ge(loaded, 16 * 6)
            for g in range(GROUPS):
                for j in range(GB):
                    n = g * GB + j
                    for pair in range(PAIRS):
                        step = n // NB * PAIRS + pair
                        m = pe.matmul(bank_a[g][:, j * P:(j + 1) * P],
                                      z_t[:, step * T + n % NB * P:step * T + (n % NB + 1) * P], wo[:, pair, :],
                                      start=(pair == 0), stop=(pair == PAIRS - 1))
                m.then_inc(out_ready, 1)
            for g in range(GROUPS):
                pe.wait_ge(x1_ready, g + 1)
                for j in range(GB):
                    m = pe.transpose(bank_b[g][:, j * P:(j + 1) * P], x1[:, g * GB + j, :], consts_f[:, :])
                m.then_inc(x1t_psum, 1)
            for g in range(GROUPS):
                pe.wait_ge(mixed_in, 2 * g + 2)
                pe.matmul(bank_a[g][:, :], w3[:, 1, :], mixed[1][g % 2][:, :], start=True, stop=True).then_inc(rk_psum, 1)
                for j in range(GB):
                    m = pe.matmul(bank_b[g][:, j * P:(j + 1) * P], mixed[0][g % 2][:, j * P:(j + 1) * P], w3[:, 0, :],
                                  start=True, stop=True)
                m.then_inc(rk_psum, 1)
                pe.wait_ge(k_act_ready, g + 1)
                for j in range(GB):
                    m = pe.matmul(bank_a[g][:, j * P:(j + 1) * P], k_act[g % 2][:, j * P:(j + 1) * P], w3[:, 2, :],
                                  start=True, stop=True)
                m.then_inc(v_psum, 1)
            for g in range(GROUPS):
                pe.wait_ge(x2_ready, g + 1)
                pe.wait_ge(gate_ready, g + 1)
                for j in range(GB):
                    m = pe.transpose(bank_b[g][:, j * P:(j + 1) * P], x2[:, g * GB + j, :], consts_f[:, :])
                m.then_inc(x2t_psum, 1)

        @block.scalar
        def _(act):
            act.wait_ge(setup_done, 1)
            norm_root(nc, act, norm1, 0, eps[:, :])
            for g in range(GROUPS):
                if g + 1 < GROUPS:
                    norm_root(nc, act, norm1, g + 1, eps[:, :])
                act.wait_ge(x1t_psum, g + 1)
                b, t0 = g // 2, g % 2 * HALF
                nc.scalar.activation(x1t[:, b, 1 + t0:1 + t0 + HALF], bank_b[g][:, :], ACT.Copy).then_inc(x1t_ready, 1)
                act.wait_ge(x1t_ready, g + 1)
                if g >= 2:
                    act.wait_ge(mixed_in, 2 * g - 2)
                for n, c in ((0, OMR), (1, OMK)):
                    nc.scalar.activation(prev[n][g % 2][:, :], x1t[:, b, t0:t0 + HALF], ACT.Identity,
                                         scale=cols[:, c:c + 1]).then_inc(prev_ready, 1)
            for g in range(GROUPS):
                act.wait_ge(rk_psum, 2 * g + 2)
                nc.scalar.activation(gate[g][:, :, :], blocks(bank_b[g]), ACT.Sigmoid).then_inc(gate_ready, 1)
            for g in range(GROUPS):
                norm_root(nc, act, norm2, g, eps[:, :])
            for g in range(GROUPS):
                cs = slice(g * HALF, (g + 1) * HALF)
                act.wait_ge(x2t_psum, g + 1)
                nc.scalar.activation(parts[0][:, cs], bank_b[g][:, :], ACT.Copy).then_inc(high_ready, 1)
                act.wait_ge(rest_ready, g + 1)
                nc.scalar.activation(parts[1][:, cs], rest[g][:, :], ACT.Copy).then_inc(mid_ready, 1)
                act.wait_ge(parts_ready, g + 1)
                for n in range(3):
                    nc.scalar.activation(signed[n][:, cs], parts[n][:, cs], ACT.Identity,
                                         scale=cols[:, SS:SS + 1]).then_inc(signed_ready, 1)

        @block.vector
        def _(dve):
            def sign(out, x, tmp, n):
                nc.vector.tensor_scalar(tmp, x, 0.0, None, ALU.is_lt)
                nc.vector.tensor_scalar(out, x, 0.0, None, ALU.is_gt).then_inc(signs_half, 1)
                dve.wait_ge(signs_half, n + 1)
                nc.vector.tensor_tensor(out, out, tmp, ALU.subtract).then_inc(signs_ready, 1)
                dve.wait_ge(signs_ready, n + 1)

            nc.vector.memset(eps[:, :], EPS)
            for b in range(B):
                nc.vector.memset(x1t[:, b, 0:1], 0.0)
            dve.wait_ge(loaded, 16 * 6)
            nc.vector.tensor_scalar(cols[:, OMR:OMK + 1], cols[:, MU_R:MU_K + 1], -1.0, 1.0, ALU.mult, ALU.add)
            sign(sv[:, :], sv[:, :], y[0][:, 0, :], 0)
            sign(cols[:, SQ:SK + 1], cols[:, SQ:SK + 1], y[0][:, 0, 0:2], 1)
            nc.vector.tensor_tensor(cols[:, SS:SS + 1], cols[:, SQ:SQ + 1], cols[:, SK:SK + 1], ALU.mult).then_inc(setup_done, 1)

            def rows(g):
                return slice(g * GB, (g + 1) * GB)

            def residual1(g):
                if g >= 2:
                    dve.wait_ge(x1_ready, g - 1)
                dve.wait_ge(out_ready, g + 1)
                nc.vector.tensor_tensor(y[g % 2][:, :, :], blocks(bank_a[g]), xr0[:, rows(g), :], ALU.add).then_inc(y1_ready, 1)
                dve.wait_ge(y1_ready, g + 1)
                norm_statistics(nc, dve, norm1, g, y[g % 2])

            residual1(0)
            for g in range(GROUPS):
                if g + 1 < GROUPS:
                    residual1(g + 1)
                norm_apply(nc, dve, norm1, g, y[g % 2], x1[:, rows(g), :], x1_ready)
            dve.wait_ge(x1_ready, GROUPS)
            for g in range(GROUPS):
                b, t0 = g // 2, g % 2 * HALF
                for n, c in ((0, MU_R), (1, MU_K)):
                    dve.wait_ge(prev_ready, 2 * g + n + 1)
                    if g >= 2:
                        dve.wait_ge(rk_psum, 2 * g - 2)
                    nc.vector.scalar_tensor_tensor(mixed[n][g % 2][:, :], x1t[:, b, 1 + t0:1 + t0 + HALF], cols[:, c:c + 1],
                                                   prev[n][g % 2][:, :], ALU.mult, ALU.add).then_inc(mixed_in, 1)
                dve.wait_ge(rk_psum, 2 * g + 1)
                if g >= 2:
                    dve.wait_ge(v_psum, g - 1)
                nc.vector.tensor_scalar(rest[g % 2][:, :], bank_a[g][:, :], 0.0, None, ALU.max).then_inc(relu_ready, 1)
                dve.wait_ge(relu_ready, g + 1)
                nc.vector.tensor_tensor(k_act[g % 2][:, :], rest[g % 2][:, :], rest[g % 2][:, :], ALU.mult).then_inc(k_act_ready, 1)
            def residual2(g):
                if g >= 2:
                    dve.wait_ge(x2_ready, g - 1)
                dve.wait_ge(v_psum, g + 1)
                dve.wait_ge(gate_ready, g + 1)
                nc.vector.tensor_tensor(y[g % 2][:, :, :], blocks(bank_a[g]), gate[g][:, :, :], ALU.mult).then_inc(gated_ready, 1)
                dve.wait_ge(gated_ready, g + 1)
                nc.vector.tensor_tensor(y[g % 2][:, :, :], y[g % 2][:, :, :], x1[:, rows(g), :], ALU.add).then_inc(y2_ready, 1)
                dve.wait_ge(y2_ready, g + 1)
                norm_statistics(nc, dve, norm2, g, y[g % 2])

            residual2(0)
            for g in range(GROUPS):
                if g + 1 < GROUPS:
                    residual2(g + 1)
                norm_apply(nc, dve, norm2, g, y[g % 2], x2[:, rows(g), :], x2_ready)
            for g in range(GROUPS):
                gs, cs = rows(g), slice(g * HALF, (g + 1) * HALF)
                dve.wait_ge(x2_ready, g + 1)
                nc.vector.tensor_tensor(x2_signed[:, gs, :], x2[:, gs, :],
                                        sv[:, :].unsqueeze(1).broadcast_to([P, GB, P]), ALU.mult)
                dve.wait_ge(high_ready, g + 1)
                nc.vector.tensor_tensor(rest[g][:, :], bank_b[g][:, :], parts[0][:, cs], ALU.subtract).then_inc(rest_ready, 1)
                dve.wait_ge(mid_ready, g + 1)
                nc.vector.tensor_tensor(parts[2][:, cs], rest[g][:, :], parts[1][:, cs], ALU.subtract).then_inc(parts_ready, 1)


H1 = 16
DH1 = 8
QUAD = 4
QUADS = B * H1 // QUAD
PARTS = 3
STACK = 96
BLOCK_STEPS = [[0], [1], [2], [3], [4, 5], [6, 7]]
KEY_PIECES = {0: [(0, 0, 512), (512, 512, 512)], 1: [(128, 128, 384), (512, 512, 512)],
              2: [(256, 256, 256), (512, 512, 512)], 3: [(384, 384, 128), (512, 512, 512)],
              4: [(512, 512, 512)], 5: [(128, 640, 384)], 6: [(0, 768, 256)], 7: [(256, 896, 128)]}
SPAN = [(0, 1024), (128, 1024), (256, 1024), (384, 1024), (128, 1024), (0, 384)]
RING1 = 3


def sigmoid_attention(nc, consts, q_parts, k_parts, x2_signed, out_t):
    with ExitStack() as ctx:
        def sb(name, shape, dt=F32):
            return ctx.enter_context(nc.sbuf_tensor("a1_" + name, shape, dt))

        def sem(name):
            return ctx.enter_context(nc.semaphore("a1_" + name))

        tiles = [ctx.enter_context(nc.psum_tensor(f"a1_tile{n}", [P, 2 * HALF], F32)) for n in range(SLOTS)]
        acc = ctx.enter_context(nc.psum_tensor("a1_acc", [P, 2 * HALF], F32))
        q_stack = [sb(f"q{n}", [STACK, QUAD, T], BF16) for n in range(2)]
        k_stack = [sb(f"k{n}", [STACK, QUAD, T], BF16) for n in range(2)]
        values = [sb(f"v{n}", [P, NB, QUAD, 32]) for n in range(2)]
        a = [[sb(f"a{j}{n}", [P, T]) for n in range(RING1)] for j in range(QUAD)]
        consts_f = sb("consts", [P, 2 * P])
        ident = sb("ident", [P, P], BF16)
        below = sb("below", [P, P], BF16)

        consts_loaded = sem("consts_loaded")
        setup_done = sem("setup_done")
        zeroed = sem("zeroed")
        stacked = [sem(f"stacked{n}") for n in range(2)]
        values_ready = sem("values_ready")
        scores_ready = sem("scores_ready")
        attn_ready = sem("attn_ready")
        steps_done = sem("steps_done")
        acc_copied = sem("acc_copied")
        NS = len(BLOCK_STEPS)
        NT = NS * QUAD
        LOADS = 2 * PARTS * PARTS * 16

        block = ctx.enter_context(nc.Block())

        def first(s):
            return isinstance(s, int) and s == 0

        @block.sync
        def _(sp):
            sp.dma_start(consts_f[:, :], consts).then_inc(consts_loaded, 16)

            def load(s, par):
                for n in range(PARTS):
                    rows = slice(n * PARTS * DH1, (n + 1) * PARTS * DH1)
                    h0, b = s % (QUADS // B) * (QUAD * DH1), s // (QUADS // B)
                    src = q_parts[n, bass.ds(h0, QUAD * DH1), bass.ds(b * T, T)].rearrange("(j d) t -> d j t", j=QUAD)
                    for c in range(PARTS):
                        r = slice((n * PARTS + c) * DH1, (n * PARTS + c + 1) * DH1)
                        sp.dma_start(q_stack[par][r, :, :], src).then_inc(stacked[par], 16)
                        src_k = k_parts[c, bass.ds(h0, QUAD * DH1), bass.ds(b * T, T)].rearrange("(j d) t -> d j t", j=QUAD)
                        sp.dma_start(k_stack[par][r, :, :], src_k).then_inc(stacked[par], 16)

            sp.wait_ge(zeroed, 4)
            load(0, 0)
            load(1, 1)

            def body(s, par):
                sp.wait_ge(scores_ready, (s - 1) * NT)
                load(s, par)

            with sp.Fori(1, QUADS // 2) as u:
                body(u * 2, 0)
                body(u * 2 + 1, 1)

        @block.tensor
        def _(pe):
            def scores(s, par, k):
                for j in range(QUAD):
                    at = k * QUAD + j
                    tile = tiles[at % SLOTS]
                    if not (first(s) and at < SLOTS):
                        pe.wait_ge(attn_ready, s * NT + (at - SLOTS + 1))
                    for i in BLOCK_STEPS[k]:
                        keys = k_stack[par][:, j, i * P:(i + 1) * P]
                        for n, (col, q0, width) in enumerate(KEY_PIECES[i]):
                            out = tile[:, col:col + width]
                            if n == 0:
                                pe.matmul(out, keys, q_stack[par][:, j, q0:q0 + width], start=True, stop=True)
                                m = pe.matmul(tile[:, col:col + P], ident[:, :], below[:, :], start=False, stop=True,
                                              skip_group_check=True)
                            else:
                                m = pe.matmul(out, keys, q_stack[par][:, j, q0:q0 + width], start=True, stop=True)
                    m.then_inc(scores_ready, 1)

            def weigh(s, par, k):
                if k == 0:
                    pe.wait_ge(values_ready, s + 1)
                    if not first(s):
                        pe.wait_ge(acc_copied, s)
                pe.wait_ge(attn_ready, s * NT + (k + 1) * QUAD)
                for i in BLOCK_STEPS[k]:
                    for col, q0, width in KEY_PIECES[i]:
                        for j in range(QUAD):
                            m = pe.matmul(acc[32 * j:32 * j + 32, q0:q0 + width], values[par][:, i, j, :],
                                          a[j][k % RING1][:, col:col + width], start=(i == 0), stop=True,
                                          skip_group_check=True)
                m.then_inc(steps_done, 1)

            def body(s, par):
                pe.wait_ge(stacked[par], s * (LOADS // 2) + (LOADS // 2 if par else LOADS))
                for k in range(NS):
                    scores(s, par, k)
                    if k >= 1:
                        weigh(s, par, k - 1)
                    elif not first(s):
                        weigh(s - 1, 1 - par, NS - 1)

            pe.wait_ge(setup_done, 1)
            pe.wait_ge(zeroed, 4)
            body(0, 0)
            with pe.Fori(0, QUADS // 2 - 1) as u:
                body(u * 2 + 1, 1)
                body(u * 2 + 2, 0)
            body(QUADS - 1, 1)
            weigh(QUADS - 1, 1, NS - 1)

        @block.scalar
        def _(act):
            def body(s):
                for k in range(NS):
                    for j in range(QUAD):
                        at = k * QUAD + j
                        act.wait_ge(scores_ready, s * NT + (at + 1))
                        if not (first(s) and k < RING1) and j == 0:
                            act.wait_ge(steps_done, s * NS + (k - RING1 + 1))
                        c0, c1 = SPAN[k]
                        nc.scalar.activation(a[j][k % RING1][:, c0:c1], tiles[at % SLOTS][:, c0:c1], ACT.Sigmoid,
                                             scale=4.0 * DH1 ** -0.5).then_inc(attn_ready, 1)

            body(0)
            with act.Fori(1, QUADS) as s:
                body(s)

        @block.vector
        def _(dve):
            for n in range(2):
                nc.vector.memset(q_stack[n][64:STACK, :, :], 0.0).then_inc(zeroed, 1)
                nc.vector.memset(k_stack[n][64:STACK, :, :], 0.0).then_inc(zeroed, 1)
            dve.wait_ge(consts_loaded, 16)
            for n in range(2):
                nc.vector.memset(values[n][:, :, :, :], 0.0).then_inc(zeroed, 1)
            nc.vector.tensor_copy(ident[:, :], consts_f[:, 0:P])
            nc.vector.tensor_tensor(below[:, :], consts_f[:, P:2 * P], consts_f[:, 0:P], ALU.subtract).then_inc(zeroed, 1)
            dve.wait_ge(zeroed, 7)
            nc.vector.tensor_scalar(below[:, :], below[:, :], -1e30, None, ALU.mult).then_inc(setup_done, 1)

            def prepare(s, par):
                b, h0 = s // (QUADS // B), s % (QUADS // B) * (QUAD * DH1)
                nc.vector.tensor_copy(values[par][:, :, :, 0:DH1],
                                      x2_signed[:, bass.ds(b * NB, NB), bass.ds(h0, QUAD * DH1)]
                                      .rearrange("p n (j d) -> p n j d", j=QUAD)).then_inc(values_ready, 1)

            def copy(s):
                dve.wait_ge(steps_done, s * NS + NS)
                nc.vector.tensor_copy(out_t[:, bass.ds(s * T, T)], acc[:, :]).then_inc(acc_copied, 1)

            prepare(0, 0)
            prepare(1, 1)

            with dve.Fori(0, QUADS // 2 - 1) as u:
                copy(u * 2)
                prepare(u * 2 + 2, 0)
                copy(u * 2 + 1)
                prepare(u * 2 + 3, 1)
            copy(QUADS - 2)
            copy(QUADS - 1)


E1 = 8
CAPACITY = B * T // E1


def experts(nc, consts, w_router, b_router, w1, b1, w2, b2, x2, out_t, out):
    N = B * NB
    with ExitStack() as ctx:
        def sb(name, shape, dt=F32):
            return ctx.enter_context(nc.sbuf_tensor("e_" + name, shape, dt))

        def sem(name):
            return ctx.enter_context(nc.semaphore("e_" + name))

        bank = [ctx.enter_context(nc.psum_tensor(f"e_bank{n}", [P, HALF], F32)) for n in range(8)]

        def blocks(x):
            return x[:, :].rearrange("p (j d) -> p j d", j=GB)

        CW = 3 * P + E1
        consts_f = sb("consts", [P, CW])
        wr, br = sb("wr", [P, E1]), sb("br", [P, E1])
        w1s, w2s = sb("w1", [P, E1, P]), sb("w2", [P, E1, P])
        b1s, b2s = sb("b1", [P, E1]), sb("b2", [E1, P])
        upto = sb("upto", [P, P], BF16)
        ones = sb("ones", [P, P], BF16)
        x3 = sb("x3", [P, N, P])
        x3t = sb("x3t", [P, N * P])
        gx = sb("gx", [P, N, P])
        gxt = sb("gxt", [P, N * P])
        logits = sb("logits", [P, N, E1])
        ex = sb("ex", [P, N, E1])
        tied = sb("tied", [P, N, E1])
        top = sb("top", [P, N])
        gate = sb("gate", [P, N])
        chosen = sb("chosen", [P, N, E1], BF16)
        weight = sb("weight", [P, N, E1])
        weight_t = sb("weightt", [E1, N * P])
        y = sb("y", [P, N, P])
        hid = [sb(f"hid{n}", [P, HALF]) for n in range(2)]
        final = sb("final", [P, N, P])
        eps = sb("eps", [P, 1])

        loaded = sem("loaded")
        setup_done = sem("setup_done")
        attn_psum = sem("attn_psum")
        attn_read = sem("attn_read")
        x3_ready = sem("x3_ready")
        x3t_psum = sem("x3t_psum")
        x3t_ready = sem("x3t_ready")
        logits_psum = sem("logits_psum")
        shifted_ready = sem("shifted_ready")
        exp_ready = sem("exp_ready")
        chosen_ready = sem("chosen_ready")
        places_psum = sem("places_psum")
        gx_ready = sem("gx_ready")
        gxt_psum = sem("gxt_psum")
        gxt_ready = sem("gxt_ready")
        weight_ready = sem("weight_ready")
        weight_psum = sem("weight_psum")
        weight_t_ready = sem("weight_t_ready")
        bias_psum = sem("bias_psum")
        hid_psum = sem("hid_psum")
        hid_ready = sem("hid_ready")
        expert_psum = sem("expert_psum")
        expert_read = sem("expert_read")
        final_ready = sem("final_ready")
        stored = sem("stored")
        routed = sem("routed")
        norm3 = norm_buffers(sb, sem, "norm3")
        norm4 = norm_buffers(sb, sem, "norm4")

        block = ctx.enter_context(nc.Block())

        @block.sync
        def _(sp):
            for dst, src in ((consts_f[:, :], consts), (wr[:, :], w_router), (br[:, :], b_router.partition_broadcast(P)),
                             (w1s[:, :, :], w1), (w2s[:, :, :], w2), (b1s[:, :], b1), (b2s[:, :], b2)):
                sp.dma_start(dst, src).then_inc(loaded, 16)
            for g in range(GROUPS):
                sp.wait_ge(final_ready, g + 1)
                gs = slice(g * GB, (g + 1) * GB)
                sp.dma_start(out[:, gs, :], final[:, gs, :]).then_inc(stored, 16)
            sp.wait_ge(stored, 16 * GROUPS)

        @block.tensor
        def _(pe):
            ident = consts_f[:, 0:P]
            pe.wait_ge(loaded, 16 * 7)
            pe.wait_ge(setup_done, 1)
            quads = QUADS // B
            for n in range(N):
                if n >= 4:
                    pe.wait_ge(attn_read, n - 3)
                for q in range(quads):
                    c0 = (n // NB * quads + q) * T + n % NB * P
                    m = pe.transpose(bank[n % 4][:, q * P:(q + 1) * P], out_t[:, c0:c0 + P], ident)
                m.then_inc(attn_psum, 1)
            for g in range(GROUPS):
                pe.wait_ge(x3_ready, g + 1)
                for j in range(GB):
                    m = pe.transpose(bank[4 + g][:, j * P:(j + 1) * P], x3[:, g * GB + j, :], ident)
                m.then_inc(x3t_psum, 1)
            pe.wait_ge(attn_read, N)
            for g in range(GROUPS):
                pe.wait_ge(x3t_ready, g + 1)
                for n in range(g * GB, (g + 1) * GB):
                    m = pe.matmul(bank[0][:, n * E1:(n + 1) * E1], x3t[:, n * P:(n + 1) * P], wr[:, :], start=True, stop=True)
            m.then_inc(logits_psum, 1)
            pe.wait_ge(chosen_ready, 1)
            places = bank[1][:, 0:N * E1].rearrange("p (n e) -> p n e", n=N)
            pe.matmul(places, upto[:, :], chosen[:, :, :], start=True, stop=True)
            for back in range(1, N):
                m = pe.matmul(places[:, back:N, :], ones[:, :], chosen[:, 0:N - back, :], start=False, stop=True,
                              skip_group_check=True)
            m.then_inc(places_psum, 1)
            pe.wait_ge(x3t_ready, GROUPS)
            for g in range(GROUPS):
                pe.wait_ge(gx_ready, g + 1)
                for j in range(GB):
                    m = pe.transpose(bank[4 + g][:, j * P:(j + 1) * P], gx[:, g * GB + j, :], ident)
                m.then_inc(gxt_psum, 1)
            pe.wait_ge(weight_ready, 1)
            for n in range(N):
                m = pe.transpose(bank[n // GB][0:E1, n % GB * P:(n % GB + 1) * P], weight[:, n, :], ident)
            m.then_inc(weight_psum, 1)
            pe.wait_ge(gxt_ready, GROUPS)
            for g in range(GROUPS):
                pe.wait_ge(weight_t_ready, g + 1)
                for j in range(GB):
                    n = g * GB + j
                    m = pe.matmul(bank[4 + g][:, j * P:(j + 1) * P], weight_t[:, n * P:(n + 1) * P], b2s[:, :], start=True, stop=True)
                m.then_inc(bias_psum, 1)

            def hidden(step):
                g, x = step // E1, step % E1
                if step >= 2:
                    pe.wait_ge(hid_ready, step - 1)
                pe.matmul(bank[step % 2][:, :], w1s[:, x, :], gxt[:, g * HALF:(g + 1) * HALF], start=True,
                          stop=True).then_inc(hid_psum, 1)

            def output(step):
                g, x = step // E1, step % E1
                pe.wait_ge(hid_ready, step + 1)
                if step >= 2:
                    pe.wait_ge(expert_read, step - 1)
                for j in range(GB):
                    m = pe.matmul(bank[2 + step % 2][:, j * P:(j + 1) * P], hid[step % 2][:, j * P:(j + 1) * P], w2s[:, x, :],
                                  start=True, stop=True)
                m.then_inc(expert_psum, 1)

            for step in range(GROUPS * E1):
                hidden(step)
                if step >= 1:
                    output(step - 1)
            output(GROUPS * E1 - 1)

        @block.scalar
        def _(act):
            act.wait_ge(setup_done, 1)
            norm_root(nc, act, norm3, 0, eps[:, :])
            for g in range(GROUPS):
                if g + 1 < GROUPS:
                    norm_root(nc, act, norm3, g + 1, eps[:, :])
                act.wait_ge(x3t_psum, g + 1)
                nc.scalar.activation(x3t[:, g * HALF:(g + 1) * HALF], bank[4 + g][:, :], ACT.Copy).then_inc(x3t_ready, 1)
            act.wait_ge(shifted_ready, 1)
            nc.scalar.activation(ex[:, :, :], ex[:, :, :], ACT.Exp).then_inc(exp_ready, 1)
            for g in range(GROUPS):
                act.wait_ge(gxt_psum, g + 1)
                nc.scalar.activation(gxt[:, g * HALF:(g + 1) * HALF], bank[4 + g][:, :], ACT.Copy).then_inc(gxt_ready, 1)
            act.wait_ge(weight_psum, 1)
            for g in range(GROUPS):
                nc.scalar.activation(weight_t[:, g * HALF:(g + 1) * HALF], bank[g][0:E1, :], ACT.Copy).then_inc(weight_t_ready, 1)
            for step in range(GROUPS * E1):
                act.wait_ge(hid_psum, step + 1)
                if step >= 2:
                    act.wait_ge(expert_psum, step - 1)
                nc.scalar.activation(hid[step % 2][:, :], bank[step % 2][:, :], ACT.Relu,
                                     bias=b1s[:, step % E1:step % E1 + 1]).then_inc(hid_ready, 1)
                if step % E1 == 3 and step > E1:
                    norm_root(nc, act, norm4, step // E1 - 1, eps[:, :])
            norm_root(nc, act, norm4, GROUPS - 1, eps[:, :])

        @block.vector
        def _(dve):
            dve.wait_ge(loaded, 16 * 7)
            nc.vector.memset(ones[:, :], 1.0)
            nc.vector.memset(eps[:, :], EPS)
            nc.vector.tensor_copy(upto[:, :], consts_f[:, 2 * P:3 * P]).then_inc(setup_done, 1)
            quads = QUADS // B
            def rows(g):
                return slice(g * GB, (g + 1) * GB)

            def residual3(g):
                for n in range(g * GB, (g + 1) * GB):
                    dve.wait_ge(attn_psum, n + 1)
                    attn = bank[n % 4][:, :].rearrange("p (h c) -> p h c", h=H1)[:, :, 0:DH1]
                    nc.vector.tensor_tensor(y[:, n, :].rearrange("p (h c) -> p h c", h=H1), attn,
                                            x2[:, n, :].rearrange("p (h c) -> p h c", h=H1), ALU.add).then_inc(attn_read, 1)
                dve.wait_ge(attn_read, (g + 1) * GB)
                if g >= 2:
                    dve.wait_ge(x3_ready, g - 1)
                norm_statistics(nc, dve, norm3, g, y[:, rows(g), :])

            residual3(0)
            for g in range(GROUPS):
                if g + 1 < GROUPS:
                    residual3(g + 1)
                norm_apply(nc, dve, norm3, g, y[:, rows(g), :], x3[:, rows(g), :], x3_ready)

            def wide(x):
                return x[:, :].unsqueeze(2).broadcast_to([P, N, E1])

            dve.wait_ge(logits_psum, 1)
            nc.vector.tensor_tensor(logits[:, :, :], bank[0][:, 0:N * E1].rearrange("p (n e) -> p n e", n=N),
                                         br[:, :].unsqueeze(1).broadcast_to([P, N, E1]), ALU.add).then_inc(routed, 1)
            dve.wait_ge(routed, 1)
            nc.vector.tensor_reduce(top[:, :], logits[:, :, :], AX.X, ALU.max).then_inc(routed, 1)
            dve.wait_ge(routed, 2)
            nc.vector.tensor_tensor(ex[:, :, :], logits[:, :, :], wide(top), ALU.subtract).then_inc(shifted_ready, 1)
            nc.vector.tensor_tensor(tied[:, :, :], logits[:, :, :], wide(top), ALU.is_equal).then_inc(routed, 1)
            dve.wait_ge(routed, 3)
            nc.vector.tensor_tensor(tied[:, :, :], tied[:, :, :],
                                         consts_f[:, 3 * P:3 * P + E1].unsqueeze(1).broadcast_to([P, N, E1]), ALU.mult).then_inc(routed, 1)
            dve.wait_ge(routed, 4)
            nc.vector.tensor_reduce(top[:, :], tied[:, :, :], AX.X, ALU.max).then_inc(routed, 1)
            dve.wait_ge(routed, 5)
            nc.vector.tensor_tensor(chosen[:, :, :], tied[:, :, :], wide(top), ALU.is_equal).then_inc(chosen_ready, 1)
            dve.wait_ge(exp_ready, 1)
            nc.vector.tensor_reduce(gate[:, :], ex[:, :, :], AX.X, ALU.add).then_inc(routed, 1)
            dve.wait_ge(routed, 6)
            nc.vector.reciprocal(gate[:, :], gate[:, :]).then_inc(routed, 1)
            dve.wait_ge(routed, 7)
            for g in range(GROUPS):
                gs = slice(g * GB, (g + 1) * GB)
                nc.vector.tensor_tensor(gx[:, gs, :], x3[:, gs, :], gate[:, gs].unsqueeze(2).broadcast_to([P, GB, P]),
                                        ALU.mult).then_inc(gx_ready, 1)
            dve.wait_ge(places_psum, 1)
            dve.wait_ge(chosen_ready, 1)
            nc.vector.tensor_scalar(tied[:, :, :], bank[1][:, 0:N * E1].rearrange("p (n e) -> p n e", n=N),
                                         float(CAPACITY), None, ALU.is_lt).then_inc(routed, 1)
            dve.wait_ge(routed, 8)
            nc.vector.tensor_tensor(tied[:, :, :], tied[:, :, :], chosen[:, :, :], ALU.mult).then_inc(routed, 1)
            dve.wait_ge(routed, 9)
            nc.vector.tensor_tensor(weight[:, :, :], tied[:, :, :], wide(gate), ALU.mult).then_inc(weight_ready, 1)
            for g in range(GROUPS):
                gs = slice(g * GB, (g + 1) * GB)
                dve.wait_ge(bias_psum, g + 1)
                nc.vector.tensor_tensor(y[:, gs, :], blocks(bank[4 + g]), x3[:, gs, :], ALU.add).then_inc(routed, 1)
            dve.wait_ge(routed, 13)
            dve.wait_ge(weight_ready, 1)
            for g in range(GROUPS):
                gs = slice(g * GB, (g + 1) * GB)
                for x in range(E1):
                    step = g * E1 + x
                    dve.wait_ge(expert_psum, step + 1)
                    if step >= 1:
                        dve.wait_ge(expert_read, step)
                    for j in range(GB):
                        n = g * GB + j
                        m = nc.vector.scalar_tensor_tensor(y[:, n, :], bank[2 + step % 2][:, j * P:(j + 1) * P],
                                                           weight[:, n, x:x + 1], y[:, n, :], ALU.mult, ALU.add)
                    m.then_inc(expert_read, 1)
                dve.wait_ge(expert_read, (g + 1) * E1)
                if g >= 2:
                    dve.wait_ge(final_ready, g - 1)
                norm_statistics(nc, dve, norm4, g, y[:, gs, :])
                if g >= 1:
                    norm_apply(nc, dve, norm4, g - 1, y[:, rows(g - 1), :], final[:, rows(g - 1), :], final_ready)
            norm_apply(nc, dve, norm4, GROUPS - 1, y[:, rows(GROUPS - 1), :], final[:, rows(GROUPS - 1), :], final_ready)


def build(nc, a, out):
    q_parts = nc.dram_tensor("q_parts", (PARTS, P, B * T), BF16, kind="Internal").ap()
    k_parts = nc.dram_tensor("k_parts", (PARTS, P, B * T), BF16, kind="Internal").ap()
    with ExitStack() as ctx:
        x2 = ctx.enter_context(nc.sbuf_tensor("x2", [P, B * NB, P], F32))
        x2_signed = ctx.enter_context(nc.sbuf_tensor("x2_signed", [P, B * NB, P], F32))
        with nc.sbuf_tensor("z_t", [P, STEPS * T], F32) as z_t:
            softmax_attention(nc, a["x_t"], a["w_pairs"], a["consts"][:, 0:2 * P], z_t)
            channel_mix(nc, a["x_rows"], a["w_o"], a["w_rkv"], a["columns"], a["sign_v"], a["consts"][:, 0:P], z_t,
                        x2, x2_signed, q_parts, k_parts)
        out_t = ctx.enter_context(nc.sbuf_tensor("out_t", [P, QUADS * T], F32))
        sigmoid_attention(nc, a["consts"][:, 0:2 * P], q_parts, k_parts, x2_signed, out_t)
        experts(nc, a["consts"], a["w_router"], a["b_router"], a["w1"], a["b1"], a["w2"], a["b2"], x2, out_t, out)


def kernel(**inputs):
    import numpy as np
    import concourse.bacc as bacc
    from concourse.bass_utils import run_bass_kernel_spmd

    x = {name: np.asarray(value) for name, value in inputs.items()}

    def rows(y):
        return y.reshape(-1, P, y.shape[-1]).transpose(1, 0, 2)

    heads = np.stack([x["L0_attn_W_K"], x["L0_attn_W_Q"], x["L0_attn_W_V"]])
    e1 = x["L1_ffn_W1"].shape[0]
    arrays = {
        "x_t": x["L0_attn_x"].transpose(0, 2, 1).reshape(B * P, T),
        "x_rows": rows(x["L0_attn_x"]),
        "w_pairs": heads.reshape(3, PAIRS, P, P).transpose(1, 3, 0, 2).reshape(PAIRS * P, 3 * P),
        "w_o": x["L0_attn_W_O"].reshape(P, PAIRS, P).transpose(2, 1, 0),
        "w_rkv": np.stack([x["L0_ffn_W_r"].T, x["L0_ffn_W_k"].T, x["L0_ffn_W_v"].T], axis=1),
        "columns": np.stack([x["L0_ffn_mu_r"], x["L0_ffn_mu_k"], x["L1_attn_bv_q"].reshape(-1),
                             x["L1_attn_bv_k"].reshape(-1)], axis=1),
        "sign_v": x["L1_attn_bv_v"].reshape(-1),
        "w_router": x["L1_ffn_Wr"],
        "b_router": x["L1_ffn_br"],
        "w1": x["L1_ffn_W1"].transpose(1, 0, 2),
        "b1": x["L1_ffn_b1"].T,
        "w2": x["L1_ffn_W2"].transpose(1, 0, 2),
        "b2": x["L1_ffn_b2"],
        "consts": np.concatenate([np.eye(P), np.tril(np.ones((P, P))), np.triu(np.ones((P, P))),
                                  np.tile(np.arange(e1, 0, -1), (P, 1))], axis=1).astype(np.float32),
    }
    arrays = {name: np.ascontiguousarray(value) for name, value in arrays.items()}
    nc = bacc.Bacc("TRN2", target_bir_lowering=False, num_devices=1)
    a = {name: nc.dram_tensor(f"in_{name}", value.shape, mybir.dt.from_np(value.dtype), kind="ExternalInput").ap()
         for name, value in arrays.items()}
    out = nc.dram_tensor("out", (P, B * NB, P), F32, kind="ExternalOutput").ap()
    build(nc, a, out)
    result = run_bass_kernel_spmd(nc, [{f"in_{name}": value for name, value in arrays.items()}], core_ids=[0])
    return result.results[0]["out"].transpose(1, 0, 2).reshape(B, T, P)
```

```python
from contextlib import ExitStack

import concourse.bass as bass
from concourse import mybir

ALU = mybir.AluOpType
ACT = mybir.ActivationFunctionType
AX = mybir.AxisListType
F32 = mybir.dt.float32
F32R = mybir.dt.float32r
BF16 = mybir.dt.bfloat16

P = 128
B = 2
T = 1024
NB = T // P
HALF = 512

PAIRS = 8
DH0 = 64
STEPS = B * PAIRS
TILES = [[(0, 7)], [(1, 7)], [(0, 6)], "k", "q", [(1, 6)], [(0, 5)], [(1, 5)], [(1, 4)], "v", [(1, 3), (1, 2)], [(0, 4)], [(0, 3), (0, 2)], [(0, 1), (0, 0)], [(1, 1), (1, 0)]]
SLOTS = 3
SCALE_AT = {1: [(1, 1)], 2: [(1, 0), (0, 7)], 6: [(0, 6)], 9: [(0, 5)], 12: [(0, 4)], 13: [(0, 3), (0, 2)]}
WEIGH_AT = {1: [(1, 3)], 2: [(1, 2)], 4: [(1, 1), (1, 0)], 6: [(0, 7)], 9: [(0, 6)], 12: [(0, 5)], 13: [(0, 4)]}
COPY_AT = 4


def left_over(table):
    return [i for k in sorted(table) for back, i in table[k] if back]


UNITS = [unit for tile in TILES if tile not in ("k", "q", "v") for unit in tile]
UNIT_AT = {unit: n for n, unit in enumerate(UNITS)}
PIECES = {7: [(0, 0, 512), (512, 512, 512)], 6: [(0, 0, 512), (512, 512, 384)],
          5: [(128, 0, 384), (512, 384, 384)], 4: [(256, 0, 256), (512, 256, 384)],
          3: [(0, 0, 512)], 2: [(512, 0, 384)], 1: [(0, 0, 256)], 0: [(512, 0, 256)]}
RING = 4


def softmax_attention(nc, psum, x_t, w_pairs, consts, z_t):
    with ExitStack() as ctx:
        def sb(name, shape, dt=F32):
            return ctx.enter_context(nc.sbuf_tensor("a0_" + name, shape, dt))

        def sem(name):
            return ctx.enter_context(nc.semaphore("a0_" + name))

        tiles = [psum[:, 2 * n * HALF:2 * (n + 1) * HALF] for n in range(SLOTS)]
        z_acc = psum[:, 2 * SLOTS * HALF:]

        w_cur = [sb(f"w{n}", [P, 3 * P]) for n in range(2)]
        x_cur = [sb(f"x{n}", [P, T]) for n in range(2)]
        x_hi, x_lo = sb("x_hi", [P, B * T], F32R), sb("x_lo", [P, B * T], F32R)
        w_hi, w_lo = ([sb(f"{s}{n}", [P, 2 * P], F32R) for n in range(2)] for s in ("w_hi", "w_lo"))
        k_hi, k_lo, q_hi, q_lo = (sb(n, [P, T], F32R) for n in ("k_hi", "k_lo", "q_hi", "q_lo"))
        k_stack, qh_stack, ql_stack = ([[sb(f"{s}{n}{h}", [P, T], F32R) for h in range(2)] for n in range(2)]
                                       for s in ("ks", "qh", "ql"))
        v_cur = [sb(f"v{n}", [P, T]) for n in range(2)]
        v_scaled = [sb(f"vs{n}", [P, 2, DH0]) for n in range(RING)]
        e = [[sb(f"e{h}{n}", [P, T]) for n in range(RING)] for h in range(2)]
        row_min = sb("min", [P, 2, NB])
        row_sum = sb("sum", [P, 2, NB])
        row_rec = sb("rec", [P, NB, 2])
        consts_f = sb("consts", [P, 2 * P])
        ident = sb("ident", [P, P], BF16)
        above = sb("above", [P, P], BF16)

        consts_loaded = sem("consts_loaded")
        consts_ready = sem("consts_ready")
        operands_loaded = [sem(f"operands_loaded{n}") for n in range(2)]
        x_loaded = [sem(f"x_loaded{b}") for b in range(B)]
        x_high_ready = sem("x_high_ready")
        x_low_ready = sem("x_low_ready")
        w_high_ready = sem("w_high_ready")
        w_low_ready = sem("w_low_ready")
        proj_ready = sem("proj_ready")
        high_ready = sem("high_ready")
        low_ready = sem("low_ready")
        v_ready = sem("v_ready")
        stacked = [sem(f"stacked{h}") for h in range(2)]
        scores_ready = sem("scores_ready")
        min_ready = sem("min_ready")
        exp_ready = sem("exp_ready")
        rec_ready = sem("rec_ready")
        v_scaled_ready = sem("v_scaled_ready")
        z_steps = sem("z_steps")
        z_copied = sem("z_copied")

        def ring_free(eng, s, i):
            if not (isinstance(s, int) and 8 * s + 7 - i < RING):
                eng.wait_ge(z_steps, s * 8 + (8 - i - RING))

        block = ctx.enter_context(nc.Block())

        @block.sync
        def _(sp):
            x_raw = e[0][0][:, :], e[0][1][:, :]

            def load_operands(n, par):
                sp.dma_start(w_cur[par][:, :], w_pairs[bass.ds(n % PAIRS * P, P), :]).then_inc(operands_loaded[par], 16)
                sp.dma_start(x_cur[par][:, :], x_t[bass.ds(n // PAIRS * P, P), :]).then_inc(operands_loaded[par], 16)

            def stack(n, par):
                heads = [(h, slice(h * DH0, (h + 1) * DH0)) for h in range(2)]
                sp.wait_ge(low_ready, n * 2 + 1)
                for h, rows in heads:
                    for half, part in ((slice(0, DH0), k_hi), (slice(DH0, P), k_lo)):
                        sp.dma_start(k_stack[par][h][half, :].bitcast(F32), part[rows, :].bitcast(F32)).then_inc(stacked[h], 16)
                sp.wait_ge(low_ready, n * 2 + 2)
                for h, rows in heads:
                    for half in (slice(0, DH0), slice(DH0, P)):
                        sp.dma_start(qh_stack[par][h][half, :].bitcast(F32), q_hi[rows, :].bitcast(F32)).then_inc(stacked[h], 16)
                        sp.dma_start(ql_stack[par][h][half, :].bitcast(F32), q_lo[rows, :].bitcast(F32)).then_inc(stacked[h], 16)

            def body(s, par):
                stack(s + 1, 1 - par)
                if not (isinstance(s, int) and s == STEPS - 2):
                    sp.wait_ge(v_ready, s + 2)
                    load_operands(s + 3, 1 - par)

            sp.dma_start(x_raw[0], x_t[0:P, :]).then_inc(x_loaded[0], 16)
            load_operands(0, 0)
            sp.dma_start(consts_f[:, :], consts).then_inc(consts_loaded, 16)
            sp.dma_start(x_raw[1], x_t[P:2 * P, :]).then_inc(x_loaded[1], 16)
            load_operands(1, 1)
            stack(0, 0)
            sp.wait_ge(v_ready, 1)
            load_operands(2, 0)
            body(0, 0)
            with sp.Fori(0, STEPS // 2 - 2) as u:
                body(u * 2 + 1, 1)
                body(u * 2 + 2, 0)
            for s in range(STEPS - 3, STEPS - 1):
                stack(s + 1, (s + 1) % 2)

        @block.tensor
        def _(pe):
            def project(n, par, what, tile):
                c = "kqv".index(what)
                if what == "k":
                    pe.wait_ge(w_low_ready, n + 1)
                    pe.wait_ge(operands_loaded[par], n * 16 + (16 if par else 32))
                if what == "v":
                    for i in range(NB):
                        m = pe.matmul(tile[:, i * P:(i + 1) * P], x_cur[par][:, i * P:(i + 1) * P],
                                      w_cur[par][:, c * P:(c + 1) * P], start=True, stop=True)
                else:
                    cs = slice(c * P, (c + 1) * P)
                    for c0 in (0, HALF):
                        at = bass.ds(n // PAIRS * T + c0, HALF)
                        pe.matmul(tile[:, c0:c0 + HALF], w_hi[par][:, cs], x_hi[:, at], start=True, stop=False)
                        pe.matmul(tile[:, c0:c0 + HALF], w_hi[par][:, cs], x_lo[:, at], start=False, stop=False)
                        m = pe.matmul(tile[:, c0:c0 + HALF], w_lo[par][:, cs], x_hi[:, at], start=False, stop=True)
                m.then_inc(proj_ready, 1)

            def scores(par, unit, tile):
                h, i = unit
                keys = k_stack[par][h][:, i * P:(i + 1) * P]
                pieces = PIECES[i]
                for col, q0, n in pieces:
                    out = tile[:, col:col + n]
                    diagonal = (col, q0, n) == pieces[-1]
                    pe.matmul(out, keys, qh_stack[par][h][:, q0:q0 + n], start=True, stop=False)
                    if diagonal:
                        diag = col + i * P - q0
                        pe.matmul(tile[:, diag:diag + P], ident[:, :], above[:, :], start=False, stop=False,
                                  skip_group_check=True)
                    m = pe.matmul(out, keys, ql_stack[par][h][:, q0:q0 + n], start=False, stop=True)
                m.then_inc(scores_ready, 1)

            def weigh(s, i):
                pe.wait_ge(v_scaled_ready, s * 8 + (8 - i))
                if i == NB - 1 and not (isinstance(s, int) and s == 0):
                    pe.wait_ge(z_copied, s)
                w = (i + 1) * P
                for c0, c1 in ((0, min(w, HALF)), (HALF, w)):
                    if c1 <= c0:
                        continue
                    for h in range(2):
                        m = pe.matmul(z_acc[h * DH0:(h + 1) * DH0, c0:c1], v_scaled[i % RING][:, h, :],
                                      e[h][i % RING][:, c0:c1], start=(i == NB - 1),
                                      stop=True, skip_group_check=True)
                m.then_inc(z_steps, 1)

            def tile_free(s, k):
                last = isinstance(s, int) and s == STEPS - 1
                k -= SLOTS
                while last and k >= 0 and TILES[k] in ("k", "q", "v"):
                    k -= SLOTS
                if k < 0:
                    s, k = s - 1, k + len(TILES)
                if isinstance(s, int) and s < 0:
                    return
                if TILES[k] == "v":
                    pe.wait_ge(v_ready, s + 2)
                elif TILES[k] in ("k", "q"):
                    pe.wait_ge(low_ready, (s + 1) * 2 + 1 + "kq".index(TILES[k]))
                else:
                    pe.wait_ge(exp_ready, s * 16 + UNIT_AT[TILES[k][-1]] + 1)

            def body(s, par):
                last = isinstance(s, int) and s == STEPS - 1
                for k, what in enumerate(TILES):
                    tile = tiles[k % SLOTS]
                    if what not in ("k", "q", "v"):
                        tile_free(s, k)
                        if k < 2:
                            pe.wait_ge(stacked[k], s * 96 + 96)
                        for unit in what:
                            scores(par, unit, tile)
                    elif not last:
                        tile_free(s, k)
                        project(s + 1, 1 - par, what, tile)
                    for back, i in WEIGH_AT.get(k, []):
                        if not (back and isinstance(s, int) and s == 0):
                            weigh(s - back, i)

            pe.wait_ge(x_low_ready, 1)
            for k, what in enumerate("kqv"):
                project(0, 0, what, tiles[k])
            pe.wait_ge(low_ready, 2)
            pe.wait_ge(v_ready, 1)
            pe.wait_ge(consts_ready, 1)
            body(0, 0)
            with pe.Fori(0, STEPS // 2 - 1) as u:
                body(u * 2 + 1, 1)
                body(u * 2 + 2, 0)
            body(STEPS - 1, 1)
            for i in left_over(WEIGH_AT):
                weigh(STEPS - 1, i)

        @block.scalar
        def _(act):
            def high(n, what, tile):
                c = "kq".index(what)
                act.wait_ge(proj_ready, n * 3 + (1 + c))
                if what == "k" and not (isinstance(n, int) and n == 0):
                    act.wait_ge(stacked[0], n * 96)
                    act.wait_ge(stacked[1], n * 96)
                if what == "k":
                    nc.scalar.activation(k_hi[:, :], tile[:, :], ACT.Copy).then_inc(high_ready, 1)
                else:
                    nc.scalar.activation(q_hi[:, :], tile[:, :], ACT.Copy, scale=-DH0 ** -0.5).then_inc(high_ready, 1)

            def split_weights(n, par):
                act.wait_ge(operands_loaded[par], n * 16 + (16 if par else 32))
                nc.scalar.activation(w_hi[par][:, :], w_cur[par][:, 0:2 * P], ACT.Copy).then_inc(w_high_ready, 1)

            def values(n, par, tile):
                act.wait_ge(proj_ready, n * 3 + 3)
                nc.scalar.activation(v_cur[par][:, :], tile[:, :], ACT.Copy).then_inc(v_ready, 1)

            def exponentials(s, unit, tile):
                h, i = unit
                n = UNIT_AT[unit]
                ring_free(act, s, i)
                act.wait_ge(min_ready, s * 16 + (n + 1))
                w, col = (i + 1) * P, PIECES[i][0][0]
                nc.scalar.activation(e[h][i % RING][:, 0:w], tile[:, col:col + w], ACT.Exp, bias=row_min[:, h, i:i + 1],
                                     scale=-1.0, accum_out=row_sum[:, h, i:i + 1]).then_inc(exp_ready, 1)

            def copy_z(s):
                act.wait_ge(z_steps, s * 8 + 8)
                nc.scalar.activation(z_t[:, bass.ds(s * T, T)], z_acc[:, :], ACT.Copy).then_inc(z_copied, 1)

            def body(s, par):
                last = isinstance(s, int) and s == STEPS - 1
                if not last:
                    split_weights(s + 1, 1 - par)
                for k, what in enumerate(TILES):
                    tile = tiles[k % SLOTS]
                    if what not in ("k", "q", "v"):
                        for unit in what:
                            exponentials(s, unit, tile)
                    elif what == "v" and not last:
                        values(s + 1, 1 - par, tile)
                    elif not last:
                        high(s + 1, what, tile)
                    if k == COPY_AT and not (isinstance(s, int) and s == 0):
                        copy_z(s - 1)

            def split_x(b):
                act.wait_ge(x_loaded[b], 16)
                nc.scalar.activation(x_hi[:, b * T:(b + 1) * T], e[0][b][:, :], ACT.Copy).then_inc(x_high_ready, 1)

            split_x(0)
            split_weights(0, 0)
            high(0, "k", tiles[0])
            high(0, "q", tiles[1])
            values(0, 0, tiles[2])
            split_x(1)
            act.wait_ge(x_low_ready, 2)
            body(0, 0)
            with act.Fori(0, STEPS // 2 - 1) as u:
                body(u * 2 + 1, 1)
                body(u * 2 + 2, 0)
            body(STEPS - 1, 1)
            copy_z(STEPS - 1)

        @block.vector
        def _(dve):
            def low(n, what, tile):
                c = "kq".index(what)
                dve.wait_ge(high_ready, n * 2 + (1 + c))
                if what == "k":
                    nc.vector.tensor_tensor(k_lo[:, :], tile[:, :], k_hi[:, :].bitcast(F32), ALU.subtract).then_inc(low_ready, 1)
                else:
                    nc.vector.scalar_tensor_tensor(q_lo[:, :], tile[:, :], -DH0 ** -0.5, q_hi[:, :].bitcast(F32), ALU.mult,
                                                   ALU.subtract).then_inc(low_ready, 1)

            def split_weights(n, par):
                dve.wait_ge(w_high_ready, n + 1)
                nc.vector.tensor_tensor(w_lo[par][:, :], w_cur[par][:, 0:2 * P], w_hi[par][:, :].bitcast(F32),
                                        ALU.subtract).then_inc(w_low_ready, 1)

            def minimum(s, unit, tile):
                h, i = unit
                dve.wait_ge(scores_ready, s * 16 + (UNIT_AT[unit] + 1))
                w, col = (i + 1) * P, PIECES[i][0][0]
                nc.vector.tensor_reduce(row_min[:, h, i:i + 1], tile[:, col:col + w], AX.X, ALU.min).then_inc(min_ready, 1)

            def scale_values(s, par, i):
                dve.wait_ge(exp_ready, s * 16 + (max(UNIT_AT[(0, i)], UNIT_AT[(1, i)]) + 1))
                nc.vector.reciprocal(row_rec[:, i, :], row_sum[:, :, i]).then_inc(rec_ready, 1)
                ring_free(dve, s, i)
                dve.wait_ge(rec_ready, s * 8 + (8 - i))
                nc.vector.tensor_tensor(v_scaled[i % RING][:, :, :],
                                        v_cur[par][:, i * P:(i + 1) * P].rearrange("p (h d) -> p h d", h=2),
                                        row_rec[:, i, :].unsqueeze(2).broadcast_to([P, 2, DH0]), ALU.mult).then_inc(v_scaled_ready, 1)

            def body(s, par):
                last = isinstance(s, int) and s == STEPS - 1
                for k, what in enumerate(TILES):
                    tile = tiles[k % SLOTS]
                    if what in ("k", "q") and not last:
                        low(s + 1, what, tile)
                    elif what not in ("k", "q", "v"):
                        for unit in what:
                            minimum(s, unit, tile)
                    if k == 0 and not last:
                        split_weights(s + 1, 1 - par)
                    for back, i in SCALE_AT.get(k, []):
                        if not (back and isinstance(s, int) and s == 0):
                            scale_values(s - back, (par + back) % 2, i)

            def split_x(b):
                dve.wait_ge(x_high_ready, b + 1)
                nc.vector.tensor_tensor(x_lo[:, b * T:(b + 1) * T], e[0][b][:, :], x_hi[:, b * T:(b + 1) * T].bitcast(F32),
                                        ALU.subtract).then_inc(x_low_ready, 1)

            split_x(0)
            split_weights(0, 0)
            dve.wait_ge(consts_loaded, 16)
            nc.vector.tensor_copy(ident[:, :], consts_f[:, 0:P])
            nc.vector.tensor_scalar(above[:, :], consts_f[:, P:2 * P], -1e30, 1e30, ALU.mult, ALU.add).then_inc(consts_ready, 1)
            low(0, "k", tiles[0])
            low(0, "q", tiles[1])
            split_x(1)
            body(0, 0)
            with dve.Fori(0, STEPS // 2 - 1) as u:
                body(u * 2 + 1, 1)
                body(u * 2 + 2, 0)
            body(STEPS - 1, 1)
            for i in left_over(SCALE_AT):
                scale_values(STEPS - 1, 1, i)


GB = HALF // P
GROUPS = B * NB // GB
EPS = 1e-5


def norm_buffers(sb, sem, name):
    return {"stats": [sb(f"{name}_stats{n}", [P, GB, 6]) for n in range(2)],
            "moments": [sb(f"{name}_moments{n}", [P, GB, 2]) for n in range(2)],
            "std": [sb(f"{name}_std{n}", [P, GB]) for n in range(2)],
            "stats_ready": sem(f"{name}_stats_ready"), "variance_ready": sem(f"{name}_variance_ready"),
            "std_ready": sem(f"{name}_std_ready"), "inverse_ready": sem(f"{name}_inverse_ready")}


def norm_statistics(nc, dve, norm, g, y):
    stats, moments = norm["stats"][g % 2], norm["moments"][g % 2]
    for j in range(GB):
        nc.vector.bn_stats(stats[:, j, :], y[:, j, :]).then_inc(norm["stats_ready"], 1)
    dve.wait_ge(norm["stats_ready"], (g + 1) * GB)
    for j in range(GB):
        nc.vector.bn_aggr(moments[:, j, :], stats[:, j, :]).then_inc(norm["variance_ready"], 1)


def norm_root(nc, act, norm, g, eps):
    act.wait_ge(norm["variance_ready"], (g + 1) * GB)
    nc.scalar.activation(norm["std"][g % 2][:, :], norm["moments"][g % 2][:, :, 1], ACT.Sqrt,
                         bias=eps).then_inc(norm["std_ready"], 1)


def norm_apply(nc, dve, norm, g, y, out, ready):
    std, moments = norm["std"][g % 2], norm["moments"][g % 2]
    dve.wait_ge(norm["std_ready"], g + 1)
    nc.vector.reciprocal(std[:, :], std[:, :]).then_inc(norm["inverse_ready"], 1)
    dve.wait_ge(norm["inverse_ready"], g + 1)
    for j in range(GB):
        last = nc.vector.tensor_scalar(out[:, j, :], y[:, j, :], moments[:, j, 0:1], std[:, j:j + 1],
                                       ALU.subtract, ALU.mult)
    last.then_inc(ready, 1)


H1 = 16
DH1 = 8
QUAD = 4
QUADS = B * H1 // QUAD
PARTS = 3
STACK = 96
BLOCK_STEPS = [[0], [1], [2], [3], [4, 5], [6, 7]]
KEY_PIECES = {0: [(0, 0, 512), (512, 512, 512)], 1: [(128, 128, 384), (512, 512, 512)],
              2: [(256, 256, 256), (512, 512, 512)], 3: [(384, 384, 128), (512, 512, 512)],
              4: [(512, 512, 512)], 5: [(128, 640, 384)], 6: [(0, 768, 256)], 7: [(256, 896, 128)]}
SPAN = [(0, 1024), (128, 1024), (256, 1024), (384, 1024), (128, 1024), (0, 384)]
RING1 = 3


def mix_and_sigmoid_attention(nc, psum, x_rows, w_o, w_rkv, columns, sign_v, consts, z_t, x2, q_parts, k_parts, out_t):
    with ExitStack() as ctx:
        def sb(name, shape, dt=F32):
            return ctx.enter_context(nc.sbuf_tensor("m_" + name, shape, dt))

        def sem(name):
            return ctx.enter_context(nc.semaphore("m_" + name))

        bank_a = [psum[:, g * HALF:(g + 1) * HALF] for g in range(GROUPS)]
        bank_b = [psum[:, (GROUPS + g) * HALF:(GROUPS + g + 1) * HALF] for g in range(GROUPS)]
        tiles = [psum[:, 2 * n * HALF:2 * (n + 1) * HALF] for n in range(SLOTS)]
        acc = psum[:, 2 * SLOTS * HALF:]

        def blocks(x):
            return x.rearrange("p (j d) -> p j d", j=GB)

        FREE = iter(range(0, QUADS * T, HALF))
        def in_out_t(width=HALF):
            starts = [next(FREE) for _ in range(width // HALF)]
            return out_t[:, starts[0]:starts[0] + width]

        x1 = in_out_t(B * T).rearrange("p (n d) -> p n d", d=P)
        mixed = [[in_out_t() for _ in range(2)] for _ in ("r", "k")]
        gate = [in_out_t() for _ in range(2)]
        y1 = [blocks(in_out_t()) for _ in range(2)]
        y2 = [blocks(in_out_t()) for _ in range(2)]
        k_act = in_out_t()
        rest = in_out_t()
        a = [[z_t[:, (j * RING1 + n) * T:(j * RING1 + n + 1) * T] for n in range(RING1)] for j in range(QUAD)]

        wo = sb("wo", [P, PAIRS, P])
        w3 = sb("w3", [P, 3, P])
        cols = sb("cols", [P, 8])
        sv = sb("sv", [P, P])
        sign_tmp = sb("sign_tmp", [P, P])
        consts_f = sb("consts", [P, 2 * P])
        x1t = sb("x1t", [P, B, T + 1])
        eps = sb("eps", [P, 1])
        parts = [sb(f"part{n}", [P, B * T], BF16) for n in range(PARTS)]
        signed = [sb(f"signed{n}", [P, B * T], BF16) for n in range(PARTS)]
        x2_signed = sb("x2_signed", [P, B * NB, P])
        q_stack = [sb(f"q{n}", [STACK, QUAD, T], BF16) for n in range(2)]
        k_stack = [sb(f"k{n}", [STACK, QUAD, T], BF16) for n in range(2)]
        values = [sb(f"v{n}", [P, NB, QUAD, 32]) for n in range(2)]
        ident = sb("ident", [P, P], BF16)
        below = sb("below", [P, P], BF16)

        w_o_loaded = sem("w_o_loaded")
        x_loaded = sem("x_loaded")
        small_loaded = sem("small_loaded")
        setup_done = sem("setup_done")
        out_ready = sem("out_ready")
        x1_ready = sem("x1_ready")
        x1t_psum = sem("x1t_psum")
        x1t_ready = sem("x1t_ready")
        prev_ready = sem("prev_ready")
        mixed_in = sem("mixed_in")
        rk_psum = sem("rk_psum")
        gate_ready = sem("gate_ready")
        relu_ready = sem("relu_ready")
        k_act_ready = sem("k_act_ready")
        v_psum = sem("v_psum")
        y1_ready = sem("y1_ready")
        gated_ready = sem("gated_ready")
        y2_ready = sem("y2_ready")
        x2_ready = sem("x2_ready")
        x2t_psum = sem("x2t_psum")
        high_ready = sem("high_ready")
        rest_ready = sem("rest_ready")
        mid_ready = sem("mid_ready")
        parts_ready = sem("parts_ready")
        signed_ready = sem("signed_ready")
        x2_signed_ready = sem("x2_signed_ready")
        parts_stored = [sem(f"parts_stored{b}") for b in range(B)]
        signs_half = sem("signs_half")
        signs_ready = sem("signs_ready")
        zeroed = sem("zeroed")
        values_zeroed = sem("values_zeroed")
        mask_half = sem("mask_half")
        first_queries = sem("first_queries")
        first_keys = sem("first_keys")
        stacked = [sem(f"stacked{n}") for n in range(2)]
        values_ready = sem("values_ready")
        scores_ready = sem("scores_ready")
        attn_ready = sem("attn_ready")
        steps_done = sem("steps_done")
        acc_copied = sem("acc_copied")
        norm1 = norm_buffers(sb, sem, "norm1")
        norm2 = norm_buffers(sb, sem, "norm2")

        MU_R, MU_K, SQ, SK, OMR, OMK, SS = range(7)
        NS = len(BLOCK_STEPS)
        NT = NS * QUAD
        LOADS = 2 * PARTS * PARTS * 16

        block = ctx.enter_context(nc.Block())

        def first(s):
            return isinstance(s, int) and s == 0

        def rows(g):
            return slice(g * GB, (g + 1) * GB)

        def tokens(g):
            return slice(g * HALF, (g + 1) * HALF)

        def stack_loads(s):
            h0, b = s % (QUADS // B) * (QUAD * DH1), s // (QUADS // B)
            for n in range(PARTS):
                for c in range(PARTS):
                    yield (slice((n * PARTS + c) * DH1, (n * PARTS + c + 1) * DH1),
                           q_parts[n, bass.ds(h0, QUAD * DH1), bass.ds(b * T, T)].rearrange("(j d) t -> d j t", j=QUAD),
                           k_parts[c, bass.ds(h0, QUAD * DH1), bass.ds(b * T, T)].rearrange("(j d) t -> d j t", j=QUAD))

        @block.sync
        def _(sp):
            sp.dma_start(wo[:, :, :], w_o).then_inc(w_o_loaded, 16)
            sp.dma_start(x1[:, :, :], x_rows).then_inc(x_loaded, 16)
            sp.dma_start(cols[:, 0:4], columns).then_inc(small_loaded, 16)
            sp.dma_start(sv[:, :], sign_v.partition_broadcast(P)).then_inc(small_loaded, 16)
            sp.dma_start(consts_f[:, :], consts).then_inc(small_loaded, 16)
            sp.dma_start(w3[:, :, :], w_rkv).then_inc(small_loaded, 16)

            def store(g):
                stored = parts_stored[g // (GROUPS // B)]
                sp.wait_ge(parts_ready, g + 1)
                for n in range(PARTS):
                    sp.dma_start(q_parts[n, :, tokens(g)], parts[n][:, tokens(g)]).then_inc(stored, 16)
                sp.wait_ge(signed_ready, (g + 1) * PARTS)
                for n in range(PARTS):
                    sp.dma_start(k_parts[n, :, tokens(g)], signed[n][:, tokens(g)]).then_inc(stored, 16)

            def load(s, par):
                for r, q_src, k_src in stack_loads(s):
                    sp.dma_start(q_stack[par][r, :, :], q_src).then_inc(stacked[par], 16)
                    sp.dma_start(k_stack[par][r, :, :], k_src).then_inc(stacked[par], 16)

            STORES = GROUPS // B * 2 * PARTS * 16
            store(0)
            store(1)
            sp.wait_ge(zeroed, 4)
            sp.wait_ge(parts_stored[0], STORES)
            for r, q_src, _ in stack_loads(0):
                sp.dma_start(q_stack[0][r, :, :], q_src).then_inc(first_queries, 16)
            store(2)
            store(3)
            load(1, 1)
            sp.wait_ge(parts_stored[1], STORES)

            def body(s, par):
                sp.wait_ge(scores_ready, (s - 1) * NT)
                load(s, par)

            with sp.Fori(1, QUADS // 2) as u:
                body(u * 2, 0)
                body(u * 2 + 1, 1)

        @block.gpsimd
        def _(pool):
            for n in range(2):
                nc.gpsimd.memset(q_stack[n][64:STACK, :, :], 0.0).then_inc(zeroed, 1)
                nc.gpsimd.memset(k_stack[n][64:STACK, :, :], 0.0).then_inc(zeroed, 1)
            pool.wait_ge(zeroed, 4)
            for n in range(2):
                nc.gpsimd.memset(values[n][:, :, :, :], 0.0).then_inc(values_zeroed, 1)

            def sign_rows(g):
                pool.wait_ge(x2_ready, g + 1)
                nc.gpsimd.tensor_tensor(x2_signed[:, rows(g), :], x2[:, rows(g), :],
                                        sv[:, :].unsqueeze(1).broadcast_to([P, GB, P]), ALU.mult).then_inc(x2_signed_ready, 1)

            pool.wait_ge(setup_done, 1)
            sign_rows(0)
            sign_rows(1)
            pool.wait_ge(parts_stored[0], GROUPS // B * 2 * PARTS * 16)
            for r, _, k_src in stack_loads(0):
                pool.dma_start(k_stack[0][r, :, :], k_src).then_inc(first_keys, 16)
            sign_rows(2)
            sign_rows(3)

        @block.tensor
        def _(pe):
            def project(g, half):
                for j in range(half * GB // 2, (half + 1) * GB // 2):
                    n = g * GB + j
                    for pair in range(PAIRS):
                        step = n // NB * PAIRS + pair
                        m = pe.matmul(bank_a[g][:, j * P:(j + 1) * P],
                                      z_t[:, step * T + n % NB * P:step * T + (n % NB + 1) * P], wo[:, pair, :],
                                      start=(pair == 0), stop=(pair == PAIRS - 1))
                if half == 1:
                    m.then_inc(out_ready, 1)

            def transpose1(g):
                pe.wait_ge(x1_ready, g + 1)
                for j in range(GB):
                    m = pe.transpose(bank_b[g][:, j * P:(j + 1) * P], x1[:, g * GB + j, :], consts_f[:, 0:P])
                m.then_inc(x1t_psum, 1)

            def receptance_and_key(g):
                pe.wait_ge(mixed_in, 2 * g + 2)
                pe.matmul(bank_a[g], w3[:, 1, :], mixed[1][g % 2], start=True, stop=True).then_inc(rk_psum, 1)
                for j in range(GB):
                    m = pe.matmul(bank_b[g][:, j * P:(j + 1) * P], mixed[0][g % 2][:, j * P:(j + 1) * P], w3[:, 0, :],
                                  start=True, stop=True)
                m.then_inc(rk_psum, 1)

            def value(g):
                pe.wait_ge(k_act_ready, g + 1)
                for j in range(GB):
                    m = pe.matmul(bank_a[g][:, j * P:(j + 1) * P], k_act[:, j * P:(j + 1) * P], w3[:, 2, :],
                                  start=True, stop=True)
                m.then_inc(v_psum, 1)

            def transpose2(g):
                pe.wait_ge(x2_ready, g + 1)
                pe.wait_ge(gate_ready, g + 1)
                for j in range(GB):
                    m = pe.transpose(bank_b[g][:, j * P:(j + 1) * P], x2[:, g * GB + j, :], consts_f[:, 0:P])
                m.then_inc(x2t_psum, 1)

            pe.wait_ge(w_o_loaded, 16)
            project(0, 0)
            pe.wait_ge(small_loaded, 16 * 4)
            project(0, 1)
            project(1, 0)
            transpose1(0)
            project(1, 1)
            receptance_and_key(0)
            project(2, 0)
            value(0)
            transpose1(1)
            project(2, 1)
            receptance_and_key(1)
            transpose2(0)
            project(3, 0)
            transpose1(2)
            value(1)
            project(3, 1)
            receptance_and_key(2)
            transpose2(1)
            transpose1(3)
            value(2)
            transpose2(2)
            receptance_and_key(3)
            value(3)
            transpose2(3)

            def scores(s, par, k):
                for j in range(QUAD):
                    at = k * QUAD + j
                    tile = tiles[at % SLOTS]
                    if not (first(s) and at < SLOTS):
                        pe.wait_ge(attn_ready, s * NT + (at - SLOTS + 1))
                    for i in BLOCK_STEPS[k]:
                        keys = k_stack[par][:, j, i * P:(i + 1) * P]
                        for n, (col, q0, width) in enumerate(KEY_PIECES[i]):
                            out = tile[:, col:col + width]
                            if n == 0:
                                pe.matmul(out, keys, q_stack[par][:, j, q0:q0 + width], start=True, stop=True)
                                m = pe.matmul(tile[:, col:col + P], ident[:, :], below[:, :], start=False, stop=True,
                                              skip_group_check=True)
                            else:
                                m = pe.matmul(out, keys, q_stack[par][:, j, q0:q0 + width], start=True, stop=True)
                    m.then_inc(scores_ready, 1)

            def weigh(s, par, k):
                if k == 0:
                    pe.wait_ge(values_ready, s + 1)
                    if first(s):
                        pe.wait_ge(parts_ready, GROUPS)
                    else:
                        pe.wait_ge(acc_copied, s)
                pe.wait_ge(attn_ready, s * NT + (k + 1) * QUAD)
                for i in BLOCK_STEPS[k]:
                    for col, q0, width in KEY_PIECES[i]:
                        for j in range(QUAD):
                            m = pe.matmul(acc[32 * j:32 * j + 32, q0:q0 + width], values[par][:, i, j, :],
                                          a[j][k % RING1][:, col:col + width], start=(i == 0), stop=True,
                                          skip_group_check=True)
                m.then_inc(steps_done, 1)

            def body(s, par):
                if first(s):
                    pe.wait_ge(first_queries, LOADS // 2)
                    pe.wait_ge(first_keys, LOADS // 2)
                else:
                    pe.wait_ge(stacked[par], s * (LOADS // 2) + (LOADS // 2 if par else 0))
                for k in range(NS):
                    scores(s, par, k)
                    if k >= 1:
                        weigh(s, par, k - 1)
                    elif not first(s):
                        weigh(s - 1, 1 - par, NS - 1)

            pe.wait_ge(zeroed, 4)
            body(0, 0)
            with pe.Fori(0, QUADS // 2 - 1) as u:
                body(u * 2 + 1, 1)
                body(u * 2 + 2, 0)
            body(QUADS - 1, 1)
            weigh(QUADS - 1, 1, NS - 1)

        @block.scalar
        def _(act):
            def transposed1(g):
                act.wait_ge(x1t_psum, g + 1)
                b, t0 = g // 2, g % 2 * HALF
                nc.scalar.activation(x1t[:, b, 1 + t0:1 + t0 + HALF], bank_b[g], ACT.Copy).then_inc(x1t_ready, 1)
                act.wait_ge(x1t_ready, g + 1)
                if g >= 2:
                    act.wait_ge(rk_psum, 2 * g - 2)
                for n, c in ((0, OMR), (1, OMK)):
                    nc.scalar.activation(mixed[n][g % 2], x1t[:, b, t0:t0 + HALF], ACT.Identity,
                                         scale=cols[:, c:c + 1]).then_inc(prev_ready, 1)

            def relu_and_gates(g):
                act.wait_ge(rk_psum, 2 * g + 1)
                if g >= 1:
                    act.wait_ge(v_psum, g)
                nc.scalar.activation(k_act, bank_a[g], ACT.Relu).then_inc(relu_ready, 1)
                act.wait_ge(rk_psum, 2 * g + 2)
                if g >= 2:
                    act.wait_ge(gated_ready, g - 1)
                nc.scalar.activation(gate[g % 2], bank_b[g], ACT.Sigmoid).then_inc(gate_ready, 1)

            def high_parts(g):
                act.wait_ge(x2t_psum, g + 1)
                nc.scalar.activation(parts[0][:, tokens(g)], bank_b[g], ACT.Copy).then_inc(high_ready, 1)
                act.wait_ge(rest_ready, g + 1)
                nc.scalar.activation(parts[1][:, tokens(g)], rest, ACT.Copy).then_inc(mid_ready, 1)

            act.wait_ge(setup_done, 1)
            norm_root(nc, act, norm1, 0, eps[:, :])
            transposed1(0)
            norm_root(nc, act, norm1, 1, eps[:, :])
            relu_and_gates(0)
            transposed1(1)
            norm_root(nc, act, norm2, 0, eps[:, :])
            relu_and_gates(1)
            norm_root(nc, act, norm1, 2, eps[:, :])
            high_parts(0)
            transposed1(2)
            norm_root(nc, act, norm2, 1, eps[:, :])
            norm_root(nc, act, norm1, 3, eps[:, :])
            relu_and_gates(2)
            high_parts(1)
            transposed1(3)
            norm_root(nc, act, norm2, 2, eps[:, :])
            relu_and_gates(3)
            high_parts(2)
            norm_root(nc, act, norm2, 3, eps[:, :])
            high_parts(3)

            def body(s):
                for k in range(NS):
                    for j in range(QUAD):
                        at = k * QUAD + j
                        act.wait_ge(scores_ready, s * NT + (at + 1))
                        if not (first(s) and k < RING1) and j == 0:
                            act.wait_ge(steps_done, s * NS + (k - RING1 + 1))
                        c0, c1 = SPAN[k]
                        nc.scalar.activation(a[j][k % RING1][:, c0:c1], tiles[at % SLOTS][:, c0:c1], ACT.Sigmoid,
                                             scale=4.0 * DH1 ** -0.5).then_inc(attn_ready, 1)

            body(0)
            with act.Fori(1, QUADS) as s:
                body(s)

        @block.vector
        def _(dve):
            def sign(out, x, tmp, n):
                nc.vector.tensor_scalar(tmp, x, 0.0, None, ALU.is_lt)
                nc.vector.tensor_scalar(out, x, 0.0, None, ALU.is_gt).then_inc(signs_half, 1)
                dve.wait_ge(signs_half, n + 1)
                nc.vector.tensor_tensor(out, out, tmp, ALU.subtract).then_inc(signs_ready, 1)
                dve.wait_ge(signs_ready, n + 1)

            def residual1(g):
                if g >= 2:
                    dve.wait_ge(x1_ready, g - 1)
                dve.wait_ge(out_ready, g + 1)
                nc.vector.tensor_tensor(y1[g % 2], blocks(bank_a[g]), x1[:, rows(g), :], ALU.add).then_inc(y1_ready, 1)
                dve.wait_ge(y1_ready, g + 1)
                norm_statistics(nc, dve, norm1, g, y1[g % 2])

            def apply1(g):
                norm_apply(nc, dve, norm1, g, y1[g % 2], x1[:, rows(g), :], x1_ready)

            def mix(g):
                b, t0 = g // 2, g % 2 * HALF
                for n, c in ((0, MU_R), (1, MU_K)):
                    dve.wait_ge(prev_ready, 2 * g + n + 1)
                    nc.vector.scalar_tensor_tensor(mixed[n][g % 2], x1t[:, b, 1 + t0:1 + t0 + HALF], cols[:, c:c + 1],
                                                   mixed[n][g % 2], ALU.mult, ALU.add).then_inc(mixed_in, 1)

            def activate_key(g):
                dve.wait_ge(relu_ready, g + 1)
                nc.vector.tensor_tensor(k_act, bank_a[g], k_act, ALU.mult).then_inc(k_act_ready, 1)

            def residual2(g):
                if g >= 2:
                    dve.wait_ge(x2_ready, g - 1)
                dve.wait_ge(v_psum, g + 1)
                dve.wait_ge(gate_ready, g + 1)
                nc.vector.tensor_tensor(y2[g % 2], blocks(bank_a[g]), blocks(gate[g % 2]), ALU.mult).then_inc(gated_ready, 1)
                dve.wait_ge(gated_ready, g + 1)
                nc.vector.tensor_tensor(y2[g % 2], y2[g % 2], x1[:, rows(g), :], ALU.add).then_inc(y2_ready, 1)
                dve.wait_ge(y2_ready, g + 1)
                norm_statistics(nc, dve, norm2, g, y2[g % 2])

            def apply2(g):
                norm_apply(nc, dve, norm2, g, y2[g % 2], x2[:, rows(g), :], x2_ready)

            def low_parts(g):
                dve.wait_ge(high_ready, g + 1)
                if g >= 1:
                    dve.wait_ge(parts_ready, g)
                nc.vector.tensor_tensor(rest, bank_b[g], parts[0][:, tokens(g)], ALU.subtract).then_inc(rest_ready, 1)
                dve.wait_ge(mid_ready, g + 1)
                nc.vector.tensor_tensor(parts[2][:, tokens(g)], rest, parts[1][:, tokens(g)],
                                        ALU.subtract).then_inc(parts_ready, 1)

            def signed_parts(g):
                dve.wait_ge(parts_ready, g + 1)
                for n in range(PARTS):
                    nc.vector.tensor_scalar(signed[n][:, tokens(g)], parts[n][:, tokens(g)], cols[:, SS:SS + 1], None,
                                            ALU.mult).then_inc(signed_ready, 1)

            nc.vector.memset(eps[:, :], EPS)
            for b in range(B):
                nc.vector.memset(x1t[:, b, 0:1], 0.0)
            dve.wait_ge(small_loaded, 16 * 4)
            nc.vector.tensor_scalar(cols[:, OMR:OMK + 1], cols[:, MU_R:MU_K + 1], -1.0, 1.0, ALU.mult, ALU.add)
            sign(sv[:, :], sv[:, :], sign_tmp[:, :], 0)
            sign(cols[:, SQ:SK + 1], cols[:, SQ:SK + 1], sign_tmp[:, 0:2], 1)
            nc.vector.tensor_copy(ident[:, :], consts_f[:, 0:P])
            nc.vector.tensor_tensor(below[:, :], consts_f[:, P:2 * P], consts_f[:, 0:P], ALU.subtract).then_inc(mask_half, 1)
            dve.wait_ge(mask_half, 1)
            nc.vector.tensor_scalar(below[:, :], below[:, :], -1e30, None, ALU.mult)
            nc.vector.tensor_tensor(cols[:, SS:SS + 1], cols[:, SQ:SQ + 1], cols[:, SK:SK + 1], ALU.mult).then_inc(setup_done, 1)

            dve.wait_ge(x_loaded, 16)
            residual1(0)
            apply1(0)
            mix(0)
            residual1(1)
            activate_key(0)
            apply1(1)
            residual2(0)
            mix(1)
            residual1(2)
            apply2(0)
            activate_key(1)
            apply1(2)
            low_parts(0)
            signed_parts(0)
            residual2(1)
            mix(2)
            residual1(3)
            apply2(1)
            activate_key(2)
            apply1(3)
            low_parts(1)
            residual2(2)
            signed_parts(1)
            apply2(2)
            mix(3)
            activate_key(3)
            low_parts(2)
            residual2(3)
            apply2(3)
            low_parts(3)
            signed_parts(2)
            signed_parts(3)

            def prepare(s, par):
                b, h0 = s // (QUADS // B), s % (QUADS // B) * (QUAD * DH1)
                nc.vector.tensor_copy(values[par][:, :, :, 0:DH1],
                                      x2_signed[:, bass.ds(b * NB, NB), bass.ds(h0, QUAD * DH1)]
                                      .rearrange("p n (j d) -> p n j d", j=QUAD)).then_inc(values_ready, 1)

            def copy(s):
                dve.wait_ge(steps_done, s * NS + NS)
                nc.vector.tensor_copy(out_t[:, bass.ds(s * T, T)], acc).then_inc(acc_copied, 1)

            dve.wait_ge(values_zeroed, 2)
            dve.wait_ge(x2_signed_ready, GROUPS)
            prepare(0, 0)
            prepare(1, 1)

            with dve.Fori(0, QUADS // 2 - 1) as u:
                copy(u * 2)
                prepare(u * 2 + 2, 0)
                copy(u * 2 + 1)
                prepare(u * 2 + 3, 1)
            copy(QUADS - 2)
            copy(QUADS - 1)


E1 = 8
CAPACITY = B * T // E1


def experts(nc, psum, consts, w_router, b_router, w1, b1, w2, b2, x2, out_t, out):
    N = B * NB
    with ExitStack() as ctx:
        def sb(name, shape, dt=F32):
            return ctx.enter_context(nc.sbuf_tensor("e_" + name, shape, dt))

        def sem(name):
            return ctx.enter_context(nc.semaphore("e_" + name))

        bank = [psum[:, n * HALF:(n + 1) * HALF] for n in range(8)]

        def blocks(x):
            return x[:, :].rearrange("p (j d) -> p j d", j=GB)

        CW = 3 * P + E1
        consts_f = sb("consts", [P, CW])
        wr, br = sb("wr", [P, E1]), sb("br", [P, E1])
        w1s, w2s = sb("w1", [P, E1, P]), sb("w2", [P, E1, P])
        b1s, b2s = sb("b1", [P, E1]), sb("b2", [E1, P])
        upto = sb("upto", [P, P], BF16)
        ones = sb("ones", [P, P], BF16)
        x3 = sb("x3", [P, N, P])
        x3t = sb("x3t", [P, N * P])
        gx = sb("gx", [P, N, P])
        gxt = sb("gxt", [P, N * P])
        logits = sb("logits", [P, N, E1])
        ex = sb("ex", [P, N, E1])
        tied = sb("tied", [P, N, E1])
        top = sb("top", [P, N])
        gate = sb("gate", [P, N])
        chosen = sb("chosen", [P, N, E1], BF16)
        weight = sb("weight", [P, N, E1])
        weight_t = sb("weightt", [E1, N * P])
        y = sb("y", [P, N, P])
        hid = [sb(f"hid{n}", [P, HALF]) for n in range(2)]
        final = sb("final", [P, N, P])
        eps = sb("eps", [P, 1])

        loaded = sem("loaded")
        setup_done = sem("setup_done")
        attn_psum = sem("attn_psum")
        attn_read = sem("attn_read")
        x3_ready = sem("x3_ready")
        x3t_psum = sem("x3t_psum")
        x3t_ready = sem("x3t_ready")
        logits_psum = sem("logits_psum")
        shifted_ready = sem("shifted_ready")
        exp_ready = sem("exp_ready")
        chosen_ready = sem("chosen_ready")
        places_psum = sem("places_psum")
        gx_ready = sem("gx_ready")
        gxt_psum = sem("gxt_psum")
        gxt_ready = sem("gxt_ready")
        weight_ready = sem("weight_ready")
        weight_psum = sem("weight_psum")
        weight_t_ready = sem("weight_t_ready")
        bias_psum = sem("bias_psum")
        hid_psum = sem("hid_psum")
        hid_ready = sem("hid_ready")
        expert_psum = sem("expert_psum")
        expert_read = sem("expert_read")
        final_ready = sem("final_ready")
        stored = sem("stored")
        routed = sem("routed")
        norm3 = norm_buffers(sb, sem, "norm3")
        norm4 = norm_buffers(sb, sem, "norm4")

        block = ctx.enter_context(nc.Block())

        @block.sync
        def _(sp):
            for dst, src in ((consts_f[:, :], consts), (wr[:, :], w_router), (br[:, :], b_router.partition_broadcast(P)),
                             (w1s[:, :, :], w1), (w2s[:, :, :], w2), (b1s[:, :], b1), (b2s[:, :], b2)):
                sp.dma_start(dst, src).then_inc(loaded, 16)
            for g in range(GROUPS):
                sp.wait_ge(final_ready, g + 1)
                gs = slice(g * GB, (g + 1) * GB)
                sp.dma_start(out[:, gs, :], final[:, gs, :]).then_inc(stored, 16)
            sp.wait_ge(stored, 16 * GROUPS)

        @block.tensor
        def _(pe):
            ident = consts_f[:, 0:P]
            pe.wait_ge(loaded, 16 * 7)
            pe.wait_ge(setup_done, 1)
            quads = QUADS // B
            for n in range(N):
                if n >= 4:
                    pe.wait_ge(attn_read, n - 3)
                for q in range(quads):
                    c0 = (n // NB * quads + q) * T + n % NB * P
                    m = pe.transpose(bank[n % 4][:, q * P:(q + 1) * P], out_t[:, c0:c0 + P], ident)
                m.then_inc(attn_psum, 1)
            for g in range(GROUPS):
                pe.wait_ge(x3_ready, g + 1)
                for j in range(GB):
                    m = pe.transpose(bank[4 + g][:, j * P:(j + 1) * P], x3[:, g * GB + j, :], ident)
                m.then_inc(x3t_psum, 1)
            pe.wait_ge(attn_read, N)
            for g in range(GROUPS):
                pe.wait_ge(x3t_ready, g + 1)
                for n in range(g * GB, (g + 1) * GB):
                    m = pe.matmul(bank[0][:, n * E1:(n + 1) * E1], x3t[:, n * P:(n + 1) * P], wr[:, :], start=True, stop=True)
            m.then_inc(logits_psum, 1)
            pe.wait_ge(chosen_ready, 1)
            places = bank[1][:, 0:N * E1].rearrange("p (n e) -> p n e", n=N)
            pe.matmul(places, upto[:, :], chosen[:, :, :], start=True, stop=True)
            for back in range(1, N):
                m = pe.matmul(places[:, back:N, :], ones[:, :], chosen[:, 0:N - back, :], start=False, stop=True,
                              skip_group_check=True)
            m.then_inc(places_psum, 1)
            pe.wait_ge(x3t_ready, GROUPS)
            for g in range(GROUPS):
                pe.wait_ge(gx_ready, g + 1)
                for j in range(GB):
                    m = pe.transpose(bank[4 + g][:, j * P:(j + 1) * P], gx[:, g * GB + j, :], ident)
                m.then_inc(gxt_psum, 1)
            pe.wait_ge(weight_ready, 1)
            for n in range(N):
                m = pe.transpose(bank[n // GB][0:E1, n % GB * P:(n % GB + 1) * P], weight[:, n, :], ident)
            m.then_inc(weight_psum, 1)
            pe.wait_ge(gxt_ready, GROUPS)
            for g in range(GROUPS):
                pe.wait_ge(weight_t_ready, g + 1)
                for j in range(GB):
                    n = g * GB + j
                    m = pe.matmul(bank[4 + g][:, j * P:(j + 1) * P], weight_t[:, n * P:(n + 1) * P], b2s[:, :], start=True, stop=True)
                m.then_inc(bias_psum, 1)

            def hidden(step):
                g, x = step // E1, step % E1
                if step >= 2:
                    pe.wait_ge(hid_ready, step - 1)
                pe.matmul(bank[step % 2][:, :], w1s[:, x, :], gxt[:, g * HALF:(g + 1) * HALF], start=True,
                          stop=True).then_inc(hid_psum, 1)

            def output(step):
                g, x = step // E1, step % E1
                pe.wait_ge(hid_ready, step + 1)
                if step >= 2:
                    pe.wait_ge(expert_read, step - 1)
                for j in range(GB):
                    m = pe.matmul(bank[2 + step % 2][:, j * P:(j + 1) * P], hid[step % 2][:, j * P:(j + 1) * P], w2s[:, x, :],
                                  start=True, stop=True)
                m.then_inc(expert_psum, 1)

            for step in range(GROUPS * E1):
                hidden(step)
                if step >= 1:
                    output(step - 1)
            output(GROUPS * E1 - 1)

        @block.scalar
        def _(act):
            act.wait_ge(setup_done, 1)
            norm_root(nc, act, norm3, 0, eps[:, :])
            for g in range(GROUPS):
                if g + 1 < GROUPS:
                    norm_root(nc, act, norm3, g + 1, eps[:, :])
                act.wait_ge(x3t_psum, g + 1)
                nc.scalar.activation(x3t[:, g * HALF:(g + 1) * HALF], bank[4 + g][:, :], ACT.Copy).then_inc(x3t_ready, 1)
            act.wait_ge(shifted_ready, 1)
            nc.scalar.activation(ex[:, :, :], ex[:, :, :], ACT.Exp).then_inc(exp_ready, 1)
            for g in range(GROUPS):
                act.wait_ge(gxt_psum, g + 1)
                nc.scalar.activation(gxt[:, g * HALF:(g + 1) * HALF], bank[4 + g][:, :], ACT.Copy).then_inc(gxt_ready, 1)
            act.wait_ge(weight_psum, 1)
            for g in range(GROUPS):
                nc.scalar.activation(weight_t[:, g * HALF:(g + 1) * HALF], bank[g][0:E1, :], ACT.Copy).then_inc(weight_t_ready, 1)
            for step in range(GROUPS * E1):
                act.wait_ge(hid_psum, step + 1)
                if step >= 2:
                    act.wait_ge(expert_psum, step - 1)
                nc.scalar.activation(hid[step % 2][:, :], bank[step % 2][:, :], ACT.Relu,
                                     bias=b1s[:, step % E1:step % E1 + 1]).then_inc(hid_ready, 1)
                if step % E1 == 3 and step > E1:
                    norm_root(nc, act, norm4, step // E1 - 1, eps[:, :])
            norm_root(nc, act, norm4, GROUPS - 1, eps[:, :])

        @block.vector
        def _(dve):
            dve.wait_ge(loaded, 16 * 7)
            nc.vector.memset(ones[:, :], 1.0)
            nc.vector.memset(eps[:, :], EPS)
            nc.vector.tensor_copy(upto[:, :], consts_f[:, 2 * P:3 * P]).then_inc(setup_done, 1)
            quads = QUADS // B
            def rows(g):
                return slice(g * GB, (g + 1) * GB)

            def residual3(g):
                for n in range(g * GB, (g + 1) * GB):
                    dve.wait_ge(attn_psum, n + 1)
                    attn = bank[n % 4][:, :].rearrange("p (h c) -> p h c", h=H1)[:, :, 0:DH1]
                    nc.vector.tensor_tensor(y[:, n, :].rearrange("p (h c) -> p h c", h=H1), attn,
                                            x2[:, n, :].rearrange("p (h c) -> p h c", h=H1), ALU.add).then_inc(attn_read, 1)
                dve.wait_ge(attn_read, (g + 1) * GB)
                if g >= 2:
                    dve.wait_ge(x3_ready, g - 1)
                norm_statistics(nc, dve, norm3, g, y[:, rows(g), :])

            residual3(0)
            for g in range(GROUPS):
                if g + 1 < GROUPS:
                    residual3(g + 1)
                norm_apply(nc, dve, norm3, g, y[:, rows(g), :], x3[:, rows(g), :], x3_ready)

            def wide(x):
                return x[:, :].unsqueeze(2).broadcast_to([P, N, E1])

            dve.wait_ge(logits_psum, 1)
            nc.vector.tensor_tensor(logits[:, :, :], bank[0][:, 0:N * E1].rearrange("p (n e) -> p n e", n=N),
                                         br[:, :].unsqueeze(1).broadcast_to([P, N, E1]), ALU.add).then_inc(routed, 1)
            dve.wait_ge(routed, 1)
            nc.vector.tensor_reduce(top[:, :], logits[:, :, :], AX.X, ALU.max).then_inc(routed, 1)
            dve.wait_ge(routed, 2)
            nc.vector.tensor_tensor(ex[:, :, :], logits[:, :, :], wide(top), ALU.subtract).then_inc(shifted_ready, 1)
            nc.vector.tensor_tensor(tied[:, :, :], logits[:, :, :], wide(top), ALU.is_equal).then_inc(routed, 1)
            dve.wait_ge(routed, 3)
            nc.vector.tensor_tensor(tied[:, :, :], tied[:, :, :],
                                         consts_f[:, 3 * P:3 * P + E1].unsqueeze(1).broadcast_to([P, N, E1]), ALU.mult).then_inc(routed, 1)
            dve.wait_ge(routed, 4)
            nc.vector.tensor_reduce(top[:, :], tied[:, :, :], AX.X, ALU.max).then_inc(routed, 1)
            dve.wait_ge(routed, 5)
            nc.vector.tensor_tensor(chosen[:, :, :], tied[:, :, :], wide(top), ALU.is_equal).then_inc(chosen_ready, 1)
            dve.wait_ge(exp_ready, 1)
            nc.vector.tensor_reduce(gate[:, :], ex[:, :, :], AX.X, ALU.add).then_inc(routed, 1)
            dve.wait_ge(routed, 6)
            nc.vector.reciprocal(gate[:, :], gate[:, :]).then_inc(routed, 1)
            dve.wait_ge(routed, 7)
            for g in range(GROUPS):
                gs = slice(g * GB, (g + 1) * GB)
                nc.vector.tensor_tensor(gx[:, gs, :], x3[:, gs, :], gate[:, gs].unsqueeze(2).broadcast_to([P, GB, P]),
                                        ALU.mult).then_inc(gx_ready, 1)
            dve.wait_ge(places_psum, 1)
            dve.wait_ge(chosen_ready, 1)
            nc.vector.tensor_scalar(tied[:, :, :], bank[1][:, 0:N * E1].rearrange("p (n e) -> p n e", n=N),
                                         float(CAPACITY), None, ALU.is_lt).then_inc(routed, 1)
            dve.wait_ge(routed, 8)
            nc.vector.tensor_tensor(tied[:, :, :], tied[:, :, :], chosen[:, :, :], ALU.mult).then_inc(routed, 1)
            dve.wait_ge(routed, 9)
            nc.vector.tensor_tensor(weight[:, :, :], tied[:, :, :], wide(gate), ALU.mult).then_inc(weight_ready, 1)
            for g in range(GROUPS):
                gs = slice(g * GB, (g + 1) * GB)
                dve.wait_ge(bias_psum, g + 1)
                nc.vector.tensor_tensor(y[:, gs, :], blocks(bank[4 + g]), x3[:, gs, :], ALU.add).then_inc(routed, 1)
            dve.wait_ge(routed, 13)
            dve.wait_ge(weight_ready, 1)
            for g in range(GROUPS):
                gs = slice(g * GB, (g + 1) * GB)
                for x in range(E1):
                    step = g * E1 + x
                    dve.wait_ge(expert_psum, step + 1)
                    if step >= 1:
                        dve.wait_ge(expert_read, step)
                    for j in range(GB):
                        n = g * GB + j
                        m = nc.vector.scalar_tensor_tensor(y[:, n, :], bank[2 + step % 2][:, j * P:(j + 1) * P],
                                                           weight[:, n, x:x + 1], y[:, n, :], ALU.mult, ALU.add)
                    m.then_inc(expert_read, 1)
                dve.wait_ge(expert_read, (g + 1) * E1)
                if g >= 2:
                    dve.wait_ge(final_ready, g - 1)
                norm_statistics(nc, dve, norm4, g, y[:, gs, :])
                if g >= 1:
                    norm_apply(nc, dve, norm4, g - 1, y[:, rows(g - 1), :], final[:, rows(g - 1), :], final_ready)
            norm_apply(nc, dve, norm4, GROUPS - 1, y[:, rows(GROUPS - 1), :], final[:, rows(GROUPS - 1), :], final_ready)


def build(nc, a, out):
    q_parts = nc.dram_tensor("q_parts", (PARTS, P, B * T), BF16, kind="Internal").ap()
    k_parts = nc.dram_tensor("k_parts", (PARTS, P, B * T), BF16, kind="Internal").ap()
    with ExitStack() as ctx:
        psum = ctx.enter_context(nc.psum_tensor("psum", [P, 8 * HALF], F32))
        z_t = ctx.enter_context(nc.sbuf_tensor("z_t", [P, STEPS * T], F32))
        softmax_attention(nc, psum, a["x_t"], a["w_pairs"], a["consts"][:, 0:2 * P], z_t)
        x2 = ctx.enter_context(nc.sbuf_tensor("x2", [P, B * NB, P], F32))
        out_t = ctx.enter_context(nc.sbuf_tensor("out_t", [P, QUADS * T], F32))
        mix_and_sigmoid_attention(nc, psum, a["x_rows"], a["w_o"], a["w_rkv"], a["columns"], a["sign_v"],
                                  a["consts"][:, 0:2 * P], z_t, x2, q_parts, k_parts, out_t)
        experts(nc, psum, a["consts"], a["w_router"], a["b_router"], a["w1"], a["b1"], a["w2"], a["b2"], x2, out_t, out)


def kernel(**inputs):
    import numpy as np
    import concourse.bacc as bacc
    from concourse.bass_utils import run_bass_kernel_spmd

    x = {name: np.asarray(value) for name, value in inputs.items()}

    def rows(y):
        return y.reshape(-1, P, y.shape[-1]).transpose(1, 0, 2)

    heads = np.stack([x["L0_attn_W_K"], x["L0_attn_W_Q"], x["L0_attn_W_V"]])
    e1 = x["L1_ffn_W1"].shape[0]
    arrays = {
        "x_t": x["L0_attn_x"].transpose(0, 2, 1).reshape(B * P, T),
        "x_rows": rows(x["L0_attn_x"]),
        "w_pairs": heads.reshape(3, PAIRS, P, P).transpose(1, 3, 0, 2).reshape(PAIRS * P, 3 * P),
        "w_o": x["L0_attn_W_O"].reshape(P, PAIRS, P).transpose(2, 1, 0),
        "w_rkv": np.stack([x["L0_ffn_W_r"].T, x["L0_ffn_W_k"].T, x["L0_ffn_W_v"].T], axis=1),
        "columns": np.stack([x["L0_ffn_mu_r"], x["L0_ffn_mu_k"], x["L1_attn_bv_q"].reshape(-1),
                             x["L1_attn_bv_k"].reshape(-1)], axis=1),
        "sign_v": x["L1_attn_bv_v"].reshape(-1),
        "w_router": x["L1_ffn_Wr"],
        "b_router": x["L1_ffn_br"],
        "w1": x["L1_ffn_W1"].transpose(1, 0, 2),
        "b1": x["L1_ffn_b1"].T,
        "w2": x["L1_ffn_W2"].transpose(1, 0, 2),
        "b2": x["L1_ffn_b2"],
        "consts": np.concatenate([np.eye(P), np.tril(np.ones((P, P))), np.triu(np.ones((P, P))),
                                  np.tile(np.arange(e1, 0, -1), (P, 1))], axis=1).astype(np.float32),
    }
    arrays = {name: np.ascontiguousarray(value) for name, value in arrays.items()}
    nc = bacc.Bacc("TRN2", target_bir_lowering=False, num_devices=1)
    a = {name: nc.dram_tensor(f"in_{name}", value.shape, mybir.dt.from_np(value.dtype), kind="ExternalInput").ap()
         for name, value in arrays.items()}
    out = nc.dram_tensor("out", (P, B * NB, P), F32, kind="ExternalOutput").ap()
    build(nc, a, out)
    result = run_bass_kernel_spmd(nc, [{f"in_{name}": value for name, value in arrays.items()}], core_ids=[0])
    return result.results[0]["out"].transpose(1, 0, 2).reshape(B, T, P)
```

```python
from contextlib import ExitStack

import concourse.bass as bass
from concourse import mybir

ALU = mybir.AluOpType
ACT = mybir.ActivationFunctionType
AX = mybir.AxisListType
F32 = mybir.dt.float32
F32R = mybir.dt.float32r
BF16 = mybir.dt.bfloat16

P = 128
B = 2
T = 1024
NB = T // P
HALF = 512

PAIRS = 8
DH0 = 64
STEPS = B * PAIRS
TILES = [[(0, 7)], [(1, 7)], [(0, 6)], "k", "q", [(1, 6)], [(0, 5)], [(1, 5)], [(1, 4)], "v", [(1, 3), (1, 2)], [(0, 4)], [(0, 3), (0, 2)], [(0, 1), (0, 0)], [(1, 1), (1, 0)]]
SLOTS = 3
SCALE_AT = {2: [(1, 1), (1, 0), (0, 7)], 6: [(0, 6)], 8: [(0, 5)], 12: [(0, 4)], 13: [(0, 3), (0, 2)]}
WEIGH_AT = {1: [(1, 3)], 2: [(1, 2)], 4: [(1, 1), (1, 0)], 6: [(0, 7)], 8: [(0, 6)], 12: [(0, 5)], 13: [(0, 4)]}
COPY_AT = 4


def left_over(table):
    return [i for k in sorted(table) for back, i in table[k] if back]


UNITS = [unit for tile in TILES if tile not in ("k", "q", "v") for unit in tile]
UNIT_AT = {unit: n for n, unit in enumerate(UNITS)}
PIECES = {7: [(0, 0, 512), (512, 512, 512)], 6: [(0, 0, 512), (512, 512, 384)],
          5: [(128, 0, 384), (512, 384, 384)], 4: [(256, 0, 256), (512, 256, 384)],
          3: [(0, 0, 512)], 2: [(512, 0, 384)], 1: [(0, 0, 256)], 0: [(512, 0, 256)]}
RING = 4


def softmax_attention(nc, psum, x_t, w_kq, w_v, consts, z_t, k_hi, w_o, w_o_loaded):
    with ExitStack() as ctx:
        def sb(name, shape, dt=F32):
            return ctx.enter_context(nc.sbuf_tensor("a0_" + name, shape, dt))

        def sem(name):
            return ctx.enter_context(nc.semaphore("a0_" + name))

        tiles = [psum[:, 2 * n * HALF:2 * (n + 1) * HALF] for n in range(SLOTS)]
        z_acc = psum[:, 2 * SLOTS * HALF:]

        x_hi, x_lo = sb("x_hi", [P, B * T], F32R), sb("x_lo", [P, B * T], F32R)
        w_raw = sb("w", [P, 2 * P])
        w_hi, w_lo = sb("w_hi", [P, 2 * P], F32R), sb("w_lo", [P, 2 * P], F32R)
        wv_raw = sb("wv", [P, 2 * P])
        wv_hi, wv_lo = sb("wv_hi", [P, 2 * P], F32R), sb("wv_lo", [P, 2 * P], F32R)
        xv_hi, xv_lo = sb("xv_hi", [P, HALF], F32R), sb("xv_lo", [P, HALF], F32R)
        k_lo, q_hi, q_lo = (sb(n, [P, T], F32R) for n in ("k_lo", "q_hi", "q_lo"))
        k_stack, qh_stack, ql_stack = ([[sb(f"{s}{n}{h}", [P, T], F32R) for h in range(2)] for n in range(2)]
                                       for s in ("ks", "qh", "ql"))
        V_SET = NB * 2 * P
        v_all = sb("v", [P, 2 * V_SET])
        v_scaled = [sb(f"vs{n}", [P, 2, DH0]) for n in range(RING)]
        e = [[sb(f"e{h}{n}", [P, T]) for n in range(RING)] for h in range(2)]
        row_min = sb("min", [P, 2, NB])
        row_sum = sb("sum", [P, 2, NB])
        row_rec = sb("rec", [P, NB, 2])
        consts_f = e[0][2][:, 0:2 * P]
        ident = sb("ident", [P, P], BF16)
        above = sb("above", [P, P], BF16)

        consts_loaded = sem("consts_loaded")
        consts_ready = sem("consts_ready")
        w_loaded = sem("w_loaded")
        wv_loaded = sem("wv_loaded")
        xv_loaded = sem("xv_loaded")
        x_loaded = [sem(f"x_loaded{b}") for b in range(B)]
        x_high_ready = sem("x_high_ready")
        x_low_ready = sem("x_low_ready")
        w_high_ready = sem("w_high_ready")
        w_low_ready = sem("w_low_ready")
        wv_high_ready = sem("wv_high_ready")
        wv_low_ready = sem("wv_low_ready")
        kq_psum = sem("kq_psum")
        v_psum = sem("v_psum")
        high_ready = sem("high_ready")
        low_ready = sem("low_ready")
        v_ready = sem("v_ready")
        stacked = [sem(f"stacked{h}") for h in range(2)]
        scores_ready = sem("scores_ready")
        min_ready = sem("min_ready")
        exp_ready = sem("exp_ready")
        rec_ready = sem("rec_ready")
        v_scaled_ready = sem("v_scaled_ready")
        z_steps = sem("z_steps")
        z_copied = sem("z_copied")

        def ring_free(eng, s, i):
            if not (isinstance(s, int) and 8 * s + 7 - i < RING):
                eng.wait_ge(z_steps, s * 8 + (8 - i - RING))

        def has(s, what):
            return not isinstance(s, int) or s <= (STEPS - 3 if what == "v" else STEPS - 2)

        block = ctx.enter_context(nc.Block())

        @block.sync
        def _(sp):
            x_raw = e[0][0][:, :], e[0][1][:, :]

            def load_w(n):
                if not (isinstance(n, int) and n == 0):
                    sp.wait_ge(w_low_ready, n)
                sp.dma_start(w_raw[:, :], w_kq[bass.ds(n % PAIRS * P, P), :]).then_inc(w_loaded, 16)

            def load_wv(n):
                if not (isinstance(n, int) and n == 0):
                    sp.wait_ge(wv_low_ready, n)
                sp.dma_start(wv_raw[:, :], w_v[bass.ds(n // 2 % (PAIRS // 2) * P, P), :]).then_inc(wv_loaded, 16)

            def load_xv(v):
                sp.wait_ge(v_psum, v)
                at = bass.ds(v // PAIRS * T + v % 2 * HALF, HALF)
                sp.dma_start(xv_hi[:, :].bitcast(F32), x_hi[:, at].bitcast(F32)).then_inc(xv_loaded, 16)
                sp.dma_start(xv_lo[:, :].bitcast(F32), x_lo[:, at].bitcast(F32)).then_inc(xv_loaded, 16)

            def stack(n, par):
                heads = [(h, slice(h * DH0, (h + 1) * DH0)) for h in range(2)]
                sp.wait_ge(low_ready, n * 2 + 1)
                for h, rows in heads:
                    for half, part in ((slice(0, DH0), k_hi), (slice(DH0, P), k_lo)):
                        sp.dma_start(k_stack[par][h][half, :].bitcast(F32), part[rows, :].bitcast(F32)).then_inc(stacked[h], 16)
                sp.wait_ge(low_ready, n * 2 + 2)
                for h, rows in heads:
                    for half in (slice(0, DH0), slice(DH0, P)):
                        sp.dma_start(qh_stack[par][h][half, :].bitcast(F32), q_hi[rows, :].bitcast(F32)).then_inc(stacked[h], 16)
                        sp.dma_start(ql_stack[par][h][half, :].bitcast(F32), q_lo[rows, :].bitcast(F32)).then_inc(stacked[h], 16)

            def body(s, par):
                stack(s + 1, 1 - par)
                load_w(s + 2)
                if par == 1:
                    load_wv(s + 3)
                load_xv(s + 3)

            load_w(0)
            sp.dma_start(x_raw[0], x_t[0:P, :]).then_inc(x_loaded[0], 16)
            load_wv(0)
            sp.dma_start(consts_f, consts).then_inc(consts_loaded, 16)
            sp.dma_start(x_raw[1], x_t[P:2 * P, :]).then_inc(x_loaded[1], 16)
            load_w(1)
            stack(0, 0)
            load_wv(2)
            load_xv(2)
            body(0, 0)
            with sp.Fori(0, STEPS // 2 - 2) as u:
                body(u * 2 + 1, 1)
                body(u * 2 + 2, 0)
            stack(STEPS - 2, 0)
            load_w(STEPS - 1)
            stack(STEPS - 1, 1)
            for h in range(2):
                sp.wait_ge(stacked[h], STEPS * 96)
            sp.dma_start(k_hi[:, :].bitcast(F32), w_o.rearrange("p n d -> p (n d)")).then_inc(w_o_loaded, 16)

        @block.tensor
        def _(pe):
            def project(n, what, tile):
                if what == "k":
                    pe.wait_ge(w_low_ready, n + 1)
                c = "kq".index(what)
                cs = slice(c * P, (c + 1) * P)
                for c0 in (0, HALF):
                    at = bass.ds(n // PAIRS * T + c0, HALF)
                    pe.matmul(tile[:, c0:c0 + HALF], w_hi[:, cs], x_hi[:, at], start=True, stop=False)
                    pe.matmul(tile[:, c0:c0 + HALF], w_hi[:, cs], x_lo[:, at], start=False, stop=False)
                    m = pe.matmul(tile[:, c0:c0 + HALF], w_lo[:, cs], x_hi[:, at], start=False, stop=True)
                m.then_inc(kq_psum, 1)

            def project_values(v, half, x_parts, tile):
                pe.wait_ge(wv_low_ready, v + (2 - half))
                if x_parts is XV:
                    pe.wait_ge(xv_loaded, v * 32 - 32)
                for i in range(NB // 2):
                    hi, lo = (x[:, i * P:(i + 1) * P] for x in x_parts)
                    out = tile[:, i * 2 * P:(i + 1) * 2 * P]
                    pe.matmul(out, hi, wv_hi[:, :], start=True, stop=False)
                    pe.matmul(out, hi, wv_lo[:, :], start=False, stop=False)
                    m = pe.matmul(out, lo, wv_hi[:, :], start=False, stop=True)
                m.then_inc(v_psum, 1)

            XV = (xv_hi, xv_lo)

            def scores(par, unit, tile):
                h, i = unit
                keys = k_stack[par][h][:, i * P:(i + 1) * P]
                pieces = PIECES[i]
                for col, q0, n in pieces:
                    out = tile[:, col:col + n]
                    diagonal = (col, q0, n) == pieces[-1]
                    pe.matmul(out, keys, qh_stack[par][h][:, q0:q0 + n], start=True, stop=False)
                    if diagonal:
                        diag = col + i * P - q0
                        pe.matmul(tile[:, diag:diag + P], ident[:, :], above[:, :], start=False, stop=False,
                                  skip_group_check=True)
                    m = pe.matmul(out, keys, ql_stack[par][h][:, q0:q0 + n], start=False, stop=True)
                m.then_inc(scores_ready, 1)

            def weigh(s, i):
                pe.wait_ge(v_scaled_ready, s * 8 + (8 - i))
                if i == NB - 1 and not (isinstance(s, int) and s == 0):
                    pe.wait_ge(z_copied, s)
                w = (i + 1) * P
                for c0, c1 in ((0, min(w, HALF)), (HALF, w)):
                    if c1 <= c0:
                        continue
                    for h in range(2):
                        m = pe.matmul(z_acc[h * DH0:(h + 1) * DH0, c0:c1], v_scaled[i % RING][:, h, :],
                                      e[h][i % RING][:, c0:c1], start=(i == NB - 1),
                                      stop=True, skip_group_check=True)
                m.then_inc(z_steps, 1)

            def tile_free(s, k):
                k -= SLOTS
                while True:
                    if k < 0:
                        s, k = s - 1, k + len(TILES)
                    if isinstance(s, int) and s < 0:
                        return
                    if TILES[k] not in ("k", "q", "v") or has(s, TILES[k]):
                        break
                    k -= SLOTS
                if TILES[k] == "v":
                    pe.wait_ge(v_ready, s + 3)
                elif TILES[k] in ("k", "q"):
                    pe.wait_ge(low_ready, (s + 1) * 2 + 1 + "kq".index(TILES[k]))
                else:
                    pe.wait_ge(exp_ready, s * 16 + UNIT_AT[TILES[k][-1]] + 1)

            def body(s, par):
                for k, what in enumerate(TILES):
                    tile = tiles[k % SLOTS]
                    if what not in ("k", "q", "v"):
                        tile_free(s, k)
                        if k < 2:
                            pe.wait_ge(stacked[k], s * 96 + 96)
                        for unit in what:
                            scores(par, unit, tile)
                    elif has(s, what):
                        tile_free(s, k)
                        if what == "v":
                            project_values(s + 2, par, XV, tile)
                        else:
                            project(s + 1, what, tile)
                    for back, i in WEIGH_AT.get(k, []):
                        if not (back and isinstance(s, int) and s == 0):
                            weigh(s - back, i)

            pe.wait_ge(x_low_ready, 1)
            project(0, "k", tiles[0])
            project(0, "q", tiles[1])
            project_values(0, 0, (x_hi, x_lo), tiles[2])
            pe.wait_ge(low_ready, 1)
            project_values(1, 1, (x_hi[:, HALF:], x_lo[:, HALF:]), tiles[0])
            pe.wait_ge(low_ready, 2)
            pe.wait_ge(v_ready, 2)
            pe.wait_ge(consts_ready, 1)
            body(0, 0)
            with pe.Fori(0, STEPS // 2 - 2) as u:
                body(u * 2 + 1, 1)
                body(u * 2 + 2, 0)
            for s in range(STEPS - 3, STEPS):
                body(s, s % 2)
            for i in left_over(WEIGH_AT):
                weigh(STEPS - 1, i)

        @block.scalar
        def _(act):
            def high(n, what, tile):
                c = "kq".index(what)
                act.wait_ge(kq_psum, n * 2 + (1 + c))
                if what == "k" and not (isinstance(n, int) and n == 0):
                    act.wait_ge(stacked[0], n * 96)
                    act.wait_ge(stacked[1], n * 96)
                if what == "k":
                    nc.scalar.activation(k_hi[:, :], tile[:, :], ACT.Copy).then_inc(high_ready, 1)
                else:
                    nc.scalar.activation(q_hi[:, :], tile[:, :], ACT.Copy, scale=-DH0 ** -0.5).then_inc(high_ready, 1)

            def split_weights(n):
                act.wait_ge(w_loaded, n * 16 + 16)
                if not (isinstance(n, int) and n == 0):
                    act.wait_ge(kq_psum, n * 2)
                nc.scalar.activation(w_hi[:, :], w_raw[:, :], ACT.Copy).then_inc(w_high_ready, 1)

            def split_value_weights(n):
                act.wait_ge(wv_loaded, n * 8 + 16)
                if not (isinstance(n, int) and n == 0):
                    act.wait_ge(v_psum, n)
                nc.scalar.activation(wv_hi[:, :], wv_raw[:, :], ACT.Copy).then_inc(wv_high_ready, 2)

            def values(v, half, tile):
                act.wait_ge(v_psum, v + 1)
                if not (isinstance(v, int) and v - half <= 2):
                    act.wait_ge(v_scaled_ready, (v - half - 2) * 8)
                at = bass.ds(v // 2 % 2 * V_SET + half * (V_SET // 2), V_SET // 2)
                nc.scalar.activation(v_all[:, at], tile[:, :], ACT.Copy).then_inc(v_ready, 1)

            def exponentials(s, unit, tile):
                h, i = unit
                n = UNIT_AT[unit]
                ring_free(act, s, i)
                act.wait_ge(min_ready, s * 16 + (n + 1))
                w, col = (i + 1) * P, PIECES[i][0][0]
                nc.scalar.activation(e[h][i % RING][:, 0:w], tile[:, col:col + w], ACT.Exp, bias=row_min[:, h, i:i + 1],
                                     scale=-1.0, accum_out=row_sum[:, h, i:i + 1]).then_inc(exp_ready, 1)

            def copy_z(s):
                act.wait_ge(z_steps, s * 8 + 8)
                nc.scalar.activation(z_t[:, bass.ds(s * T, T)], z_acc[:, :], ACT.Copy).then_inc(z_copied, 1)

            def body(s, par):
                if has(s, "k"):
                    split_weights(s + 1)
                if has(s, "v") and par == 0:
                    split_value_weights(s + 2)
                for k, what in enumerate(TILES):
                    tile = tiles[k % SLOTS]
                    if what not in ("k", "q", "v"):
                        for unit in what:
                            exponentials(s, unit, tile)
                    elif what == "v" and has(s, what):
                        values(s + 2, par, tile)
                    elif what != "v" and has(s, what):
                        high(s + 1, what, tile)
                    if k == COPY_AT and not (isinstance(s, int) and s == 0):
                        copy_z(s - 1)

            def split_x(b):
                act.wait_ge(x_loaded[b], 16)
                nc.scalar.activation(x_hi[:, b * T:(b + 1) * T], e[0][b][:, :], ACT.Copy).then_inc(x_high_ready, 1)

            split_weights(0)
            split_x(0)
            split_value_weights(0)
            high(0, "k", tiles[0])
            high(0, "q", tiles[1])
            values(0, 0, tiles[2])
            values(1, 1, tiles[0])
            split_x(1)
            act.wait_ge(x_low_ready, 2)
            act.wait_ge(consts_ready, 1)
            body(0, 0)
            with act.Fori(0, STEPS // 2 - 2) as u:
                body(u * 2 + 1, 1)
                body(u * 2 + 2, 0)
            for s in range(STEPS - 3, STEPS):
                body(s, s % 2)
            copy_z(STEPS - 1)

        @block.vector
        def _(dve):
            def low(n, what, tile):
                c = "kq".index(what)
                dve.wait_ge(high_ready, n * 2 + (1 + c))
                if what == "k":
                    nc.vector.tensor_tensor(k_lo[:, :], tile[:, :], k_hi[:, :].bitcast(F32), ALU.subtract).then_inc(low_ready, 1)
                else:
                    nc.vector.scalar_tensor_tensor(q_lo[:, :], tile[:, :], -DH0 ** -0.5, q_hi[:, :].bitcast(F32), ALU.mult,
                                                   ALU.subtract).then_inc(low_ready, 1)

            def split_weights(n):
                dve.wait_ge(w_high_ready, n + 1)
                nc.vector.tensor_tensor(w_lo[:, :], w_raw[:, :], w_hi[:, :].bitcast(F32), ALU.subtract).then_inc(w_low_ready, 1)

            def split_value_weights(n):
                dve.wait_ge(wv_high_ready, n + 2)
                nc.vector.tensor_tensor(wv_lo[:, :], wv_raw[:, :], wv_hi[:, :].bitcast(F32),
                                        ALU.subtract).then_inc(wv_low_ready, 2)

            def minimum(s, unit, tile):
                h, i = unit
                dve.wait_ge(scores_ready, s * 16 + (UNIT_AT[unit] + 1))
                w, col = (i + 1) * P, PIECES[i][0][0]
                nc.vector.tensor_reduce(row_min[:, h, i:i + 1], tile[:, col:col + w], AX.X, ALU.min).then_inc(min_ready, 1)

            def scale_values(s, par, i):
                dve.wait_ge(exp_ready, s * 16 + (max(UNIT_AT[(0, i)], UNIT_AT[(1, i)]) + 1))
                nc.vector.reciprocal(row_rec[:, i, :], row_sum[:, :, i]).then_inc(rec_ready, 1)
                ring_free(dve, s, i)
                dve.wait_ge(rec_ready, s * 8 + (8 - i))
                if i == NB - 1:
                    dve.wait_ge(v_ready, s + (2 - par))
                nc.vector.tensor_tensor(v_scaled[i % RING][:, :, :],
                                        v_all[:, bass.ds(s // 2 % 2 * V_SET + (i * 2 + par) * P, P)]
                                        .rearrange("p (h d) -> p h d", h=2),
                                        row_rec[:, i, :].unsqueeze(2).broadcast_to([P, 2, DH0]), ALU.mult).then_inc(v_scaled_ready, 1)

            def body(s, par):
                for k, what in enumerate(TILES):
                    tile = tiles[k % SLOTS]
                    if what in ("k", "q"):
                        if has(s, what):
                            low(s + 1, what, tile)
                    elif what != "v":
                        for unit in what:
                            minimum(s, unit, tile)
                    if k == 0 and has(s, "k"):
                        split_weights(s + 1)
                    if k == 0 and has(s, "v") and par == 0:
                        split_value_weights(s + 2)
                    for back, i in SCALE_AT.get(k, []):
                        if not (back and isinstance(s, int) and s == 0):
                            scale_values(s - back, (par + back) % 2, i)

            def split_x(b):
                dve.wait_ge(x_high_ready, b + 1)
                nc.vector.tensor_tensor(x_lo[:, b * T:(b + 1) * T], e[0][b][:, :], x_hi[:, b * T:(b + 1) * T].bitcast(F32),
                                        ALU.subtract).then_inc(x_low_ready, 1)

            split_weights(0)
            split_x(0)
            split_value_weights(0)
            dve.wait_ge(consts_loaded, 16)
            nc.vector.tensor_copy(ident[:, :], consts_f[:, P:2 * P])
            nc.vector.tensor_scalar(above[:, :], consts_f[:, 0:P], -1e30, 1e30, ALU.mult, ALU.add).then_inc(consts_ready, 1)
            low(0, "k", tiles[0])
            low(0, "q", tiles[1])
            split_x(1)
            body(0, 0)
            with dve.Fori(0, STEPS // 2 - 2) as u:
                body(u * 2 + 1, 1)
                body(u * 2 + 2, 0)
            for s in range(STEPS - 3, STEPS):
                body(s, s % 2)
            for i in left_over(SCALE_AT):
                scale_values(STEPS - 1, 1, i)


GB = HALF // P
GROUPS = B * NB // GB
EPS = 1e-5


def norm_buffers(sb, sem, name):
    return {"stats": [sb(f"{name}_stats{n}", [P, GB, 6]) for n in range(2)],
            "moments": [sb(f"{name}_moments{n}", [P, GB, 2]) for n in range(2)],
            "std": [sb(f"{name}_std{n}", [P, GB]) for n in range(2)],
            "stats_ready": sem(f"{name}_stats_ready"), "variance_ready": sem(f"{name}_variance_ready"),
            "std_ready": sem(f"{name}_std_ready"), "inverse_ready": sem(f"{name}_inverse_ready")}


def norm_statistics(nc, dve, norm, g, y):
    stats, moments = norm["stats"][g % 2], norm["moments"][g % 2]
    for j in range(GB):
        nc.vector.bn_stats(stats[:, j, :], y[:, j, :]).then_inc(norm["stats_ready"], 1)
    dve.wait_ge(norm["stats_ready"], (g + 1) * GB)
    for j in range(GB):
        nc.vector.bn_aggr(moments[:, j, :], stats[:, j, :]).then_inc(norm["variance_ready"], 1)


def norm_root(nc, act, norm, g, eps):
    act.wait_ge(norm["variance_ready"], (g + 1) * GB)
    nc.scalar.activation(norm["std"][g % 2][:, :], norm["moments"][g % 2][:, :, 1], ACT.Sqrt,
                         bias=eps).then_inc(norm["std_ready"], 1)


def norm_apply(nc, dve, norm, g, y, out, ready):
    std, moments = norm["std"][g % 2], norm["moments"][g % 2]
    dve.wait_ge(norm["std_ready"], g + 1)
    nc.vector.reciprocal(std[:, :], std[:, :]).then_inc(norm["inverse_ready"], 1)
    dve.wait_ge(norm["inverse_ready"], g + 1)
    for j in range(GB):
        last = nc.vector.tensor_scalar(out[:, j, :], y[:, j, :], moments[:, j, 0:1], std[:, j:j + 1],
                                       ALU.subtract, ALU.mult)
    last.then_inc(ready, 1)


H1 = 16
DH1 = 8
QUAD = 4
QUADS = B * H1 // QUAD
PARTS = 3
STACK = 96
BLOCK_STEPS = [[0], [1], [2], [3], [4, 5], [6, 7]]
KEY_PIECES = {0: [(0, 0, 512), (512, 512, 512)], 1: [(128, 128, 384), (512, 512, 512)],
              2: [(256, 256, 256), (512, 512, 512)], 3: [(384, 384, 128), (512, 512, 512)],
              4: [(512, 512, 512)], 5: [(128, 640, 384)], 6: [(0, 768, 256)], 7: [(256, 896, 128)]}
SPAN = [(0, 1024), (128, 1024), (256, 1024), (384, 1024), (128, 1024), (0, 384)]
RING1 = 3
NS = len(BLOCK_STEPS)
NT = NS * QUAD
WEIGH_BEHIND = (5, 6)
TURN_AT = (22, 5)
MOVES = QUAD * QUAD
PREPARE_AT = 12
STATISTICS_AT = (10, 13)
SPLIT_AT = (5, 8)


def pieces_at(at):
    return [(back, k, p) for back in (1, 0) for k in range(NS) for p in range(2)
            if (k + 1) * QUAD - 1 + WEIGH_BEHIND[p] - back * NT == at]


def mix_and_sigmoid_attention(nc, psum, x_rows, wo, w_o_loaded, w_rkv, columns, sign_v, z_t, q_parts, k_parts, y3, acc_read, x3_ready, norm3, experts, last_part):
    with ExitStack() as ctx:
        def sb(name, shape, dt=F32):
            return ctx.enter_context(nc.sbuf_tensor("m_" + name, shape, dt))

        def sem(name):
            return ctx.enter_context(nc.semaphore("m_" + name))

        bank_a = [psum[:, g * HALF:(g + 1) * HALF] for g in range(GROUPS)]
        bank_b = [psum[:, (GROUPS + g) * HALF:(GROUPS + g + 1) * HALF] for g in range(GROUPS)]
        tiles = [psum[:, 2 * n * HALF:2 * (n + 1) * HALF] for n in range(SLOTS)]
        acc = psum[:, 2 * SLOTS * HALF:]

        def blocks(x):
            return x.rearrange("p (j d) -> p j d", j=GB)

        x2 = sb("x2", [P, B * NB, P])
        work = sb("work", [P, 8 * T])
        FREE = iter(range(0, QUADS * T, HALF))
        def in_work(width=HALF):
            starts = [next(FREE) for _ in range(width // HALF)]
            return work[:, starts[0]:starts[0] + width]

        x1 = in_work(B * T).rearrange("p (n d) -> p n d", d=P)
        mixed = [[in_work() for _ in range(2)] for _ in ("r", "k")]
        gate = [in_work() for _ in range(2)]
        y1 = [blocks(in_work()) for _ in range(2)]
        y2 = [blocks(in_work()) for _ in range(2)]
        k_act = in_work()
        rest = in_work()
        squares = work[:, 0:T]
        out_rows = work[:, T:T + NB * QUAD * DH1].rearrange("p (n j d) -> p n j d", n=NB, j=QUAD)
        a = [[z_t[:, (j * RING1 + n) * T:(j * RING1 + n + 1) * T] for n in range(RING1)] for j in range(QUAD)]

        w3 = sb("w3", [P, 3, P])
        cols = sb("cols", [P, 8])
        sv = sb("sv", [P, P])
        sign_tmp = k_act[:, 0:P]
        x1t = sb("x1t", [P, B, T + 1])
        eps = sb("eps", [P, 1])
        parts = [sb(f"part{n}", [P, B * T], BF16) for n in range(PARTS)]
        signed = [sb(f"signed{n}", [P, B * T], BF16) for n in range(PARTS)]
        q_stack = [sb(f"q{n}", [STACK, QUAD, T], BF16) for n in range(2)]
        k_stack = [sb(f"k{n}", [STACK, QUAD, T], BF16) for n in range(2)]
        values = [sb(f"v{n}", [P, NB, QUAD, 32]) for n in range(2)]

        x_loaded = sem("x_loaded")
        small_loaded = sem("small_loaded")
        setup_done = sem("setup_done")
        out_ready = sem("out_ready")
        x1_ready = sem("x1_ready")
        x1t_psum = sem("x1t_psum")
        x1t_ready = sem("x1t_ready")
        prev_ready = sem("prev_ready")
        mixed_in = sem("mixed_in")
        rk_psum = sem("rk_psum")
        gate_ready = sem("gate_ready")
        relu_ready = sem("relu_ready")
        k_act_ready = sem("k_act_ready")
        v_psum = sem("v_psum")
        y1_ready = sem("y1_ready")
        gated_ready = sem("gated_ready")
        y2_ready = sem("y2_ready")
        x2_ready = sem("x2_ready")
        x2t_psum = sem("x2t_psum")
        high_ready = sem("high_ready")
        rest_ready = sem("rest_ready")
        mid_ready = sem("mid_ready")
        parts_ready = sem("parts_ready")
        signed_ready = sem("signed_ready")
        parts_stored = [sem(f"parts_stored{b}") for b in range(B)]
        signs_half = sem("signs_half")
        signs_ready = sem("signs_ready")
        zeroed = sem("zeroed")
        b2_zeroed = sem("b2_zeroed")
        experts_loaded = sem("experts_loaded")
        w1_high = sem("w1_high")
        values_zeroed = sem("values_zeroed")
        first_queries = sem("first_queries")
        first_keys = sem("first_keys")
        stacked = [sem(f"stacked{n}") for n in range(2)]
        values_ready = sem("values_ready")
        scores_ready = sem("scores_ready")
        attn_ready = sem("attn_ready")
        steps_done = sem("steps_done")
        masked_ready = sem("masked_ready")
        rows_ready = sem("rows_ready")
        y3_ready = sem("y3_ready")
        norm1 = norm_buffers(sb, sem, "norm1")
        norm2 = norm_buffers(sb, sem, "norm2")

        ident, from_key_on = experts["consts"][:, P:2 * P], experts["consts"][:, 2 * P:3 * P]
        EXPERT_LOADS = len(experts["loads"])
        MU_R, MU_K, SQ, SK, OMR, OMK, SS = range(7)
        LOADS = 2 * PARTS * PARTS * 16

        block = ctx.enter_context(nc.Block())

        def first(s):
            return isinstance(s, int) and s == 0

        def rows(g):
            return slice(g * GB, (g + 1) * GB)

        def tokens(g):
            return slice(g * HALF, (g + 1) * HALF)

        def stack_loads(s):
            h0, b = s % (QUADS // B) * (QUAD * DH1), s // (QUADS // B)
            for n in range(PARTS):
                for c in range(PARTS):
                    yield (slice((n * PARTS + c) * DH1, (n * PARTS + c + 1) * DH1),
                           q_parts[n, bass.ds(h0, QUAD * DH1), bass.ds(b * T, T)].rearrange("(j d) t -> d j t", j=QUAD),
                           k_parts[c, bass.ds(h0, QUAD * DH1), bass.ds(b * T, T)].rearrange("(j d) t -> d j t", j=QUAD))

        @block.sync
        def _(sp):
            sp.dma_start(x1[:, :, :], x_rows).then_inc(x_loaded, 16)
            sp.dma_start(cols[:, 0:4], columns).then_inc(small_loaded, 16)
            sp.dma_start(sv[:, :], sign_v.partition_broadcast(P)).then_inc(small_loaded, 16)
            sp.dma_start(experts["consts"][:, :], experts["consts_dram"]).then_inc(small_loaded, 16)
            sp.dma_start(w3[:, :, :], w_rkv).then_inc(small_loaded, 16)

            def store(g):
                stored = parts_stored[g // (GROUPS // B)]
                sp.wait_ge(parts_ready, g + 1)
                for n in range(PARTS):
                    sp.dma_start(q_parts[n, :, tokens(g)], parts[n][:, tokens(g)]).then_inc(stored, 16)
                sp.wait_ge(signed_ready, (g + 1) * PARTS)
                for n in range(PARTS):
                    sp.dma_start(k_parts[n, :, tokens(g)], signed[n][:, tokens(g)]).then_inc(stored, 16)

            def load(s, par):
                for r, q_src, k_src in stack_loads(s):
                    sp.dma_start(q_stack[par][r, :, :], q_src).then_inc(stacked[par], 16)
                    sp.dma_start(k_stack[par][r, :, :], k_src).then_inc(stacked[par], 16)

            STORES = GROUPS // B * 2 * PARTS * 16
            store(0)
            store(1)
            sp.wait_ge(zeroed, 4)
            sp.wait_ge(parts_stored[0], STORES)
            for r, q_src, _ in stack_loads(0):
                sp.dma_start(q_stack[0][r, :, :], q_src).then_inc(first_queries, 16)
            store(2)
            store(3)
            load(1, 1)
            sp.wait_ge(b2_zeroed, 2)
            sp.wait_ge(out_ready, GROUPS)
            for dst, src in experts["loads"]:
                sp.dma_start(dst, src).then_inc(experts_loaded, 16)
            sp.wait_ge(parts_stored[1], STORES)

            def body(s, par):
                sp.wait_ge(scores_ready, (s - 1) * NT)
                load(s, par)

            with sp.Fori(1, QUADS // 2) as u:
                body(u * 2, 0)
                body(u * 2 + 1, 1)
            last_part["sync"](sp)

        @block.gpsimd
        def _(pool):
            nc.gpsimd.memset(experts["b2"][:, :], 0.0).then_inc(b2_zeroed, 1)
            nc.gpsimd.memset(experts["w_router"][:, :], 0.0).then_inc(b2_zeroed, 1)
            pool.wait_ge(b2_zeroed, 2)
            for n in range(2):
                nc.gpsimd.memset(q_stack[n][64:STACK, :, :], 0.0).then_inc(zeroed, 1)
                nc.gpsimd.memset(k_stack[n][64:STACK, :, :], 0.0).then_inc(zeroed, 1)
            pool.wait_ge(zeroed, 4)
            for n in range(2):
                nc.gpsimd.memset(values[n][:, :, :, :], 0.0).then_inc(values_zeroed, 1)

            pool.wait_ge(parts_stored[0], GROUPS // B * 2 * PARTS * 16)
            for r, _, k_src in stack_loads(0):
                pool.dma_start(k_stack[0][r, :, :], k_src).then_inc(first_keys, 16)
            last_part["gpsimd"](pool)

        @block.tensor
        def _(pe):
            def project(g, half):
                for j in range(half * GB // 2, (half + 1) * GB // 2):
                    n = g * GB + j
                    for pair in range(PAIRS):
                        step = n // NB * PAIRS + pair
                        m = pe.matmul(bank_a[g][:, j * P:(j + 1) * P],
                                      z_t[:, step * T + n % NB * P:step * T + (n % NB + 1) * P], wo[:, pair, :],
                                      start=(pair == 0), stop=(pair == PAIRS - 1))
                if half == 1:
                    m.then_inc(out_ready, 1)

            def transpose1(g):
                pe.wait_ge(x1_ready, g + 1)
                for j in range(GB):
                    m = pe.transpose(bank_b[g][:, j * P:(j + 1) * P], x1[:, g * GB + j, :], ident)
                m.then_inc(x1t_psum, 1)

            def receptance_and_key(g):
                pe.wait_ge(mixed_in, 2 * g + 2)
                pe.matmul(bank_a[g], w3[:, 1, :], mixed[1][g % 2], start=True, stop=True).then_inc(rk_psum, 1)
                for j in range(GB):
                    m = pe.matmul(bank_b[g][:, j * P:(j + 1) * P], mixed[0][g % 2][:, j * P:(j + 1) * P], w3[:, 0, :],
                                  start=True, stop=True)
                m.then_inc(rk_psum, 1)

            def value(g):
                pe.wait_ge(k_act_ready, g + 1)
                for j in range(GB):
                    m = pe.matmul(bank_a[g][:, j * P:(j + 1) * P], k_act[:, j * P:(j + 1) * P], w3[:, 2, :],
                                  start=True, stop=True)
                m.then_inc(v_psum, 1)

            def transpose2(g):
                pe.wait_ge(x2_ready, g + 1)
                pe.wait_ge(gate_ready, g + 1)
                for j in range(GB):
                    m = pe.transpose(bank_b[g][:, j * P:(j + 1) * P], x2[:, g * GB + j, :], ident)
                m.then_inc(x2t_psum, 1)

            pe.wait_ge(w_o_loaded, 16)
            project(0, 0)
            project(0, 1)
            project(1, 0)
            project(1, 1)
            transpose1(0)
            project(2, 0)
            receptance_and_key(0)
            value(0)
            pe.wait_ge(small_loaded, 16 * 4)
            transpose1(1)
            project(2, 1)
            receptance_and_key(1)
            project(3, 0)
            transpose2(0)
            value(1)
            transpose1(2)
            project(3, 1)
            receptance_and_key(2)
            transpose2(1)
            transpose1(3)
            value(2)
            receptance_and_key(3)
            value(3)
            transpose2(2)
            transpose2(3)

            def scores(s, par, at):
                k, j = at // QUAD, at % QUAD
                tile = tiles[at % SLOTS]
                if not (first(s) and at < SLOTS):
                    pe.wait_ge(attn_ready, s * NT + (at - SLOTS + 1))
                for i in BLOCK_STEPS[k]:
                    keys = k_stack[par][:, j, i * P:(i + 1) * P]
                    for col, q0, width in KEY_PIECES[i]:
                        m = pe.matmul(tile[:, col:col + width], keys, q_stack[par][:, j, q0:q0 + width], start=True, stop=True)
                m.then_inc(scores_ready, 1)

            def weigh(s, par, k, piece):
                if k == 0 and piece == 0:
                    pe.wait_ge(values_ready, s + 1)
                if k == 0 and first(s):
                    pe.wait_ge(parts_ready, GROUPS)
                elif k == 0:
                    pe.wait_ge(acc_read[piece], s)
                if piece == 0:
                    pe.wait_ge(masked_ready, s * NT + (k + 1) * QUAD)
                i, (col, q0, width) = [(i, cut) for i in BLOCK_STEPS[k] for cut in KEY_PIECES[i]][piece]
                for j in range(QUAD):
                    m = pe.matmul(acc[32 * j:32 * j + 32, q0:q0 + width], values[par][:, i, j, :],
                                  a[j][k % RING1][:, col:col + width], start=(i == 0), stop=True,
                                  skip_group_check=True)
                if piece == 1:
                    m.then_inc(steps_done, 1)

            def body(s, par):
                if first(s):
                    pe.wait_ge(first_queries, LOADS // 2)
                    pe.wait_ge(first_keys, LOADS // 2)
                else:
                    pe.wait_ge(stacked[par], s * (LOADS // 2) + (LOADS // 2 if par else 0))
                for at in range(NT):
                    scores(s, par, at)
                    for back, k, piece in pieces_at(at):
                        if not (back and first(s)):
                            weigh(s - back, (par + back) % 2, k, piece)

            pe.wait_ge(zeroed, 4)
            body(0, 0)
            with pe.Fori(0, QUADS // 2 - 1) as u:
                body(u * 2 + 1, 1)
                body(u * 2 + 2, 0)
            body(QUADS - 1, 1)
            for at in range(NT):
                for back, k, piece in pieces_at(at):
                    if back:
                        weigh(QUADS - 1, 1, k, piece)
            last_part["tensor"](pe)

        @block.scalar
        def _(act):
            def transposed1(g):
                act.wait_ge(x1t_psum, g + 1)
                b, t0 = g // 2, g % 2 * HALF
                nc.scalar.activation(x1t[:, b, 1 + t0:1 + t0 + HALF], bank_b[g], ACT.Copy).then_inc(x1t_ready, 1)
                act.wait_ge(x1t_ready, g + 1)
                if g >= 2:
                    act.wait_ge(rk_psum, 2 * g - 2)
                for n, c in ((0, OMR), (1, OMK)):
                    nc.scalar.activation(mixed[n][g % 2], x1t[:, b, t0:t0 + HALF], ACT.Identity,
                                         scale=cols[:, c:c + 1]).then_inc(prev_ready, 1)

            def relu_and_gates(g):
                act.wait_ge(rk_psum, 2 * g + 1)
                if g >= 1:
                    act.wait_ge(v_psum, g)
                nc.scalar.activation(k_act, bank_a[g], ACT.Relu).then_inc(relu_ready, 1)
                act.wait_ge(rk_psum, 2 * g + 2)
                if g >= 2:
                    act.wait_ge(gated_ready, g - 1)
                nc.scalar.activation(gate[g % 2], bank_b[g], ACT.Sigmoid).then_inc(gate_ready, 1)

            def high_parts(g):
                act.wait_ge(x2t_psum, g + 1)
                nc.scalar.activation(parts[0][:, tokens(g)], bank_b[g], ACT.Copy).then_inc(high_ready, 1)
                act.wait_ge(rest_ready, g + 1)
                nc.scalar.activation(parts[1][:, tokens(g)], rest, ACT.Copy).then_inc(mid_ready, 1)

            act.wait_ge(setup_done, 1)
            norm_root(nc, act, norm1, 0, eps[:, :])
            transposed1(0)
            norm_root(nc, act, norm1, 1, eps[:, :])
            relu_and_gates(0)
            transposed1(1)
            norm_root(nc, act, norm2, 0, eps[:, :])
            norm_root(nc, act, norm1, 2, eps[:, :])
            relu_and_gates(1)
            high_parts(0)
            transposed1(2)
            norm_root(nc, act, norm2, 1, eps[:, :])
            norm_root(nc, act, norm1, 3, eps[:, :])
            relu_and_gates(2)
            high_parts(1)
            transposed1(3)
            norm_root(nc, act, norm2, 2, eps[:, :])
            relu_and_gates(3)
            norm_root(nc, act, norm2, 3, eps[:, :])
            high_parts(2)
            high_parts(3)

            def body(s):
                for k in range(NS):
                    for j in range(QUAD):
                        at = k * QUAD + j
                        act.wait_ge(scores_ready, s * NT + (at + 1))
                        if not (first(s) and k < RING1) and j == 0:
                            act.wait_ge(steps_done, s * NS + (k - RING1 + 1))
                        c0, c1 = SPAN[k]
                        nc.scalar.activation(a[j][k % RING1][:, c0:c1], tiles[at % SLOTS][:, c0:c1], ACT.Sigmoid,
                                             scale=4.0 * DH1 ** -0.5).then_inc(attn_ready, 1)

            body(0)
            with act.Fori(1, QUADS) as s:
                body(s)
            norm_root(nc, act, norm3, 0, eps[:, :])
            norm_root(nc, act, norm3, 1, eps[:, :])
            last_part["scalar"](act)

        @block.vector
        def _(dve):
            def sign(out, x, tmp, n):
                nc.vector.tensor_scalar(tmp, x, 0.0, None, ALU.is_lt)
                nc.vector.tensor_scalar(out, x, 0.0, None, ALU.is_gt).then_inc(signs_half, 1)
                dve.wait_ge(signs_half, n + 1)
                nc.vector.tensor_tensor(out, out, tmp, ALU.subtract).then_inc(signs_ready, 1)
                dve.wait_ge(signs_ready, n + 1)

            def residual1(g):
                if g >= 2:
                    dve.wait_ge(x1_ready, g - 1)
                dve.wait_ge(out_ready, g + 1)
                nc.vector.tensor_tensor(y1[g % 2], blocks(bank_a[g]), x1[:, rows(g), :], ALU.add).then_inc(y1_ready, 1)
                dve.wait_ge(y1_ready, g + 1)
                norm_statistics(nc, dve, norm1, g, y1[g % 2])

            def apply1(g):
                norm_apply(nc, dve, norm1, g, y1[g % 2], x1[:, rows(g), :], x1_ready)

            def mix(g):
                b, t0 = g // 2, g % 2 * HALF
                for n, c in ((0, MU_R), (1, MU_K)):
                    dve.wait_ge(prev_ready, 2 * g + n + 1)
                    nc.vector.scalar_tensor_tensor(mixed[n][g % 2], x1t[:, b, 1 + t0:1 + t0 + HALF], cols[:, c:c + 1],
                                                   mixed[n][g % 2], ALU.mult, ALU.add).then_inc(mixed_in, 1)

            def activate_key(g):
                dve.wait_ge(relu_ready, g + 1)
                nc.vector.tensor_tensor(k_act, bank_a[g], k_act, ALU.mult).then_inc(k_act_ready, 1)

            def residual2(g):
                if g >= 2:
                    dve.wait_ge(x2_ready, g - 1)
                dve.wait_ge(v_psum, g + 1)
                dve.wait_ge(gate_ready, g + 1)
                nc.vector.tensor_tensor(y2[g % 2], blocks(bank_a[g]), blocks(gate[g % 2]), ALU.mult).then_inc(gated_ready, 1)
                dve.wait_ge(gated_ready, g + 1)
                nc.vector.tensor_tensor(y2[g % 2], y2[g % 2], x1[:, rows(g), :], ALU.add).then_inc(y2_ready, 1)
                dve.wait_ge(y2_ready, g + 1)
                norm_statistics(nc, dve, norm2, g, y2[g % 2])

            def apply2(g):
                norm_apply(nc, dve, norm2, g, y2[g % 2], x2[:, rows(g), :], x2_ready)

            def low_parts(g):
                dve.wait_ge(high_ready, g + 1)
                if g >= 1:
                    dve.wait_ge(parts_ready, g)
                nc.vector.tensor_tensor(rest, bank_b[g], parts[0][:, tokens(g)], ALU.subtract).then_inc(rest_ready, 1)
                dve.wait_ge(mid_ready, g + 1)
                nc.vector.tensor_tensor(parts[2][:, tokens(g)], rest, parts[1][:, tokens(g)],
                                        ALU.subtract).then_inc(parts_ready, 1)

            def signed_parts(g):
                dve.wait_ge(parts_ready, g + 1)
                for n in range(PARTS):
                    nc.vector.tensor_scalar(signed[n][:, tokens(g)], parts[n][:, tokens(g)], cols[:, SS:SS + 1], None,
                                            ALU.mult).then_inc(signed_ready, 1)

            nc.vector.memset(eps[:, :], EPS)
            for b in range(B):
                nc.vector.memset(x1t[:, b, 0:1], 0.0)
            dve.wait_ge(small_loaded, 16 * 4)
            nc.vector.tensor_scalar(cols[:, OMR:OMK + 1], cols[:, MU_R:MU_K + 1], -1.0, 1.0, ALU.mult, ALU.add)
            sign(sv[:, :], sv[:, :], sign_tmp, 0)
            sign(cols[:, SQ:SK + 1], cols[:, SQ:SK + 1], sign_tmp[:, 0:2], 1)
            nc.vector.tensor_tensor(cols[:, SS:SS + 1], cols[:, SQ:SQ + 1], cols[:, SK:SK + 1], ALU.mult).then_inc(setup_done, 1)

            dve.wait_ge(x_loaded, 16)
            residual1(0)
            apply1(0)
            mix(0)
            residual1(1)
            activate_key(0)
            apply1(1)
            residual2(0)
            mix(1)
            residual1(2)
            apply2(0)
            activate_key(1)
            apply1(2)
            low_parts(0)
            mix(2)
            signed_parts(0)
            residual2(1)
            residual1(3)
            apply2(1)
            activate_key(2)
            apply1(3)
            low_parts(1)
            signed_parts(1)
            mix(3)
            residual2(2)
            activate_key(3)
            apply2(2)
            residual2(3)
            apply2(3)
            low_parts(2)
            low_parts(3)
            signed_parts(2)
            signed_parts(3)

            def prepare(s, par):
                b, h0 = s // (QUADS // B), s % (QUADS // B) * (QUAD * DH1)
                nc.vector.tensor_tensor(values[par][:, :, :, 0:DH1],
                                        x2[:, bass.ds(b * NB, NB), bass.ds(h0, QUAD * DH1)].rearrange("p n (j d) -> p n j d", j=QUAD),
                                        sv[:, bass.ds(h0, QUAD * DH1)].rearrange("p (j d) -> p j d", j=QUAD)
                                        .unsqueeze(1).broadcast_to([P, NB, QUAD, DH1]), ALU.mult).then_inc(values_ready, 1)

            def mask(s, at):
                k, j = at // QUAD, at % QUAD
                dve.wait_ge(attn_ready, s * NT + (at + 1))
                for i in BLOCK_STEPS[k]:
                    diagonal = a[j][k % RING1][:, KEY_PIECES[i][0][0]:KEY_PIECES[i][0][0] + P]
                    m = nc.vector.tensor_tensor(diagonal, diagonal, from_key_on, ALU.mult)
                m.then_inc(masked_ready, 1)

            def turn(s, half):
                dve.wait_ge(steps_done, s * NS + (NS if half else NB // 2))
                if half == 0 and not first(s):
                    dve.wait_ge(rows_ready, s * MOVES)
                cut = slice(half * HALF, (half + 1) * HALF)
                nc.vector.transpose(squares[:, cut], acc[:, cut]).then_inc(acc_read[half], 1)

            def move(s, n):
                j, c = n // QUAD, n % QUAD
                if n == 0:
                    dve.wait_ge(acc_read[0], s + 1)
                    dve.wait_ge(acc_read[1], s + 1)
                    if not first(s):
                        dve.wait_ge(y3_ready, s)
                nc.vector.tensor_copy(out_rows[32 * c:32 * c + 32, :, j, :],
                                      squares[32 * j:32 * j + 32, :].rearrange("p (n c d) -> p n c d", n=NB, c=QUAD)[:, :, c, 0:DH1]
                                      ).then_inc(rows_ready, 1)

            def residual3(s):
                dve.wait_ge(rows_ready, s * MOVES + MOVES)
                b, h0 = s // (QUADS // B), s % (QUADS // B) * (QUAD * DH1)
                x2_part, y3_part = (x[:, bass.ds(b * NB, NB), bass.ds(h0, QUAD * DH1)].rearrange("p n (j d) -> p n j d", j=QUAD)
                                    for x in (x2, y3))
                nc.vector.tensor_tensor(y3_part, out_rows, x2_part, ALU.add).then_inc(y3_ready, 1)

            def statistics3(g):
                dve.wait_ge(y3_ready, (g // (GROUPS // B) + 1) * (QUADS // B))
                norm_statistics(nc, dve, norm3, g, y3[:, rows(g), :])

            def apply3(g):
                norm_apply(nc, dve, norm3, g, y3[:, rows(g), :], y3[:, rows(g), :], x3_ready)

            def body(s, par):
                last = isinstance(s, int) and s == QUADS - 1
                for at in range(NT):
                    mask(s, at)
                    if not first(s):
                        if at == TURN_AT[1]:
                            turn(s - 1, 1)
                        if TURN_AT[1] < at <= TURN_AT[1] + MOVES:
                            move(s - 1, at - TURN_AT[1] - 1)
                        if at == NT - 1:
                            residual3(s - 1)
                    if at == TURN_AT[0]:
                        turn(s, 0)
                    if last and at in STATISTICS_AT:
                        statistics3(STATISTICS_AT.index(at))
                    if last and at == SPLIT_AT[0]:
                        dve.wait_ge(experts_loaded, 16 * EXPERT_LOADS)
                        nc.vector.tensor_copy(experts["w1_hi"][:, :], experts["w1"][:, :]).then_inc(w1_high, 1)
                    if last and at == SPLIT_AT[1]:
                        dve.wait_ge(w1_high, 1)
                        nc.vector.tensor_tensor(experts["w1_lo"][:, :], experts["w1"][:, :],
                                                experts["w1_hi"][:, :].bitcast(F32), ALU.subtract)
                    if at == PREPARE_AT and not last:
                        prepare(s + 1, 1 - par)

            dve.wait_ge(values_zeroed, 2)
            prepare(0, 0)
            body(0, 0)
            with dve.Fori(0, QUADS // 2 - 1) as u:
                body(u * 2 + 1, 1)
                body(u * 2 + 2, 0)
            body(QUADS - 1, 1)
            apply3(0)
            apply3(1)
            turn(QUADS - 1, 1)
            for n in range(MOVES):
                move(QUADS - 1, n)
            residual3(QUADS - 1)
            last_part["vector"](dve)


E1 = 8
CAPACITY = B * T // E1
PAD = 96


def expert_buffers(nc, ctx, z_t, consts, w_router, b_router, w1, b1, w2, b2):
    def sb(name, shape, dt=F32):
        return ctx.enter_context(nc.sbuf_tensor("e_" + name, shape, dt))

    x = {"consts": sb("consts", [P, 3 * P + E1]), "consts_dram": consts,
         "w_router": sb("wr", [P, 32]), "b_router": sb("br", [P, E1]),
         "w1": z_t[:, 14 * T:15 * T], "w2": z_t[:, 15 * T:16 * T].rearrange("p (e d) -> p e d", e=E1), "b1": sb("b1", [P, E1]),
         "b2": sb("b2", [PAD, GB * P]),
         "w1_hi": sb("w1_hi", [P, E1 * P], F32R), "w1_lo": sb("w1_lo", [P, E1 * P], F32R)}
    x["loads"] = [(x["w_router"][:, 0:E1], w_router), (x["b_router"][:, :], b_router.partition_broadcast(P)),
                  (x["w1"][:, :], w1.rearrange("p e u -> p (e u)")), (x["w2"][:, :, :], w2), (x["b1"][:, :], b1)]
    x["loads"] += [(x["b2"][j * E1:(j + 1) * E1, j * P:(j + 1) * P], b2) for j in range(GB)]
    return x


def mixture_of_experts(nc, ctx, psum, experts, z_t, y3, acc_read, x3_ready, norm3, out):
    N = B * NB
    def sb(name, shape, dt=F32):
        return ctx.enter_context(nc.sbuf_tensor("e_" + name, shape, dt))

    def sem(name):
        return ctx.enter_context(nc.semaphore("e_" + name))

    bank = [psum[:, n * HALF:(n + 1) * HALF] for n in range(8)]
    hidden_bank = bank[0], bank[7]
    output_bank = bank[2:4]
    turned_bank = bank[4:6]
    small_bank = bank[6], bank[1]
    logits_bank = [x[:, 0:P].rearrange("p (j e) -> p j e", j=GB)[:, :, 0:E1] for x in small_bank]
    places_bank = [x[:, 0:GB * E1].rearrange("p (j e) -> p j e", j=GB) for x in small_bank]
    weight_bank = [x[0:PAD, 0:P] for x in small_bank]

    def blocks(x):
        return x.rearrange("p (j d) -> p j d", j=GB)

    def rows(g):
        return slice(g * GB, (g + 1) * GB)

    def two(name, shape, dt=F32):
        return [sb(f"{name}{n}", shape, dt) for n in range(2)]

    consts_f = experts["consts"]
    ident = consts_f[:, P:2 * P]
    wr, br, b1s, b2s, w2s = (experts[name] for name in ("w_router", "b_router", "b1", "b2", "w2"))
    w1_hi, w1_lo = experts["w1_hi"], experts["w1_lo"]
    upto = sb("upto", [P, P], BF16)
    ones = sb("ones", [P, P], BF16)
    eps = sb("eps", [P, 1])
    free = iter(range(0, QUAD * RING1 * T, HALF))

    def in_z_t(width=HALF):
        starts = [next(free) for _ in range(width // HALF)]
        return z_t[:, starts[0]:starts[0] + width]

    gxt_hi, gxt_lo = two("gxt_hi", [P, HALF], F32R), two("gxt_lo", [P, HALF], F32R)
    x3 = y3
    x3t = [in_z_t() for _ in range(2)]
    logits_t = [in_z_t()[:, 0:P] for _ in range(2)]
    gx = [blocks(in_z_t()) for _ in range(2)]
    logits = two("logits", [P, GB, E1])
    ex = two("ex", [P, GB, E1])
    tied = two("tied", [P, GB, E1])
    top = two("top", [P, GB])
    gate = two("gate", [P, GB])
    chosen = [sb(f"chosen{g}", [P, GB, E1], BF16) for g in range(GROUPS)]
    earlier = two("earlier", [P, E1], BF16)
    group_sum = sb("group_sum", [P, E1])
    placed = two("placed", [P, GB, E1])
    weight = [sb(f"weight{n}", [P, PAD]) for n in range(GROUPS)]
    weight_t = two("weightt", [PAD, P])
    y = in_z_t(N * P).rearrange("p (n d) -> p n d", d=P)
    hid = [in_z_t() for _ in range(2)]
    final = in_z_t(N * P).rearrange("p (n d) -> p n d", d=P)

    setup_done = sem("setup_done")
    x3t_psum = sem("x3t_psum")
    x3t_ready = sem("x3t_ready")
    logits_t_psum = sem("logits_t_psum")
    logits_t_ready = sem("logits_t_ready")
    logits_psum = sem("logits_psum")
    routed = [sem(f"routed{g}") for g in range(GROUPS)]
    shifted_ready = sem("shifted_ready")
    exp_ready = sem("exp_ready")
    chosen_ready = sem("chosen_ready")
    group_summed = sem("group_summed")
    earlier_ready = sem("earlier_ready")
    places_psum = sem("places_psum")
    gx_ready = sem("gx_ready")
    gxt_psum = sem("gxt_psum")
    gxt_high = sem("gxt_high")
    gxt_ready = sem("gxt_ready")
    weight_ready = sem("weight_ready")
    weight_psum = sem("weight_psum")
    weight_t_ready = sem("weight_t_ready")
    bias_psum = sem("bias_psum")
    y_ready = sem("y_ready")
    hid_psum = sem("hid_psum")
    hid_ready = sem("hid_ready")
    expert_psum = sem("expert_psum")
    expert_read = sem("expert_read")
    final_ready = sem("final_ready")
    stored = [sem(f"stored{g}") for g in range(GROUPS)]
    norm4 = norm_buffers(sb, sem, "norm4")


    def sync_program(sp):
        for g in range(GROUPS):
            sp.wait_ge(final_ready, g + 1)
            sp.dma_start(out[:, rows(g), :], final[:, rows(g), :]).then_inc(stored[g], 16)
        for g in range(GROUPS):
            sp.wait_ge(stored[g], 16)

    def gpsimd_program(pool):
        nc.gpsimd.memset(eps[:, :], EPS)
        nc.gpsimd.memset(ones[:, :], 1.0)
        for g in range(GROUPS):
            nc.gpsimd.memset(weight[g][:, :], 0.0)
        nc.gpsimd.tensor_copy(upto[:, :], consts_f[:, 2 * P:3 * P]).then_inc(setup_done, 1)

    def tensor_program(pe):
        def turn_x3(g):
            pe.wait_ge(x3_ready, g + 1)
            if g >= 2:
                pe.wait_ge(y_ready, g - 1)
            for j in range(GB):
                m = pe.transpose(turned_bank[g % 2][:, j * P:(j + 1) * P], x3[:, g * GB + j, :], ident)
            m.then_inc(x3t_psum, 1)

        def router(g):
            pe.wait_ge(x3t_ready, g + 1)
            if g >= 2:
                pe.wait_ge(weight_t_ready, g - 1)
            for j in range(GB):
                m = pe.matmul(small_bank[g % 2][32 * j:32 * j + 32, 0:P], wr[:, :], x3t[g % 2][:, j * P:(j + 1) * P],
                              start=True, stop=True)
            m.then_inc(logits_t_psum, 1)

        def turn_logits(g):
            pe.wait_ge(logits_t_ready, g + 1)
            pe.transpose(small_bank[g % 2][:, 0:P], logits_t[g % 2][:, :], ident).then_inc(logits_psum, 1)

        def places(g):
            pe.wait_ge(chosen_ready, g + 1)
            at = places_bank[g % 2]
            m = pe.matmul(at, upto[:, :], chosen[g][:, :, :], start=True, stop=True)
            for back in range(1, GB):
                m = pe.matmul(at[:, back:GB, :], ones[:, :], chosen[g][:, 0:GB - back, :], start=False, stop=True,
                              skip_group_check=True)
            if g >= 1:
                pe.wait_ge(earlier_ready, g)
                m = pe.matmul(at, ones[:, :], earlier[g % 2][:, :].unsqueeze(1).broadcast_to([P, GB, E1]), start=False, stop=True,
                              skip_group_check=True)
            m.then_inc(places_psum, 1)

        def turn_gx(g):
            pe.wait_ge(gx_ready, g + 1)
            for j in range(GB):
                m = pe.transpose(turned_bank[g % 2][:, j * P:(j + 1) * P], gx[g % 2][:, j, :], ident)
            m.then_inc(gxt_psum, 1)

        def turn_weight(g):
            pe.wait_ge(weight_ready, g + 1)
            pe.transpose(weight_bank[g % 2], weight[g][:, :], ident).then_inc(weight_psum, 1)

        def bias(g):
            pe.wait_ge(weight_t_ready, g + 1)
            pe.wait_ge(gxt_ready, g + 1)
            pe.matmul(turned_bank[g % 2], weight_t[g % 2][:, :], b2s[:, :], start=True, stop=True).then_inc(bias_psum, 1)

        def hidden(step):
            g, x = step // E1, step % E1
            if x == 0:
                pe.wait_ge(gxt_high, g + 1)
            if step >= 2:
                pe.wait_ge(hid_ready, step - 1)
            at, w = hidden_bank[step % 2], slice(x * P, (x + 1) * P)
            pe.matmul(at, w1_hi[:, w], gxt_hi[g % 2][:, :], start=True, stop=False)
            pe.matmul(at, w1_lo[:, w], gxt_hi[g % 2][:, :], start=False, stop=False)
            if x == 0:
                pe.wait_ge(gxt_ready, g + 1)
            pe.matmul(at, w1_hi[:, w], gxt_lo[g % 2][:, :], start=False, stop=True).then_inc(hid_psum, 1)

        def output(step):
            pe.wait_ge(hid_ready, step + 1)
            if step >= 2:
                pe.wait_ge(expert_read, step - 1)
            for j in range(GB):
                m = pe.matmul(output_bank[step % 2][:, j * P:(j + 1) * P], hid[step % 2][:, j * P:(j + 1) * P],
                              w2s[:, step % E1, :], start=True, stop=True)
            m.then_inc(expert_psum, 1)

        turn_x3(0)
        turn_x3(1)
        pe.wait_ge(acc_read[0], QUADS)
        router(0)
        router(1)
        turn_logits(0)
        turn_logits(1)
        pe.wait_ge(setup_done, 1)
        places(0)
        turn_gx(0)
        pe.wait_ge(acc_read[1], QUADS)
        hidden(0)
        turn_weight(0)
        bias(0)
        for step in range(GROUPS * E1):
            g, x = step // E1, step % E1
            if step + 1 < GROUPS * E1:
                hidden(step + 1)
            output(step)
            if x == 0 and g + 1 < GROUPS:
                places(g + 1)
                turn_gx(g + 1)
            if x == 5 and g + 1 < GROUPS:
                turn_weight(g + 1)
            if x == 7 and g + 1 < GROUPS:
                bias(g + 1)
            for n, at in ((2, 2), (3, 9)):
                if step == at:
                    turn_x3(n)
                if step == at + 1:
                    router(n)
                if step == at + 2:
                    turn_logits(n)

    def scalar_program(act):
        def turned_x3(g):
            act.wait_ge(x3t_psum, g + 1)
            if g >= 2:
                act.wait_ge(logits_psum, g - 1)
            nc.scalar.activation(x3t[g % 2][:, :], turned_bank[g % 2], ACT.Copy).then_inc(x3t_ready, 1)

        def exponentials(g):
            act.wait_ge(shifted_ready, g + 1)
            nc.scalar.activation(ex[g % 2][:, :, :], ex[g % 2][:, :, :], ACT.Exp).then_inc(exp_ready, 1)

        def high_part(g):
            act.wait_ge(gxt_psum, g + 1)
            if g >= 2:
                act.wait_ge(hid_psum, (g - 1) * E1)
            nc.scalar.activation(gxt_hi[g % 2][:, :], turned_bank[g % 2], ACT.Copy).then_inc(gxt_high, 1)

        def turned_weight(g):
            act.wait_ge(weight_psum, g + 1)
            if g >= 2:
                act.wait_ge(bias_psum, g - 1)
            nc.scalar.activation(weight_t[g % 2][:, :], weight_bank[g % 2], ACT.Copy).then_inc(weight_t_ready, 1)

        def copied_logits(g):
            act.wait_ge(logits_t_psum, g + 1)
            if g >= 2:
                act.wait_ge(logits_psum, g - 1)
            nc.scalar.activation(logits_t[g % 2][:, :], small_bank[g % 2][:, 0:P], ACT.Copy).then_inc(logits_t_ready, 1)

        turned_x3(0)
        turned_x3(1)
        copied_logits(0)
        copied_logits(1)
        exponentials(0)
        high_part(0)
        exponentials(1)
        turned_weight(0)
        act.wait_ge(setup_done, 1)
        norm_root(nc, act, norm3, 2, eps[:, :])
        norm_root(nc, act, norm3, 3, eps[:, :])
        for step in range(GROUPS * E1):
            g, x = step // E1, step % E1
            act.wait_ge(hid_psum, step + 1)
            if step >= 2:
                act.wait_ge(expert_psum, step - 1)
            nc.scalar.activation(hid[step % 2][:, :], hidden_bank[step % 2], ACT.Relu,
                                 bias=b1s[:, x:x + 1]).then_inc(hid_ready, 1)
            if x == 1 and g + 1 < GROUPS:
                high_part(g + 1)
            if x == 5 and g + 1 < GROUPS:
                turned_weight(g + 1)
            for n, at in ((2, 2), (3, 9)):
                if step == at + 1:
                    turned_x3(n)
                if step == at + 2:
                    copied_logits(n)
                if step == at + 4:
                    exponentials(n)
            if x == 6 and g >= 1:
                norm_root(nc, act, norm4, g - 1, eps[:, :])
        norm_root(nc, act, norm4, GROUPS - 1, eps[:, :])

    def vector_program(dve):
        def wide(x):
            return x[:, :].unsqueeze(2).broadcast_to([P, GB, E1])

        def statistics3(g):
            if g >= 2:
                dve.wait_ge(x3_ready, g - 1)
            norm_statistics(nc, dve, norm3, g, y3[:, rows(g), :])

        def apply3(g):
            norm_apply(nc, dve, norm3, g, y3[:, rows(g), :], x3[:, rows(g), :], x3_ready)

        def choose(g):
            p = g % 2
            dve.wait_ge(logits_psum, g + 1)
            nc.vector.tensor_tensor(logits[p][:, :, :], logits_bank[g % 2],
                                    br[:, :].unsqueeze(1).broadcast_to([P, GB, E1]), ALU.add).then_inc(routed[g], 1)
            dve.wait_ge(routed[g], 1)
            nc.vector.tensor_reduce(top[p][:, :], logits[p][:, :, :], AX.X, ALU.max).then_inc(routed[g], 1)
            dve.wait_ge(routed[g], 2)
            nc.vector.tensor_tensor(ex[p][:, :, :], logits[p][:, :, :], wide(top[p]), ALU.subtract).then_inc(shifted_ready, 1)
            nc.vector.tensor_tensor(tied[p][:, :, :], logits[p][:, :, :], wide(top[p]), ALU.is_equal).then_inc(routed[g], 1)
            dve.wait_ge(routed[g], 3)
            nc.vector.tensor_tensor(tied[p][:, :, :], tied[p][:, :, :],
                                    consts_f[:, 3 * P:3 * P + E1].unsqueeze(1).broadcast_to([P, GB, E1]), ALU.mult).then_inc(routed[g], 1)
            dve.wait_ge(routed[g], 4)
            nc.vector.tensor_reduce(top[p][:, :], tied[p][:, :, :], AX.X, ALU.max).then_inc(routed[g], 1)
            dve.wait_ge(routed[g], 5)
            nc.vector.tensor_tensor(chosen[g][:, :, :], tied[p][:, :, :], wide(top[p]), ALU.is_equal).then_inc(chosen_ready, 1)

        def scale(g):
            p = g % 2
            dve.wait_ge(exp_ready, g + 1)
            nc.vector.tensor_reduce(gate[p][:, :], ex[p][:, :, :], AX.X, ALU.add).then_inc(routed[g], 1)
            dve.wait_ge(routed[g], 6)
            nc.vector.reciprocal(gate[p][:, :], gate[p][:, :]).then_inc(routed[g], 1)
            dve.wait_ge(routed[g], 7)
            if g >= 2:
                dve.wait_ge(gxt_psum, g - 1)
            nc.vector.tensor_tensor(gx[p][:, :, :], x3[:, rows(g), :], gate[p][:, :].unsqueeze(2).broadcast_to([P, GB, P]),
                                    ALU.mult).then_inc(gx_ready, 1)

        def accumulate(g):
            after = earlier[(g + 1) % 2]
            dve.wait_ge(chosen_ready, g + 1)
            if g >= 1:
                dve.wait_ge(places_psum, g)
            nc.vector.tensor_reduce(group_sum[:, :], chosen[g][:, :, :].rearrange("p j e -> p e j"), AX.X,
                                    ALU.add).then_inc(group_summed, 1)
            dve.wait_ge(group_summed, g + 1)
            if g == 0:
                nc.vector.tensor_copy(after[:, :], group_sum[:, :]).then_inc(earlier_ready, 1)
            else:
                nc.vector.tensor_tensor(after[:, :], earlier[g % 2][:, :], group_sum[:, :], ALU.add).then_inc(earlier_ready, 1)

        def weigh(g):
            p = g % 2
            dve.wait_ge(places_psum, g + 1)
            nc.vector.tensor_scalar(placed[p][:, :, :], places_bank[g % 2], float(CAPACITY), None,
                                    ALU.is_lt).then_inc(routed[g], 1)
            dve.wait_ge(routed[g], 8)
            nc.vector.tensor_tensor(placed[p][:, :, :], placed[p][:, :, :], chosen[g][:, :, :], ALU.mult).then_inc(routed[g], 1)
            dve.wait_ge(routed[g], 9)
            nc.vector.tensor_tensor(weight[g][:, 0:GB * E1].rearrange("p (j e) -> p j e", j=GB), placed[p][:, :, :],
                                    wide(gate[p]), ALU.mult).then_inc(weight_ready, 1)

        def low_part(g):
            dve.wait_ge(gxt_high, g + 1)
            nc.vector.tensor_tensor(gxt_lo[g % 2][:, :], turned_bank[g % 2], gxt_hi[g % 2][:, :].bitcast(F32),
                                    ALU.subtract).then_inc(gxt_ready, 1)

        def begin(g):
            dve.wait_ge(bias_psum, g + 1)
            nc.vector.tensor_tensor(y[:, rows(g), :], blocks(turned_bank[g % 2]), x3[:, rows(g), :], ALU.add).then_inc(y_ready, 1)

        def combine(step):
            g, x = step // E1, step % E1
            if x == 0:
                dve.wait_ge(y_ready, g + 1)
                dve.wait_ge(weight_ready, g + 1)
            else:
                dve.wait_ge(expert_read, step)
            dve.wait_ge(expert_psum, step + 1)
            for j in range(GB):
                n = g * GB + j
                m = nc.vector.scalar_tensor_tensor(y[:, n, :], output_bank[step % 2][:, j * P:(j + 1) * P],
                                                   weight[g][:, j * E1 + x:j * E1 + x + 1], y[:, n, :], ALU.mult, ALU.add)
            m.then_inc(expert_read, 1)

        def statistics4(g):
            dve.wait_ge(expert_read, (g + 1) * E1)
            if g >= 2:
                dve.wait_ge(final_ready, g - 1)
            norm_statistics(nc, dve, norm4, g, y[:, rows(g), :])

        def apply4(g):
            norm_apply(nc, dve, norm4, g, y[:, rows(g), :], final[:, rows(g), :], final_ready)

        dve.wait_ge(setup_done, 1)
        choose(0)
        scale(0)
        choose(1)
        low_part(0)
        accumulate(0)
        weigh(0)
        scale(1)
        accumulate(1)
        statistics3(2)
        statistics3(3)
        begin(0)
        apply3(2)
        for step in range(GROUPS * E1):
            g, x = step // E1, step % E1
            combine(step)
            if step == 1:
                apply3(3)
            if x == 2 and g + 1 < GROUPS:
                low_part(g + 1)
            if x == 3 and g + 1 < GROUPS:
                weigh(g + 1)
            if x == 1 and g >= 1:
                statistics4(g - 1)
            if x == 7 and g >= 1:
                apply4(g - 1)
            if x == 7 and g + 1 < GROUPS:
                begin(g + 1)
            for n, at in ((2, 2), (3, 9)):
                if step == at + 3:
                    choose(n)
                if step == at + 4:
                    scale(n)
                    if n + 1 < GROUPS:
                        accumulate(n)
        statistics4(GROUPS - 1)
        apply4(GROUPS - 1)

    return {"sync": sync_program, "gpsimd": gpsimd_program, "tensor": tensor_program, "scalar": scalar_program,
            "vector": vector_program}


def build(nc, a, out):
    q_parts = nc.dram_tensor("q_parts", (PARTS, P, B * T), BF16, kind="Internal").ap()
    k_parts = nc.dram_tensor("k_parts", (PARTS, P, B * T), BF16, kind="Internal").ap()
    with ExitStack() as ctx:
        psum = ctx.enter_context(nc.psum_tensor("psum", [P, 8 * HALF], F32))
        z_t = ctx.enter_context(nc.sbuf_tensor("z_t", [P, STEPS * T], F32))
        k_hi = ctx.enter_context(nc.sbuf_tensor("k_hi", [P, T], F32R))
        w_o_loaded = ctx.enter_context(nc.semaphore("w_o_loaded"))
        softmax_attention(nc, psum, a["x_t"], a["w_kq"], a["w_v"], a["consts"][:, 0:2 * P], z_t, k_hi, a["w_o"], w_o_loaded)
        wo = k_hi[:, :].bitcast(F32).rearrange("p (n d) -> p n d", d=P)
        y3 = z_t[:, QUAD * RING1 * T:QUAD * RING1 * T + B * T].rearrange("p (n d) -> p n d", d=P)
        experts = expert_buffers(nc, ctx, z_t, a["consts"], a["w_router"], a["b_router"], a["w1"], a["b1"], a["w2"], a["b2"])
        x3_ready = ctx.enter_context(nc.semaphore("x3_ready"))
        acc_read = [ctx.enter_context(nc.semaphore(f"acc_read{n}")) for n in range(2)]
        norm3 = norm_buffers(lambda name, shape: ctx.enter_context(nc.sbuf_tensor(name, shape, F32)),
                             lambda name: ctx.enter_context(nc.semaphore(name)), "norm3")
        last_part = mixture_of_experts(nc, ctx, psum, experts, z_t, y3, acc_read, x3_ready, norm3, out)
        mix_and_sigmoid_attention(nc, psum, a["x_rows"], wo, w_o_loaded, a["w_rkv"], a["columns"], a["sign_v"], z_t,
                                  q_parts, k_parts, y3, acc_read, x3_ready, norm3, experts, last_part)


def kernel(**inputs):
    import numpy as np
    import concourse.bacc as bacc
    from concourse.bass_utils import run_bass_kernel_spmd

    x = {name: np.asarray(value) for name, value in inputs.items()}

    def rows(y):
        return y.reshape(-1, P, y.shape[-1]).transpose(1, 0, 2)

    heads = np.stack([x["L0_attn_W_K"], x["L0_attn_W_Q"], x["L0_attn_W_V"]])
    e1 = x["L1_ffn_W1"].shape[0]
    arrays = {
        "x_t": x["L0_attn_x"].transpose(0, 2, 1).reshape(B * P, T),
        "x_rows": rows(x["L0_attn_x"]),
        "w_kq": heads[0:2].reshape(2, PAIRS, P, P).transpose(1, 3, 0, 2).reshape(PAIRS * P, 2 * P),
        "w_v": heads[2].reshape(PAIRS // 2, 2 * P, P).transpose(0, 2, 1).reshape(PAIRS // 2 * P, 2 * P),
        "w_o": x["L0_attn_W_O"].reshape(P, PAIRS, P).transpose(2, 1, 0),
        "w_rkv": np.stack([x["L0_ffn_W_r"].T, x["L0_ffn_W_k"].T, x["L0_ffn_W_v"].T], axis=1),
        "columns": np.stack([x["L0_ffn_mu_r"], x["L0_ffn_mu_k"], x["L1_attn_bv_q"].reshape(-1),
                             x["L1_attn_bv_k"].reshape(-1)], axis=1),
        "sign_v": x["L1_attn_bv_v"].reshape(-1),
        "w_router": x["L1_ffn_Wr"],
        "b_router": x["L1_ffn_br"],
        "w1": x["L1_ffn_W1"].transpose(1, 0, 2),
        "b1": x["L1_ffn_b1"].T,
        "w2": x["L1_ffn_W2"].transpose(1, 0, 2),
        "b2": x["L1_ffn_b2"],
        "consts": np.concatenate([np.tril(np.ones((P, P))), np.eye(P), np.triu(np.ones((P, P))),
                                  np.tile(np.arange(e1, 0, -1), (P, 1))], axis=1).astype(np.float32),
    }
    arrays = {name: np.ascontiguousarray(value) for name, value in arrays.items()}
    nc = bacc.Bacc("TRN2", target_bir_lowering=False, num_devices=1)
    a = {name: nc.dram_tensor(f"in_{name}", value.shape, mybir.dt.from_np(value.dtype), kind="ExternalInput").ap()
         for name, value in arrays.items()}
    out = nc.dram_tensor("out", (P, B * NB, P), F32, kind="ExternalOutput").ap()
    build(nc, a, out)
    result = run_bass_kernel_spmd(nc, [{f"in_{name}": value for name, value in arrays.items()}], core_ids=[0])
    return result.results[0]["out"].transpose(1, 0, 2).reshape(B, T, P)
```
